# Optimizing a Trainium2 kernel written in Bass

```python
import numpy as np
import jax
import jax.numpy as jnp

def _softmax(x, axis=-1):
    return jax.nn.softmax(x, axis=axis)

def _gelu(x):
    return jax.nn.gelu(x, approximate=True)

def _silu(x):
    return jax.nn.silu(x)

def _sigmoid(x):
    return jax.nn.sigmoid(x)

def _layernorm(x, axis=-1, eps=1e-05):
    m = jnp.mean(x, axis=axis, keepdims=True)
    v = jnp.var(x, axis=axis, keepdims=True)
    return (x - m) / jnp.sqrt(v + eps)

def _scatter_add(tgt, idx, src, axis=0):
    return tgt.at[idx].add(src)

def _segment_sum(src, seg, n):
    return jax.ops.segment_sum(src, seg, n)
kernel_name = 'mk_hybrid_d2_jaxref_r8_fa0281'

def setup_inputs(seed: int=0):
    np.random.seed(seed)
    _w = jnp.asarray

    def _L0_attn_a_setup():
        import jax, jax.numpy as jnp
        import numpy as np
        DIM = 128
        B, S = (4, 512)
        key = jax.random.key(seed)
        ks = jax.random.split(key, 12)
        d = DIM

        def lin(k, out_d, in_d):
            bound = 1.0 / np.sqrt(in_d)
            kw, kb = jax.random.split(k)
            W = jax.random.uniform(kw, (out_d, in_d), jnp.float32, -bound, bound)
            b = jax.random.uniform(kb, (out_d,), jnp.float32, -bound, bound)
            return (W, b)
        x = jax.random.normal(ks[0], (B, S, d), jnp.float32)
        random_phases = jax.random.normal(ks[1], (d,), jnp.float32) * (2.0 * np.pi)
        W_mag, b_mag = lin(ks[2], d, d)
        W_q, b_q = lin(ks[3], d, d)
        ln_g = jnp.ones((4 * d,), jnp.float32)
        ln_b = jnp.zeros((4 * d,), jnp.float32)
        W1, b1 = lin(ks[4], 2 * d, 4 * d)
        W2, b2 = lin(ks[5], d, 2 * d)
        return {'x': x, 'random_phases': random_phases, 'W_mag': W_mag, 'b_mag': b_mag, 'W_q': W_q, 'b_q': b_q, 'ln_g': ln_g, 'ln_b': ln_b, 'W1': W1, 'b1': b1, 'W2': W2, 'b2': b2}
    _L0_attn_a_in = _L0_attn_a_setup()

    def _L0_attn_b_setup():
        import jax, jax.numpy as jnp
        import numpy as np
        B, S, D = (2, 256, 128)
        H = 16
        HD = D // H

        def _rope_tables(seq_len, head_dim, dtype):
            pos = jnp.arange(seq_len, dtype=dtype)
            inv = jnp.power(10000.0, -2.0 * jnp.arange(head_dim // 2, dtype=dtype) / head_dim)
            ang = pos[:, None] * inv[None, :]
            cos_pos = jnp.repeat(jnp.cos(ang), 2, axis=-1)
            sin_pos = jnp.repeat(jnp.sin(ang), 2, axis=-1)
            return (cos_pos, sin_pos)

        def _rotate_half_interleaved(x):
            x2 = jnp.stack([-x[..., 1::2], x[..., 0::2]], axis=-1)
            return x2.reshape(x.shape)
        key = jax.random.key(seed)
        ks = jax.random.split(key, 4)
        scale = 1.0 / np.sqrt(D)
        return {'hidden_states': jax.random.normal(ks[0], (B, S, D), jnp.float32), 'Wq': jax.random.normal(ks[1], (D, D), jnp.float32) * scale, 'bq': jnp.zeros((D,), jnp.float32), 'Wk': jax.random.normal(ks[2], (D, D), jnp.float32) * scale, 'bk': jnp.zeros((D,), jnp.float32), 'Wv': jax.random.normal(ks[3], (D, D), jnp.float32) * scale, 'bv': jnp.zeros((D,), jnp.float32)}
    _L0_attn_b_in = _L0_attn_b_setup()

    def _L0_ffn_setup():
        import jax, jax.numpy as jnp
        import numpy as np
        E = 16
        K = 4
        D = 128
        F = 128
        SH_F = 256
        B, S = (1, 256)
        SCALE = 2.5

        def _swiglu(x, wg, wu, wd):
            return jax.nn.silu(x @ wg) * (x @ wu) @ wd
        key = jax.random.key(seed)
        ks = jax.random.split(key, 8)
        sd = 1.0 / np.sqrt(D)
        sf = 1.0 / np.sqrt(F)
        ssf = 1.0 / np.sqrt(SH_F)
        return {'hidden_states': jax.random.normal(ks[0], (B, S, D), jnp.float32), 'gate_w': jax.random.normal(ks[1], (E, D), jnp.float32) * sd, 'shared_wg': jax.random.normal(ks[2], (D, SH_F), jnp.float32) * sd, 'shared_wu': jax.random.normal(ks[3], (D, SH_F), jnp.float32) * sd, 'shared_wd': jax.random.normal(ks[4], (SH_F, D), jnp.float32) * ssf, 'exp_wg': jax.random.normal(ks[5], (E, D, F), jnp.float32) * sd, 'exp_wu': jax.random.normal(ks[6], (E, D, F), jnp.float32) * sd, 'exp_wd': jax.random.normal(ks[7], (E, F, D), jnp.float32) * sf}
    _L0_ffn_in = _L0_ffn_setup()

    def _L1_attn_a_setup():
        import jax, jax.numpy as jnp
        import numpy as np
        NUM_HEADS = 16
        LEVELS = 4

        def _mha(x, w_in, b_in, w_out, b_out):
            B, S, E = x.shape
            H = NUM_HEADS
            hd = E // H
            qkv = x @ w_in.T + b_in
            q, k, v = jnp.split(qkv, 3, axis=-1)
            split = lambda t: t.reshape(B, S, H, hd).transpose(0, 2, 1, 3)
            q, k, v = (split(q), split(k), split(v))
            scores = jnp.einsum('bhqd,bhkd->bhqk', q, k) / jnp.sqrt(jnp.asarray(hd, x.dtype))
            attn = jax.nn.softmax(scores, axis=-1)
            out = jnp.einsum('bhqk,bhkd->bhqd', attn, v)
            out = out.transpose(0, 2, 1, 3).reshape(B, S, E)
            return out @ w_out.T + b_out

        def _upsample_linear(x, target):
            B, L, E = x.shape
            src = (jnp.arange(target, dtype=jnp.float32) + 0.5) * (L / target) - 0.5
            src = jnp.clip(src, 0.0, L - 1)
            i0 = jnp.floor(src).astype(jnp.int32)
            i1 = jnp.minimum(i0 + 1, L - 1)
            w = (src - i0.astype(jnp.float32))[None, :, None].astype(x.dtype)
            return x[:, i0, :] * (1 - w) + x[:, i1, :] * w
        key = jax.random.key(seed)
        ks = jax.random.split(key, 7)
        B, S, E = (1, 256, 128)
        return {'query': jax.random.normal(ks[0], (B, S, E), jnp.float32), 'in_proj_w': jax.random.normal(ks[1], (LEVELS, 3 * E, E), jnp.float32) * 0.02, 'in_proj_b': jnp.zeros((LEVELS, 3 * E), jnp.float32), 'out_w': jax.random.normal(ks[2], (LEVELS, E, E), jnp.float32) * 0.02, 'out_b': jnp.zeros((LEVELS, E), jnp.float32), 'up_w': jax.random.normal(ks[3], (LEVELS - 1, E, E), jnp.float32) * 0.02, 'up_b': jnp.zeros((LEVELS - 1, E), jnp.float32)}
    _L1_attn_a_in = _L1_attn_a_setup()

    def _L1_attn_b_setup():
        import jax, jax.numpy as jnp
        import numpy as np
        B, T, C = (8, 256, 128)
        H = 4 * C
        N_LAYER, LAYER_ID = (12, 2)
        K_CLAMP = 60.0
        LN_EPS = 1e-05

        def _ln(x, g, b):
            m = jnp.mean(x, axis=-1, keepdims=True)
            v = jnp.var(x, axis=-1, keepdims=True)
            return (x - m) * jax.lax.rsqrt(v + LN_EPS) * g + b

        def _mix(x, time_mix, combined_mix):
            c = x.shape[-1]
            xm1 = jnp.pad(x[:, :-1], ((0, 0), (1, 0), (0, 0)))
            xp1 = jnp.pad(x[:, 1:], ((0, 0), (0, 1), (0, 0)))
            xc = jnp.concatenate([xm1[..., :c // 2], xp1[..., c // 2:]], axis=-1)
            return x * time_mix + xm1 * (1.0 - time_mix) + xc * combined_mix

        def _wkv(time_decay, time_first, k, v):
            ed = jnp.exp(-jnp.exp(time_decay))
            eu = jnp.exp(time_first)

            def step(carry, kv_t):
                a, b = carry
                kt, vt = kv_t
                y = (a + eu * kt * vt) / (b + eu * kt)
                return ((ed * a + kt * vt, ed * b + kt), y)
            kT = jnp.swapaxes(k, 0, 1)
            vT = jnp.swapaxes(v, 0, 1)
            z = jnp.zeros_like(kT[0])
            _, y = jax.lax.scan(step, (z, z), (kT, vT))
            return jnp.swapaxes(y, 0, 1)

        def _time_mix_block(x, time_mix, combined_mix, time_decay, time_first, Wk, Wv, Wr, Wo):
            xm = _mix(x, time_mix, combined_mix)
            k = jnp.exp(jnp.minimum(xm @ Wk.T, K_CLAMP))
            v = xm @ Wv.T
            r = xm @ Wr.T
            wkv = _wkv(time_decay, time_first, k, v)
            return jax.nn.sigmoid(r) * wkv @ Wo.T

        def _channel_mix_block(x, time_mix, combined_mix, Fk, Fv, Fr):
            xm = _mix(x, time_mix, combined_mix)
            k = jnp.square(jax.nn.relu(xm @ Fk.T))
            kv = k @ Fv.T
            return jax.nn.sigmoid(xm @ Fr.T) * kv
        key = jax.random.key(seed)
        ks = jax.random.split(key, 9)
        s = 0.02
        x = jax.random.normal(ks[0], (B, T, C), jnp.float32)
        h = np.arange(C, dtype=np.float64)
        frac = (LAYER_ID - 1) / (N_LAYER - 2)
        f1 = 3.0 + frac * (1.2 - 3.0)
        f2 = 0.65 + frac * (0.4 - 0.65)
        decay_speed = np.power(f2, h / (C - 1) * 7.0) * f1
        tm = jnp.concatenate([jnp.zeros(C // 2), jnp.ones(C // 2)]).reshape(1, 1, C).astype(jnp.float32)
        return dict(x=x, ln1_g=jnp.ones((C,), jnp.float32), ln1_b=jnp.zeros((C,), jnp.float32), ln2_g=jnp.ones((C,), jnp.float32), ln2_b=jnp.zeros((C,), jnp.float32), att_time_mix=tm, att_combined_mix=jnp.full((1, 1, C), 0.01, jnp.float32), time_decay=jnp.asarray(np.log(decay_speed), jnp.float32), time_first=jnp.full((C,), float(np.log(0.3)), jnp.float32), Wk=jax.random.normal(ks[1], (C, C), jnp.float32) * s, Wv=jax.random.normal(ks[2], (C, C), jnp.float32) * s, Wr=jax.random.normal(ks[3], (C, C), jnp.float32) * s, Wo=jax.random.normal(ks[4], (C, C), jnp.float32) * s, ffn_time_mix=tm, ffn_combined_mix=jnp.full((1, 1, C), 0.01, jnp.float32), Fk=jax.random.normal(ks[5], (H, C), jnp.float32) * s, Fv=jax.random.normal(ks[6], (C, H), jnp.float32) * s, Fr=jax.random.normal(ks[7], (C, C), jnp.float32) * s)
    _L1_attn_b_in = _L1_attn_b_setup()

    def _L1_ffn_setup():
        import jax, jax.numpy as jnp
        import numpy as np
        DIM = 128
        HIDDEN = 352
        NUM_EXPERTS = 8
        TOP_K = 2
        BATCH, SEQ = (4, 256)
        key = jax.random.key(seed)
        ks = jax.random.split(key, 5)
        x = jax.random.normal(ks[0], (BATCH, SEQ, DIM), dtype=jnp.float32)
        gate_w = jax.random.normal(ks[1], (NUM_EXPERTS, DIM), dtype=jnp.float32) * 0.02
        w1 = jax.random.normal(ks[2], (NUM_EXPERTS, HIDDEN, DIM), dtype=jnp.float32) * 0.02
        w3 = jax.random.normal(ks[3], (NUM_EXPERTS, HIDDEN, DIM), dtype=jnp.float32) * 0.02
        w2 = jax.random.normal(ks[4], (NUM_EXPERTS, DIM, HIDDEN), dtype=jnp.float32) * 0.02
        return {'x': x, 'gate_w': gate_w, 'w1': w1, 'w3': w3, 'w2': w2}
    _L1_ffn_in = _L1_ffn_setup()
    _d = {'L0_attn_a_x': _L0_attn_a_in['x'], 'L0_attn_a_random_phases': _L0_attn_a_in['random_phases'], 'L0_attn_a_W_mag': _L0_attn_a_in['W_mag'], 'L0_attn_a_b_mag': _L0_attn_a_in['b_mag'], 'L0_attn_a_W_q': _L0_attn_a_in['W_q'], 'L0_attn_a_b_q': _L0_attn_a_in['b_q'], 'L0_attn_a_ln_g': _L0_attn_a_in['ln_g'], 'L0_attn_a_ln_b': _L0_attn_a_in['ln_b'], 'L0_attn_a_W1': _L0_attn_a_in['W1'], 'L0_attn_a_b1': _L0_attn_a_in['b1'], 'L0_attn_a_W2': _L0_attn_a_in['W2'], 'L0_attn_a_b2': _L0_attn_a_in['b2'], 'L0_attn_b_Wq': _L0_attn_b_in['Wq'], 'L0_attn_b_bq': _L0_attn_b_in['bq'], 'L0_attn_b_Wk': _L0_attn_b_in['Wk'], 'L0_attn_b_bk': _L0_attn_b_in['bk'], 'L0_attn_b_Wv': _L0_attn_b_in['Wv'], 'L0_attn_b_bv': _L0_attn_b_in['bv'], 'L0_ffn_gate_w': _L0_ffn_in['gate_w'], 'L0_ffn_shared_wg': _L0_ffn_in['shared_wg'], 'L0_ffn_shared_wu': _L0_ffn_in['shared_wu'], 'L0_ffn_shared_wd': _L0_ffn_in['shared_wd'], 'L0_ffn_exp_wg': _L0_ffn_in['exp_wg'], 'L0_ffn_exp_wu': _L0_ffn_in['exp_wu'], 'L0_ffn_exp_wd': _L0_ffn_in['exp_wd'], 'L1_attn_a_in_proj_w': _L1_attn_a_in['in_proj_w'], 'L1_attn_a_in_proj_b': _L1_attn_a_in['in_proj_b'], 'L1_attn_a_out_w': _L1_attn_a_in['out_w'], 'L1_attn_a_out_b': _L1_attn_a_in['out_b'], 'L1_attn_a_up_w': _L1_attn_a_in['up_w'], 'L1_attn_a_up_b': _L1_attn_a_in['up_b'], 'L1_attn_b_ln1_g': _L1_attn_b_in['ln1_g'], 'L1_attn_b_ln1_b': _L1_attn_b_in['ln1_b'], 'L1_attn_b_ln2_g': _L1_attn_b_in['ln2_g'], 'L1_attn_b_ln2_b': _L1_attn_b_in['ln2_b'], 'L1_attn_b_att_time_mix': _L1_attn_b_in['att_time_mix'], 'L1_attn_b_att_combined_mix': _L1_attn_b_in['att_combined_mix'], 'L1_attn_b_time_decay': _L1_attn_b_in['time_decay'], 'L1_attn_b_time_first': _L1_attn_b_in['time_first'], 'L1_attn_b_Wk': _L1_attn_b_in['Wk'], 'L1_attn_b_Wv': _L1_attn_b_in['Wv'], 'L1_attn_b_Wr': _L1_attn_b_in['Wr'], 'L1_attn_b_Wo': _L1_attn_b_in['Wo'], 'L1_attn_b_ffn_time_mix': _L1_attn_b_in['ffn_time_mix'], 'L1_attn_b_ffn_combined_mix': _L1_attn_b_in['ffn_combined_mix'], 'L1_attn_b_Fk': _L1_attn_b_in['Fk'], 'L1_attn_b_Fv': _L1_attn_b_in['Fv'], 'L1_attn_b_Fr': _L1_attn_b_in['Fr'], 'L1_ffn_gate_w': _L1_ffn_in['gate_w'], 'L1_ffn_w1': _L1_ffn_in['w1'], 'L1_ffn_w3': _L1_ffn_in['w3'], 'L1_ffn_w2': _L1_ffn_in['w2']}
    _x0 = _d['L0_attn_a_x']
    _d['L0_attn_a_x'] = jax.random.normal(jax.random.fold_in(jax.random.key(seed), 1), (4, 512, 128), dtype=_x0.dtype)
    del _x0
    return _d

def reference(L0_attn_a_x, L0_attn_a_random_phases, L0_attn_a_W_mag, L0_attn_a_b_mag, L0_attn_a_W_q, L0_attn_a_b_q, L0_attn_a_ln_g, L0_attn_a_ln_b, L0_attn_a_W1, L0_attn_a_b1, L0_attn_a_W2, L0_attn_a_b2, L0_attn_b_Wq, L0_attn_b_bq, L0_attn_b_Wk, L0_attn_b_bk, L0_attn_b_Wv, L0_attn_b_bv, L0_ffn_gate_w, L0_ffn_shared_wg, L0_ffn_shared_wu, L0_ffn_shared_wd, L0_ffn_exp_wg, L0_ffn_exp_wu, L0_ffn_exp_wd, L1_attn_a_in_proj_w, L1_attn_a_in_proj_b, L1_attn_a_out_w, L1_attn_a_out_b, L1_attn_a_up_w, L1_attn_a_up_b, L1_attn_b_ln1_g, L1_attn_b_ln1_b, L1_attn_b_ln2_g, L1_attn_b_ln2_b, L1_attn_b_att_time_mix, L1_attn_b_att_combined_mix, L1_attn_b_time_decay, L1_attn_b_time_first, L1_attn_b_Wk, L1_attn_b_Wv, L1_attn_b_Wr, L1_attn_b_Wo, L1_attn_b_ffn_time_mix, L1_attn_b_ffn_combined_mix, L1_attn_b_Fk, L1_attn_b_Fv, L1_attn_b_Fr, L1_ffn_gate_w, L1_ffn_w1, L1_ffn_w3, L1_ffn_w2):

    def _L0_attn_a_ref(x, random_phases, W_mag, b_mag, W_q, b_q, ln_g, ln_b, W1, b1, W2, b2):
        import jax, jax.numpy as jnp
        import numpy as np
        DIM = 128
        B, S = (4, 512)
        Bx, Sx, D = x.shape
        magnitude = jax.nn.sigmoid(jnp.einsum('bsd,ed->bse', x, W_mag) + b_mag) * 5.0
        position = jnp.arange(Sx, dtype=x.dtype)[None, :, None]
        phi = random_phases[None, None, :] * position * 0.01
        cos_phi = jnp.cos(phi)
        sin_phi = jnp.sin(phi)
        weighted = magnitude * x
        mem_r = jnp.cumsum(weighted * cos_phi, axis=1)
        mem_i = jnp.cumsum(weighted * sin_phi, axis=1)
        acc_mag = jnp.cumsum(magnitude, axis=1)
        inv_sqrt = 1.0 / jnp.sqrt(acc_mag + 1e-08)
        mr = mem_r * inv_sqrt
        mi = mem_i * inv_sqrt
        q_off = jnp.einsum('bsd,ed->bse', x, W_q) + b_q
        phi_q = phi + q_off
        cq = jnp.cos(phi_q)
        sq = jnp.sin(phi_q)
        retrieved_r = mr * cq + mi * sq
        retrieved_i = mi * cq - mr * sq
        context = jnp.concatenate([x * cos_phi, x * sin_phi, retrieved_r, retrieved_i], axis=-1)
        mu = jnp.mean(context, axis=-1, keepdims=True)
        var = jnp.mean((context - mu) ** 2, axis=-1, keepdims=True)
        h = (context - mu) / jnp.sqrt(var + 1e-05) * ln_g + ln_b
        h = jax.nn.gelu(jnp.einsum('bsf,gf->bsg', h, W1) + b1, approximate=False)
        out = jnp.einsum('bsg,dg->bsd', h, W2) + b2
        return x + out

    def _L0_attn_b_ref(hidden_states, Wq, bq, Wk, bk, Wv, bv):
        import jax, jax.numpy as jnp
        import numpy as np
        B, S, D = (2, 256, 128)
        H = 16
        HD = D // H

        def _rope_tables(seq_len, head_dim, dtype):
            pos = jnp.arange(seq_len, dtype=dtype)
            inv = jnp.power(10000.0, -2.0 * jnp.arange(head_dim // 2, dtype=dtype) / head_dim)
            ang = pos[:, None] * inv[None, :]
            cos_pos = jnp.repeat(jnp.cos(ang), 2, axis=-1)
            sin_pos = jnp.repeat(jnp.sin(ang), 2, axis=-1)
            return (cos_pos, sin_pos)

        def _rotate_half_interleaved(x):
            x2 = jnp.stack([-x[..., 1::2], x[..., 0::2]], axis=-1)
            return x2.reshape(x.shape)
        b, s, d = hidden_states.shape
        q = hidden_states @ Wq + bq
        k = hidden_states @ Wk + bk
        v = hidden_states @ Wv + bv
        q = q.reshape(b, s, H, HD).transpose(0, 2, 1, 3)
        k = k.reshape(b, s, H, HD).transpose(0, 2, 1, 3)
        v = v.reshape(b, s, H, HD).transpose(0, 2, 1, 3)
        cos_pos, sin_pos = _rope_tables(s, HD, hidden_states.dtype)
        q = q * cos_pos + _rotate_half_interleaved(q) * sin_pos
        k = k * cos_pos + _rotate_half_interleaved(k) * sin_pos
        scores = jnp.einsum('bhqd,bhkd->bhqk', q, k) / jnp.sqrt(jnp.asarray(HD, hidden_states.dtype))
        probs = jax.nn.softmax(scores, axis=-1)
        ctx = jnp.einsum('bhqk,bhkd->bhqd', probs, v)
        ctx = ctx.transpose(0, 2, 1, 3).reshape(b, s, d)
        return ctx

    def _L0_ffn_ref(hidden_states, gate_w, shared_wg, shared_wu, shared_wd, exp_wg, exp_wu, exp_wd):
        import jax, jax.numpy as jnp
        import numpy as np
        E = 16
        K = 4
        D = 128
        F = 128
        SH_F = 256
        B, S = (1, 256)
        SCALE = 2.5

        def _swiglu(x, wg, wu, wd):
            return jax.nn.silu(x @ wg) * (x @ wu) @ wd
        b, s, d = hidden_states.shape
        x = hidden_states.reshape(-1, d)
        t = x.shape[0]
        scores = jax.nn.sigmoid(x @ gate_w.T)
        topk_w, topk_idx = jax.lax.top_k(scores, K)
        topk_w = topk_w / (jnp.sum(topk_w, axis=-1, keepdims=True) + 1e-20)
        topk_w = topk_w * SCALE
        cw = jnp.zeros((t, E), x.dtype).at[jnp.arange(t)[:, None], topk_idx].add(topk_w)
        shared_out = _swiglu(x, shared_wg, shared_wu, shared_wd)

        def body(acc, p):
            wg, wu, wd, w = p
            return (acc + w[:, None] * _swiglu(x, wg, wu, wd), None)
        routed_out, _ = jax.lax.scan(body, jnp.zeros_like(x), (exp_wg, exp_wu, exp_wd, cw.T))
        return (shared_out + routed_out).reshape(b, s, d)

    def _L1_attn_a_ref(query, in_proj_w, in_proj_b, out_w, out_b, up_w, up_b):
        import jax, jax.numpy as jnp
        import numpy as np
        NUM_HEADS = 16
        LEVELS = 4

        def _mha(x, w_in, b_in, w_out, b_out):
            B, S, E = x.shape
            H = NUM_HEADS
            hd = E // H
            qkv = x @ w_in.T + b_in
            q, k, v = jnp.split(qkv, 3, axis=-1)
            split = lambda t: t.reshape(B, S, H, hd).transpose(0, 2, 1, 3)
            q, k, v = (split(q), split(k), split(v))
            scores = jnp.einsum('bhqd,bhkd->bhqk', q, k) / jnp.sqrt(jnp.asarray(hd, x.dtype))
            attn = jax.nn.softmax(scores, axis=-1)
            out = jnp.einsum('bhqk,bhkd->bhqd', attn, v)
            out = out.transpose(0, 2, 1, 3).reshape(B, S, E)
            return out @ w_out.T + b_out

        def _upsample_linear(x, target):
            B, L, E = x.shape
            src = (jnp.arange(target, dtype=jnp.float32) + 0.5) * (L / target) - 0.5
            src = jnp.clip(src, 0.0, L - 1)
            i0 = jnp.floor(src).astype(jnp.int32)
            i1 = jnp.minimum(i0 + 1, L - 1)
            w = (src - i0.astype(jnp.float32))[None, :, None].astype(x.dtype)
            return x[:, i0, :] * (1 - w) + x[:, i1, :] * w
        B, S, E = query.shape
        outs = []
        for lvl in range(LEVELS):
            stride = 2 ** lvl
            x = query[:, ::stride, :]
            outs.append(_mha(x, in_proj_w[lvl], in_proj_b[lvl], out_w[lvl], out_b[lvl]))
        current = outs[-1]
        for lvl in range(LEVELS - 2, -1, -1):
            fine = outs[lvl]
            if current.shape[1] != fine.shape[1]:
                current = _upsample_linear(current, fine.shape[1])
            current = current @ up_w[lvl].T + up_b[lvl]
            current = current + fine
        return current

    def _L1_attn_b_ref(x, ln1_g, ln1_b, ln2_g, ln2_b, att_time_mix, att_combined_mix, time_decay, time_first, Wk, Wv, Wr, Wo, ffn_time_mix, ffn_combined_mix, Fk, Fv, Fr):
        import jax, jax.numpy as jnp
        import numpy as np
        B, T, C = (8, 256, 128)
        H = 4 * C
        N_LAYER, LAYER_ID = (12, 2)
        K_CLAMP = 60.0
        LN_EPS = 1e-05

        def _ln(x, g, b):
            m = jnp.mean(x, axis=-1, keepdims=True)
            v = jnp.var(x, axis=-1, keepdims=True)
            return (x - m) * jax.lax.rsqrt(v + LN_EPS) * g + b

        def _mix(x, time_mix, combined_mix):
            c = x.shape[-1]
            xm1 = jnp.pad(x[:, :-1], ((0, 0), (1, 0), (0, 0)))
            xp1 = jnp.pad(x[:, 1:], ((0, 0), (0, 1), (0, 0)))
            xc = jnp.concatenate([xm1[..., :c // 2], xp1[..., c // 2:]], axis=-1)
            return x * time_mix + xm1 * (1.0 - time_mix) + xc * combined_mix

        def _wkv(time_decay, time_first, k, v):
            ed = jnp.exp(-jnp.exp(time_decay))
            eu = jnp.exp(time_first)

            def step(carry, kv_t):
                a, b = carry
                kt, vt = kv_t
                y = (a + eu * kt * vt) / (b + eu * kt)
                return ((ed * a + kt * vt, ed * b + kt), y)
            kT = jnp.swapaxes(k, 0, 1)
            vT = jnp.swapaxes(v, 0, 1)
            z = jnp.zeros_like(kT[0])
            _, y = jax.lax.scan(step, (z, z), (kT, vT))
            return jnp.swapaxes(y, 0, 1)

        def _time_mix_block(x, time_mix, combined_mix, time_decay, time_first, Wk, Wv, Wr, Wo):
            xm = _mix(x, time_mix, combined_mix)
            k = jnp.exp(jnp.minimum(xm @ Wk.T, K_CLAMP))
            v = xm @ Wv.T
            r = xm @ Wr.T
            wkv = _wkv(time_decay, time_first, k, v)
            return jax.nn.sigmoid(r) * wkv @ Wo.T

        def _channel_mix_block(x, time_mix, combined_mix, Fk, Fv, Fr):
            xm = _mix(x, time_mix, combined_mix)
            k = jnp.square(jax.nn.relu(xm @ Fk.T))
            kv = k @ Fv.T
            return jax.nn.sigmoid(xm @ Fr.T) * kv
        x = _ln(x, ln1_g, ln1_b)
        x = x + _time_mix_block(x, att_time_mix, att_combined_mix, time_decay, time_first, Wk, Wv, Wr, Wo)
        x = _ln(x, ln2_g, ln2_b)
        x = x + _channel_mix_block(x, ffn_time_mix, ffn_combined_mix, Fk, Fv, Fr)
        return x

    def _L1_ffn_ref(x, gate_w, w1, w3, w2):
        import jax, jax.numpy as jnp
        import numpy as np
        DIM = 128
        HIDDEN = 352
        NUM_EXPERTS = 8
        TOP_K = 2
        BATCH, SEQ = (4, 256)
        orig_shape = x.shape
        xf = x.reshape(-1, x.shape[-1])
        T = xf.shape[0]
        E, K = (gate_w.shape[0], TOP_K)
        scores = jax.nn.softmax(xf @ gate_w.T, axis=-1)
        expert_weights, expert_indices = jax.lax.top_k(scores, K)
        expert_weights = expert_weights / jnp.sum(expert_weights, axis=-1, keepdims=True)
        x_rep = jnp.repeat(xf, K, axis=0)
        flat_idx = expert_indices.reshape(-1)
        y = jnp.zeros_like(x_rep)
        for e in range(E):
            m = (flat_idx == e)[:, None]
            xe = jnp.where(m, x_rep, 0.0)
            h = jax.nn.silu(xe @ w1[e].T) * (xe @ w3[e].T)
            out = h @ w2[e].T
            y = y + jnp.where(m, out, 0.0)
        y = jnp.sum(y.reshape(T, K, -1) * expert_weights[..., None], axis=1)
        return y.reshape(orig_shape)
    x = L0_attn_a_x
    x = x + _L0_attn_a_ref(_layernorm(x, axis=-1), L0_attn_a_random_phases, L0_attn_a_W_mag, L0_attn_a_b_mag, L0_attn_a_W_q, L0_attn_a_b_q, L0_attn_a_ln_g, L0_attn_a_ln_b, L0_attn_a_W1, L0_attn_a_b1, L0_attn_a_W2, L0_attn_a_b2)
    x = x + _L0_ffn_ref(_layernorm(x, axis=-1), L0_ffn_gate_w, L0_ffn_shared_wg, L0_ffn_shared_wu, L0_ffn_shared_wd, L0_ffn_exp_wg, L0_ffn_exp_wu, L0_ffn_exp_wd)
    x = x + _L0_attn_b_ref(_layernorm(x, axis=-1), L0_attn_b_Wq, L0_attn_b_bq, L0_attn_b_Wk, L0_attn_b_bk, L0_attn_b_Wv, L0_attn_b_bv)
    x = x + _L0_ffn_ref(_layernorm(x, axis=-1), L0_ffn_gate_w, L0_ffn_shared_wg, L0_ffn_shared_wu, L0_ffn_shared_wd, L0_ffn_exp_wg, L0_ffn_exp_wu, L0_ffn_exp_wd)
    x = x + _L1_attn_a_ref(_layernorm(x, axis=-1), L1_attn_a_in_proj_w, L1_attn_a_in_proj_b, L1_attn_a_out_w, L1_attn_a_out_b, L1_attn_a_up_w, L1_attn_a_up_b)
    x = x + _L1_ffn_ref(_layernorm(x, axis=-1), L1_ffn_gate_w, L1_ffn_w1, L1_ffn_w3, L1_ffn_w2)
    x = x + _L1_attn_b_ref(_layernorm(x, axis=-1), L1_attn_b_ln1_g, L1_attn_b_ln1_b, L1_attn_b_ln2_g, L1_attn_b_ln2_b, L1_attn_b_att_time_mix, L1_attn_b_att_combined_mix, L1_attn_b_time_decay, L1_attn_b_time_first, L1_attn_b_Wk, L1_attn_b_Wv, L1_attn_b_Wr, L1_attn_b_Wo, L1_attn_b_ffn_time_mix, L1_attn_b_ffn_combined_mix, L1_attn_b_Fk, L1_attn_b_Fv, L1_attn_b_Fr)
    x = x + _L1_ffn_ref(_layernorm(x, axis=-1), L1_ffn_gate_w, L1_ffn_w1, L1_ffn_w3, L1_ffn_w2)
    return x

_drawn_inputs = setup_inputs


def setup_inputs(seed=0):
    import zlib

    import numpy as np

    out = dict(_drawn_inputs(seed))
    spreads = {'L0_attn_a_ln_g': (1.0, 0.2),
     'L0_attn_a_ln_b': (0.0, 0.1),
     'L0_attn_b_bq': (0.0, 0.513),
     'L0_attn_b_bk': (0.0, 0.43),
     'L0_attn_b_bv': (0.0, 0.1),
     'L1_attn_a_in_proj_b': (0.0, 0.8),
     'L1_attn_a_out_b': (0.0, 0.1),
     'L1_attn_a_up_b': (0.0, 0.1),
     'L1_attn_b_ln1_g': (1.0, 0.2),
     'L1_attn_b_ln1_b': (0.0, 0.323),
     'L1_attn_b_ln2_g': (1.0, 0.2),
     'L1_attn_b_ln2_b': (0.0, 0.295),
     'L1_attn_b_att_combined_mix': (0.009999999776482582, 0.6),
     'L1_attn_b_time_first': (-1.2039728164672852, 0.6),
     'L1_attn_b_ffn_combined_mix': (0.009999999776482582, 0.6)}
    factors = {'L0_attn_a_b_mag': 4.028,
     'L1_attn_a_in_proj_w': 8.0,
     'L1_attn_a_out_w': 6.137,
     'L1_attn_a_up_w': 4.297,
     'L1_attn_b_att_time_mix': 8.0,
     'L1_attn_b_time_decay': 8.0,
     'L1_attn_b_Wk': 8.0,
     'L1_attn_b_Wv': 8.0,
     'L1_attn_b_Wr': 8.0,
     'L1_attn_b_Wo': 8.0,
     'L1_attn_b_ffn_time_mix': 8.0,
     'L1_attn_b_Fk': 8.0,
     'L1_attn_b_Fv': 8.0,
     'L1_attn_b_Fr': 8.0,
     'L1_ffn_gate_w': 8.0,
     'L1_ffn_w1': 8.0,
     'L1_ffn_w3': 8.0,
     'L1_ffn_w2': 8.0}
    for name, (base, spread) in spreads.items():
        noise = np.random.default_rng([zlib.crc32(name.encode()), seed]).standard_normal(out[name].shape)
        drawn = base * np.exp(spread * noise) if base else spread * noise
        out[name] = jnp.asarray(drawn.astype(out[name].dtype))
    for name, factor in factors.items():
        out[name] = (out[name] * factor).astype(out[name].dtype)
    return out
```

```python
from contextlib import ExitStack

import numpy as np

import concourse.bass as bass
from concourse import mybir

F32 = mybir.dt.float32
F32R = mybir.dt.float32r
BF16 = mybir.dt.bfloat16
ACT = mybir.ActivationFunctionType
ALU = mybir.AluOpType
AX = mybir.AxisListType

P = 128
B = 4
S = 512
NT = B * S
CH = 512
NC = NT // CH
TILES = NT // P
HEADS = 16
HD = P // HEADS
EPS = 1e-5
HIDDEN0, EXPERTS0, TOP0, SHARED0 = 128, 16, 4, 256
HIDDEN1, EXPERTS1, TOP1 = 352, 8, 2
TILES0 = (HIDDEN0 * EXPERTS0 + SHARED0) // P
TILES1 = HIDDEN1 * EXPERTS1 // P
SCALE0 = 2.5
CREDIT = 32
LEVELS = 4


class Signal:

    def __init__(self, sem, step=1):
        self.sem, self.step, self.base = sem, step, CREDIT * step

    def at(self, n):
        return n * self.step + self.base

    def advance(self, n):
        self.base += n * self.step


class Chain:

    def __init__(self, eng, signal, it=0, per=0):
        self.eng, self.own, self.first, self.n = eng, signal, it * per, 0

    def link(self, ins):
        self.n += 1
        ins.then_inc(self.own.sem, 1)
        self.eng.wait_ge(self.own.sem, self.own.at(self.first + self.n))


class Kernel:

    def __init__(self, nc, args, stack):
        self.nc, self.args, self.stack = nc, args, stack
        self.counts = {}
        self.names = 0

    def sb(self, name, shape, dt=F32, stack=None):
        self.names += 1
        return (stack or self.stack).enter_context(self.nc.sbuf_tensor(f"{name}_{self.names}", shape, dt))

    def ps(self, name, shape, dt=F32, stack=None):
        self.names += 1
        return (stack or self.stack).enter_context(self.nc.psum_tensor(f"{name}_{self.names}", shape, dt))

    def scratch(self, name, shape):
        self.names += 1
        return self.nc.dram_tensor(f"{name}_{self.names}", shape, BF16).ap()

    def count_of(self, name):
        return self.counts[name]


SIGNALS = {
    "tensor": ["centred", "variance", "gate_scores", "weights_turned", "gate_up", "routed_rows", "mlp_out", "magnitude_product", "angle_product", "context_mean", "hidden_product", "projection", "rotation", "values_turned", "peak_scores", "peaks_turned", "scores", "context_sums", "sums_spread", "level_product"],
    "scalar": ["squared", "weights_high", "logs", "rstd", "gate_probs", "gate_exp", "silu", "h_hi", "turned_kept", "sines", "sigmoids", "gelus", "projected", "values_copied", "peak_rows", "probs", "context_kept", "level_kept"],
    "vector": ["dve_step", "weights_low_odd", "normed", "norm_hi", "norm_lo", "routed", "weighted", "residual", "silu_up", "angles", "angle_reduced", "magnitudes", "magnitude_sum", "memories", "context_centred", "context_normed", "rotated", "values_kept", "parts_made", "peak_found", "peaks_split", "stacks_set", "upsampled", "mix_step", "mixed", "key_clamped", "averaged"],
    "gpsimd": ["pool_step", "weights_low_even", "h_lo", "weighted_waves", "values_spread", "key_values", "gated"],
    "dma": ["inputs_in", "weights_in_0", "weights_in_1", "weights_in_2", "weights_in_3", "consts_in", "out_stored", "parts_stored", "stack_in_0", "stack_in_1", "peaks_out", "peaks_in"],
}


def open_signals(k):
    for owner, names in SIGNALS.items():
        for name in names:
            k.counts[name] = Signal(k.stack.enter_context(k.nc.semaphore(name)), 16 if owner == "dma" else 1)
    with k.nc.Block() as block:
        def opened(owner):
            def program(eng):
                for name in SIGNALS[owner]:
                    eng.sem_inc(k.counts[name].sem, k.counts[name].base)
            return program

        block.tensor(opened("tensor"))
        block.scalar(opened("scalar"))
        block.vector(opened("vector"))
        block.gpsimd(opened("gpsimd"))
        block.sync(opened("dma"))


def layernorm(k, src, dst, gain=None, shift=None, parts=None, also=None):
    nc = k.nc
    centred, variance, squared, logs, rstd = (k.count_of(n) for n in ("centred", "variance", "squared", "logs", "rstd"))
    normed, step, norm_hi = k.count_of("normed"), k.count_of("dve_step"), k.count_of("norm_hi")
    with ExitStack() as st:
        xc = k.ps("xc", [P, NC, CH], stack=st)
        var = k.ps("var", [P, NC, CH], stack=st)
        sq = k.sb("sq", [P, NC, CH], stack=st)
        rs = k.sb("rs", [P, NC, CH], stack=st)
        with nc.Block() as block:

            @block.tensor
            def _(pe):
                for c in range(NC):
                    pe.matmul(xc[:, c, :], k.centring, src[:, c * CH:(c + 1) * CH], start=True, stop=True).then_inc(centred.sem, 1)
                for c in range(NC):
                    pe.wait_ge(squared.sem, squared.at(c + 1))
                    pe.matmul(var[:, c, :], k.mean_of[:, :], sq[:, c, :], start=True, stop=True).then_inc(variance.sem, 1)

            @block.scalar
            def _(act):
                for c in range(NC):
                    act.wait_ge(centred.sem, centred.at(c + 1))
                    act.activation(sq[:, c, :], xc[:, c, :], ACT.Square).then_inc(squared.sem, 1)
                for c in range(NC):
                    act.wait_ge(variance.sem, variance.at(c + 1))
                    act.activation(rs[:, c, :], var[:, c, :], ACT.Ln, bias=k.eps[:, 0:1]).then_inc(logs.sem, 1)
                for c in range(NC):
                    act.wait_ge(logs.sem, logs.at(c + 1))
                    act.activation(rs[:, c, :], rs[:, c, :], ACT.Exp, scale=-0.5).then_inc(rstd.sem, 1)
                if also:
                    also["scalar"](act)

            @block.vector
            def _(dve):
                for c in range(NC):
                    cols = slice(c * CH, (c + 1) * CH)
                    dve.wait_ge(rstd.sem, rstd.at(c + 1))
                    dve.tensor_tensor(dst[:, cols], xc[:, c, :], rs[:, c, :], ALU.mult).then_inc(normed.sem, 1)
                for c in range(NC):
                    cols = slice(c * CH, (c + 1) * CH)
                    dve.wait_ge(normed.sem, normed.at(c + 1))
                    if gain is not None:
                        dve.tensor_scalar(dst[:, cols], dst[:, cols], gain, shift, ALU.mult, ALU.add).then_inc(step.sem, 1)
                    if parts is not None:
                        dve.tensor_copy(parts[0][:, cols], dst[:, cols]).then_inc(norm_hi.sem, 1)
                if parts is not None:
                    for c in range(NC):
                        cols = slice(c * CH, (c + 1) * CH)
                        dve.wait_ge(norm_hi.sem, norm_hi.at(c + 1))
                        dve.tensor_tensor(parts[1][:, cols], dst[:, cols], parts[0][:, cols].bitcast(F32), ALU.subtract)
                if also:
                    also["vector"](dve)

            if also:
                block.gpsimd(also["gpsimd"])
                block.sync(also["sync"])
        for s, n in ((centred, NC), (variance, NC), (squared, NC), (logs, NC), (rstd, NC), (normed, NC),
                     (step, NC if gain is not None else 0), (norm_hi, NC if parts is not None else 0)):
            s.advance(n)


RAW = 4


def expert_loader(k, weights, tiles, hi, lo):
    weights_in = [k.count_of(f"weights_in_{n}") for n in range(RAW)]
    high = k.count_of("weights_high")
    low = k.count_of("weights_low_even"), k.count_of("weights_low_odd")
    raw = k.raw_weights
    width = 2 * 3 * P
    pieces = tiles // 2

    def part(n):
        return slice(n * width, (n + 1) * width)

    def round_high(act):
        for n in range(pieces):
            arrived = weights_in[n % RAW]
            act.wait_ge(arrived.sem, arrived.at(n // RAW + 1))
            act.activation(hi[:, part(n)], raw[:, n % RAW, :], ACT.Copy).then_inc(high.sem, 1)

    def rest_of(which):
        def program(eng):
            for n in range(which, pieces, 2):
                eng.wait_ge(high.sem, high.at(n + 1))
                eng.tensor_tensor(lo[:, part(n)], raw[:, n % RAW, :], hi[:, part(n)].bitcast(F32), ALU.subtract).then_inc(low[which].sem, 1)
        return program

    def load(sp):
        for n in range(pieces):
            if n >= RAW:
                used = low[n % 2]
                sp.wait_ge(used.sem, used.at((n - RAW) // 2 + 1))
            sp.dma_start(raw[:, n % RAW, :], weights[:, part(n)]).then_inc(weights_in[n % RAW].sem, 16)

    def done():
        for n in range(RAW):
            weights_in[n].advance(len(range(n, pieces, RAW)))
        high.advance(pieces)
        low[0].advance(len(range(0, pieces, 2)))
        low[1].advance(len(range(1, pieces, 2)))

    return {"scalar": round_high, "gpsimd": rest_of(0), "vector": rest_of(1), "sync": load}, done


def routed_mlp(k, x, hi, lo, w_hi, w_lo, tiles, experts, top, gate, rows, softmax):
    nc = k.nc
    scores, turned, gate_up = k.count_of("gate_scores"), k.count_of("weights_turned"), k.count_of("gate_up")
    rowsig, out_sum = k.count_of("routed_rows"), k.count_of("mlp_out")
    probs_ready, routed, step = k.count_of("gate_probs"), k.count_of("routed"), k.count_of("dve_step")
    kept = k.count_of("turned_kept")
    silu, h_hi, h_lo, weighted, silu_up, residual = (k.count_of(n) for n in ("silu", "h_hi", "h_lo", "weighted", "silu_up", "residual"))

    wide = k.route_rows
    with ExitStack() as st:
        logits = k.ps("logits", [P, TILES, experts], stack=st)
        rowsT = k.ps("rowsT", [P, TILES, P], BF16, stack=st)
        sc = k.sb("sc", [P, TILES, experts], stack=st)
        rest = k.sb("rest", [P, TILES, experts], stack=st)
        best = k.sb("best", [P, TILES, 8], stack=st)
        peak = k.sb("peak", [P, TILES], stack=st)
        total = k.sb("total", [P, TILES], stack=st)
        wts = k.sb("wts", [P, TILES, experts], stack=st)
        split = k.sb("split", [P, TILES, P], BF16, stack=st)
        with nc.Block() as block:

            @block.tensor
            def _(pe):
                for t in range(TILES):
                    last = pe.matmul(logits[:, t, :], x[:, t * P:(t + 1) * P], gate, start=(t == 0), stop=True, skip_group_check=True)
                last.then_inc(scores.sem, 1)
                pe.wait_ge(routed.sem, routed.at(1))
                for t in range(TILES):
                    last = pe.transpose(rowsT[:, t, :], split[:, t, :], k.ident_bf[:, :])
                    if t % 8 == 7:
                        last.then_inc(turned.sem, 1)

            @block.scalar
            def _(act):
                if softmax:
                    act.wait_ge(k.count_of("silu_up").sem, k.count_of("silu_up").at(1))
                    act.activation(sc[:, :, :], rest[:, :, :], ACT.Exp).then_inc(probs_ready.sem, 1)
                else:
                    act.wait_ge(scores.sem, scores.at(1))
                    act.activation(sc[:, :, :], logits[:, :, :], ACT.Sigmoid).then_inc(probs_ready.sem, 1)
                for n in range(2):
                    act.wait_ge(turned.sem, turned.at(n + 1))
                    act.activation(wide[:, n * 8 * P:(n + 1) * 8 * P].rearrange("p (t n) -> p t n", n=P),
                                   rowsT[:, n * 8:(n + 1) * 8, :], ACT.Copy)

            @block.vector
            def _(dve):
                chain = Chain(dve, step)

                def over(a):
                    return a[:, :].unsqueeze(2).to_broadcast([P, TILES, experts])

                dve.memset(split[:, :, :], 0.0).then_inc(step.sem, 1)
                chain.n += 1
                dve.wait_ge(step.sem, step.at(1))
                chain.link(dve.memset(split[:, :, 96:97], 1.0))
                if softmax:
                    dve.wait_ge(scores.sem, scores.at(1))
                    chain.link(dve.tensor_reduce(peak[:, :], logits[:, :, :], AX.X, ALU.max))
                    dve.tensor_tensor(rest[:, :, :], logits[:, :, :], over(peak), ALU.subtract).then_inc(silu_up.sem, 1)
                    dve.wait_ge(probs_ready.sem, probs_ready.at(1))
                    chain.link(dve.tensor_reduce(total[:, :], sc[:, :, :], AX.X, ALU.add))
                    chain.link(dve.reciprocal(total[:, :], total[:, :]))
                    chain.link(dve.tensor_tensor(sc[:, :, :], sc[:, :, :], over(total), ALU.mult))
                dve.wait_ge(probs_ready.sem, probs_ready.at(1))
                for t in range(TILES):
                    last = dve.max(best[:, t, :], sc[:, t, :])
                chain.link(last)
                chain.link(dve.memset(best[:, :, top:8], -2.0))
                for t in range(TILES):
                    last = dve.match_replace(rest[:, t, :], best[:, t, :], sc[:, t, :], -1.0)
                chain.link(last)
                chain.link(dve.scalar_tensor_tensor(out=wts[:, :, :], in0=rest[:, :, :], scalar=0.0, in1=sc[:, :, :], op0=ALU.max, op1=ALU.subtract))
                chain.link(dve.tensor_reduce(total[:, :], wts[:, :, :], AX.X, ALU.add))
                if softmax:
                    chain.link(dve.reciprocal(total[:, :], total[:, :]))
                    chain.link(dve.tensor_tensor(wts[:, :, :], wts[:, :, :], over(total), ALU.mult))
                else:
                    chain.link(dve.tensor_scalar(total[:, :], total[:, :], -1e-20, None, ALU.add))
                    chain.link(dve.reciprocal(total[:, :], total[:, :]))
                    chain.link(dve.tensor_tensor(wts[:, :, :], wts[:, :, :], over(total), ALU.mult))
                    chain.link(dve.tensor_scalar(wts[:, :, :], wts[:, :, :], SCALE0, None, ALU.mult))
                chain.link(dve.tensor_copy(split[:, :, 0:experts], wts[:, :, :]))
                chain.link(dve.tensor_tensor(wts[:, :, :], wts[:, :, :], split[:, :, 0:experts], ALU.subtract))
                chain.link(dve.tensor_copy(split[:, :, 32:32 + experts], wts[:, :, :]))
                dve.tensor_tensor(split[:, :, 64:64 + experts], wts[:, :, :], split[:, :, 32:32 + experts], ALU.subtract).then_inc(routed.sem, 1)
                step.advance(chain.n)
        for s, n in ((scores, 1), (turned, 2), (probs_ready, 1), (routed, 1), (silu_up, 1 if softmax else 0)):
            s.advance(n)

    LAG, RING, PAIR = 3, 4, 2
    assert PAIR * tiles % RING == 0 and tiles % 2 == 0 and LAG < RING
    with ExitStack() as st:
        g_ps = k.ps("g_ps", [P, 2, CH], stack=st)
        u_ps = k.ps("u_ps", [P, 2, CH], stack=st)
        r_ps = k.ps("r_ps", [P, 2, CH], stack=st)
        o_ps = k.ps("o_ps", [P, PAIR, CH], stack=st)
        sg = k.sb("sg", [P, RING, CH], stack=st)
        hw = k.sb("hw", [P, RING, CH], stack=st)
        hh = k.sb("hh", [P, RING, CH], F32R, stack=st)
        hl = k.sb("hl", [P, RING, CH], F32R, stack=st)

        def weight(part, j, which):
            at = (j * 3 + which) * P
            return part[:, at:at + P]

        def number(i, half, j):
            m = half * tiles + j
            return i * (PAIR * tiles) + m, m % RING, m % 2

        with nc.Block() as block:

            @block.tensor
            def _(pe):
                def up(i, half, j):
                    n, _, bank = number(i, half, j)
                    cols = bass.ts(i * PAIR + half, CH)
                    pe.wait_ge(weighted.sem, weighted.at(n - 1))
                    for which, banks in ((0, g_ps), (1, u_ps)):
                        at = banks[:, bank, :]
                        pe.matmul(at, weight(w_hi, j, which), hi[:, cols], start=True, stop=False)
                        pe.matmul(at, weight(w_lo, j, which), hi[:, cols], start=False, stop=False)
                        last = pe.matmul(at, weight(w_hi, j, which), lo[:, cols], start=False, stop=True)
                        if which == 0:
                            last.then_inc(gate_up.sem, 1)
                    pe.matmul(r_ps[:, bank, :], rows[:, j, :], wide[:, cols], start=True, stop=True).then_inc(rowsig.sem, 1)

                def down(i, half, j):
                    n, slot, _ = number(i, half, j)
                    at = o_ps[:, half, :]
                    if j == 0:
                        pe.wait_ge(residual.sem, residual.at(i * PAIR + half - 1))
                    pe.wait_ge(h_hi.sem, h_hi.at(n + 1))
                    pe.matmul(at, weight(w_hi, j, 2), hh[:, slot, :], start=(j == 0), stop=False)
                    pe.matmul(at, weight(w_lo, j, 2), hh[:, slot, :], start=False, stop=False)
                    pe.wait_ge(h_lo.sem, h_lo.at(n + 1))
                    last = pe.matmul(at, weight(w_hi, j, 2), hl[:, slot, :], start=False, stop=(j == tiles - 1))
                    if j == tiles - 1:
                        last.then_inc(out_sum.sem, 1)

                def pair(i, more):
                    for half in range(PAIR):
                        for j in range(tiles):
                            down(i, half, j)
                            if j + LAG < tiles:
                                up(i, half, j + LAG)
                            elif half == 0:
                                up(i, 1, j + LAG - tiles)
                            elif more:
                                up(i + 1, 0, j + LAG - tiles)

                for j in range(LAG):
                    up(0, 0, j)
                with pe.Fori(0, NC // PAIR - 1) as i:
                    pair(i, True)
                pair(NC // PAIR - 1, False)

            def tiles_of(i):
                for half in range(PAIR):
                    for j in range(tiles):
                        yield half, j, *number(i, half, j)

            @block.scalar
            def _(act):
                def gates(n, slot, bank):
                    act.wait_ge(gate_up.sem, gate_up.at(n + 1))
                    act.activation(sg[:, slot, :], g_ps[:, bank, :], ACT.Silu).then_inc(silu.sem, 1)

                def high(n, slot):
                    act.wait_ge(weighted.sem, weighted.at(n + 1))
                    act.activation(hh[:, slot, :], hw[:, slot, :], ACT.Copy).then_inc(h_hi.sem, 1)

                def pair(i, more):
                    m = PAIR * tiles
                    for half, j, n, slot, bank in tiles_of(i):
                        if half * tiles + j + 1 < m or more:
                            gates(n + 1, (slot + 1) % RING, 1 - bank)
                        high(n, slot)

                gates(0, 0, 0)
                with act.Fori(0, NC // PAIR - 1) as i:
                    pair(i, True)
                pair(NC // PAIR - 1, False)

            @block.vector
            def _(dve):
                with dve.Fori(0, NC // PAIR) as i:
                    for half, j, n, slot, bank in tiles_of(i):
                        dve.wait_ge(silu.sem, silu.at(n + 1))
                        dve.wait_ge(rowsig.sem, rowsig.at(n + 1))
                        dve.tensor_tensor(hw[:, slot, :], sg[:, slot, :], u_ps[:, bank, :], ALU.mult).then_inc(silu_up.sem, 1)
                        dve.wait_ge(silu_up.sem, silu_up.at(n + 1))
                        dve.tensor_tensor(hw[:, slot, :], hw[:, slot, :], r_ps[:, bank, :], ALU.mult).then_inc(weighted.sem, 1)
                        if j == tiles - 1:
                            cols = bass.ts(i * PAIR + half, CH)
                            dve.wait_ge(out_sum.sem, out_sum.at(i * PAIR + half + 1))
                            dve.tensor_tensor(k.X[:, cols], k.X[:, cols], o_ps[:, half, :], ALU.add).then_inc(residual.sem, 1)

            @block.gpsimd
            def _(pool):
                with pool.Fori(0, NC // PAIR) as i:
                    for half, j, n, slot, bank in tiles_of(i):
                        pool.wait_ge(h_hi.sem, h_hi.at(n + 1))
                        pool.tensor_tensor(hl[:, slot, :], hw[:, slot, :], hh[:, slot, :].bitcast(F32), ALU.subtract).then_inc(h_lo.sem, 1)
        for s in (gate_up, rowsig, silu, silu_up, weighted, h_hi, h_lo):
            s.advance(NC * tiles)
        for s in (out_sum, residual):
            s.advance(NC)


TWO_PI = 2 * np.pi
TURN = (6.28125, float(np.float32(0.0019350051879882812)), float(TWO_PI - 6.28125 - 0.0019350051879882812))
ROUND = 1.5 * 2.0 ** 23
ALMOST_PI = 3.1415925


def turn_down(chain, dve, angle, turns):
    chain.link(dve.tensor_scalar(turns, angle, 1 / TWO_PI, ROUND, ALU.mult, ALU.add))
    chain.link(dve.tensor_scalar(turns, turns, ROUND, None, ALU.subtract))
    for part in TURN:
        chain.link(dve.scalar_tensor_tensor(out=angle, in0=turns, scalar=-part, in1=angle, op0=ALU.mult, op1=ALU.add))
    chain.link(dve.tensor_scalar(angle, angle, ALMOST_PI, -ALMOST_PI, ALU.min, ALU.max))


def phase_memory(k, x, mats, vec, positions):
    nc = k.nc
    sig = k.count_of
    with ExitStack() as st:
        phi = k.sb("phi", [P, S], stack=st)
        cos = k.sb("cos", [P, S], stack=st)
        sin = k.sb("sin", [P, S], stack=st)
        turns = k.sb("turns", [P, S], stack=st)
        ones = k.sb("ones_row", [P, S], stack=st)
        mem_r = k.sb("mem_r", [P, NT], stack=st)
        mem_i = k.sb("mem_i", [P, NT], stack=st)
        angle = k.sb("angle", [P, NT], stack=st)
        inv = k.sb("inv", [P, NT], stack=st)
        context = k.sb("context", [P, 4, NT], stack=st)

        with ExitStack() as st2:
            mag = k.sb("mag", [P, NT], stack=st2)
            wr = k.sb("wr", [P, NT], stack=st2)
            wi = k.sb("wi", [P, NT], stack=st2)
            wx = k.sb("wx", [P, NT], stack=st2)
            m_ps = k.ps("m_ps", [P, B, S], stack=st2)
            q_ps = k.ps("q_ps", [P, B, S], stack=st2)
            with nc.Block() as block:

                @block.tensor
                def _(pe):
                    with pe.Fori(0, B) as b:
                        cols = bass.ts(b, S)
                        pe.matmul(m_ps[:, b, :], mats("W_mag"), x[:, cols], start=True, stop=True).then_inc(sig("magnitude_product").sem, 1)
                        pe.matmul(q_ps[:, b, :], mats("W_q"), x[:, cols], start=True, stop=True).then_inc(sig("angle_product").sem, 1)

                @block.scalar
                def _(act):
                    act.wait_ge(sig("angle_reduced").sem, sig("angle_reduced").at(1))
                    act.activation(sin[:, :], phi[:, :], ACT.Sin).then_inc(sig("sines").sem, 1)
                    act.activation(cos[:, :], phi[:, :], ACT.Abs).then_inc(sig("sines").sem, 1)
                    act.wait_ge(sig("sines").sem, sig("sines").at(2))
                    act.activation(cos[:, :], cos[:, :], ACT.Sin, scale=-1.0, bias=k.half_pi[:, 0:1]).then_inc(sig("sines").sem, 1)
                    with act.Fori(0, B) as b:
                        act.wait_ge(sig("magnitude_product").sem, sig("magnitude_product").at(b + 1))
                        act.activation(mag[:, bass.ts(b, S)], m_ps[:, b, :], ACT.Sigmoid, bias=vec("b_mag")).then_inc(sig("sigmoids").sem, 1)
                    for b in range(B):
                        cols = bass.ts(b, S)
                        act.wait_ge(sig("magnitude_sum").sem, sig("magnitude_sum").at(b + 1))
                        act.activation(inv[:, cols], inv[:, cols], ACT.Ln, bias=k.tiny[:, 0:1]).then_inc(sig("logs").sem, 1)
                    for b in range(B):
                        cols = bass.ts(b, S)
                        act.wait_ge(sig("logs").sem, sig("logs").at(b + 1))
                        act.activation(inv[:, cols], inv[:, cols], ACT.Exp, scale=-0.5).then_inc(sig("rstd").sem, 1)

                @block.vector
                def _(dve):
                    chain = Chain(dve, sig("dve_step"))
                    chain.link(dve.memset(ones[:, :], 1.0))
                    chain.link(dve.tensor_scalar(phi[:, :], positions, vec("phases"), 0.01, ALU.mult, ALU.mult))
                    with dve.Fori(0, B) as b:
                        dve.wait_ge(sig("angle_product").sem, sig("angle_product").at(b + 1))
                        dve.scalar_tensor_tensor(out=angle[:, bass.ts(b, S)], in0=q_ps[:, b, :], scalar=vec("b_q"), in1=phi[:, :],
                                                 op0=ALU.add, op1=ALU.add).then_inc(sig("angles").sem, 1)
                    dve.wait_ge(sig("angles").sem, sig("angles").at(B))
                    turn_down(chain, dve, phi[:, :], turns[:, :])
                    dve.sem_inc(sig("angle_reduced").sem, 1)
                    sig("dve_step").advance(chain.n)
                    with dve.Fori(0, B) as b:
                        cols = bass.ts(b, S)
                        dve.wait_ge(sig("sigmoids").sem, sig("sigmoids").at(b + 1))
                        dve.tensor_scalar(mag[:, cols], mag[:, cols], 5.0, None, ALU.mult).then_inc(sig("magnitudes").sem, 1)
                        dve.wait_ge(sig("magnitudes").sem, sig("magnitudes").at(b + 1))
                        dve.tensor_tensor_scan(inv[:, cols], ones[:, :], mag[:, cols], 0.0, ALU.mult, ALU.add).then_inc(sig("magnitude_sum").sem, 1)
                        dve.wait_ge(sig("weighted_waves").sem, sig("weighted_waves").at(b * 2 + 1))
                        dve.tensor_tensor_scan(mem_r[:, cols], ones[:, :], wr[:, cols], 0.0, ALU.mult, ALU.add).then_inc(sig("memories").sem, 1)
                        dve.wait_ge(sig("weighted_waves").sem, sig("weighted_waves").at(b * 2 + 2))
                        dve.tensor_tensor_scan(mem_i[:, cols], ones[:, :], wi[:, cols], 0.0, ALU.mult, ALU.add).then_inc(sig("memories").sem, 1)
                    with dve.Fori(0, B) as b:
                        cols = bass.ts(b, S)
                        dve.wait_ge(sig("rstd").sem, sig("rstd").at(b + 1))
                        dve.wait_ge(sig("memories").sem, sig("memories").at(b * 2 + 2))
                        dve.tensor_tensor(mem_r[:, cols], mem_r[:, cols], inv[:, cols], ALU.mult)
                        dve.tensor_tensor(mem_i[:, cols], mem_i[:, cols], inv[:, cols], ALU.mult)

                @block.gpsimd
                def _(pool):
                    pool.wait_ge(sig("sines").sem, sig("sines").at(3))
                    with pool.Fori(0, B) as b:
                        cols = bass.ts(b, S)
                        pool.wait_ge(sig("magnitudes").sem, sig("magnitudes").at(b + 1))
                        pool.tensor_tensor(wx[:, cols], mag[:, cols], x[:, cols], ALU.mult).then_inc(sig("pool_step").sem, 1)
                        pool.wait_ge(sig("pool_step").sem, sig("pool_step").at(b + 1))
                        pool.tensor_tensor(wr[:, cols], wx[:, cols], cos[:, :], ALU.mult).then_inc(sig("weighted_waves").sem, 1)
                        pool.tensor_tensor(wi[:, cols], wx[:, cols], sin[:, :], ALU.mult).then_inc(sig("weighted_waves").sem, 1)
            for name, n in (("magnitude_product", B), ("angle_product", B), ("angle_reduced", 1), ("sines", 3), ("sigmoids", B), ("logs", B), ("rstd", B),
                            ("angles", B), ("magnitudes", B), ("magnitude_sum", B), ("memories", 2 * B), ("pool_step", B), ("weighted_waves", 2 * B)):
                sig(name).advance(n)

        with ExitStack() as st2:
            sq = k.sb("sq", [P, NT], stack=st2)
            cq = k.sb("cq", [P, NT], stack=st2)
            a = k.sb("a", [P, S], stack=st2)
            steps = 6
            with nc.Block() as block:

                @block.vector
                def _(dve):
                    with dve.Fori(0, B) as b:
                        chain = Chain(dve, sig("dve_step"), b, steps)
                        turn_down(chain, dve, angle[:, bass.ts(b, S)], turns[:, :])
                        assert chain.n == steps
                        dve.sem_inc(sig("angle_reduced").sem, 1)
                    sig("dve_step").advance(B * steps)
                    steps2 = 6
                    with dve.Fori(0, B) as b:
                        cols = bass.ts(b, S)
                        chain = Chain(dve, sig("dve_step"), b, steps2)
                        dve.wait_ge(sig("sines").sem, sig("sines").at(b * 3 + 3))
                        chain.link(dve.tensor_tensor(a[:, :], mem_i[:, cols], sq[:, cols], ALU.mult))
                        chain.link(dve.tensor_tensor(context[:, 2, cols], mem_r[:, cols], cq[:, cols], ALU.mult))
                        chain.link(dve.tensor_tensor(context[:, 2, cols], context[:, 2, cols], a[:, :], ALU.add))
                        chain.link(dve.tensor_tensor(a[:, :], mem_r[:, cols], sq[:, cols], ALU.mult))
                        chain.link(dve.tensor_tensor(context[:, 3, cols], mem_i[:, cols], cq[:, cols], ALU.mult))
                        chain.link(dve.tensor_tensor(context[:, 3, cols], context[:, 3, cols], a[:, :], ALU.subtract))
                        assert chain.n == steps2
                    sig("dve_step").advance(B * steps2)

                @block.scalar
                def _(act):
                    for b in range(B):
                        cols = bass.ts(b, S)
                        act.wait_ge(sig("angle_reduced").sem, sig("angle_reduced").at(b + 1))
                        act.activation(sq[:, cols], angle[:, cols], ACT.Sin).then_inc(sig("sines").sem, 1)
                        act.activation(cq[:, cols], angle[:, cols], ACT.Abs).then_inc(sig("sines").sem, 1)
                        act.wait_ge(sig("sines").sem, sig("sines").at(b * 3 + 2))
                        act.activation(cq[:, cols], cq[:, cols], ACT.Sin, scale=-1.0, bias=k.half_pi[:, 0:1]).then_inc(sig("sines").sem, 1)

                @block.gpsimd
                def _(pool):
                    with pool.Fori(0, B) as b:
                        cols = bass.ts(b, S)
                        pool.tensor_tensor(context[:, 0, cols], x[:, cols], cos[:, :], ALU.mult)
                        pool.tensor_tensor(context[:, 1, cols], x[:, cols], sin[:, :], ALU.mult)
            sig("angle_reduced").advance(B)
            sig("sines").advance(3 * B)

        with ExitStack() as st2:
            mu = k.ps("mu", [P, 2, S], stack=st2)
            var = k.ps("var", [P, 2, S], stack=st2)
            h_ps = k.ps("h_ps", [P, 2, S], stack=st2)
            o_ps = k.ps("o_ps", [P, 2, S], stack=st2)
            sqr = k.sb("sqr", [P, 4, S], stack=st2)
            rs = k.sb("rs", [P, NT], stack=st2)
            hidden = k.sb("hidden", [P, 2, S], stack=st2)
            with nc.Block() as block:

                def variances(pe, b):
                    for f in range(4):
                        pe.wait_ge(sig("squared").sem, sig("squared").at(b * 4 + f + 1))
                        last = pe.matmul(var[:, b % 2, :], k.mean_of_4[:, :], sqr[:, f, :], start=(f == 0), stop=(f == 3))
                    last.then_inc(sig("variance").sem, 1)

                @block.tensor
                def _(pe):
                    for b in range(B):
                        for f in range(4):
                            last = pe.matmul(mu[:, b % 2, :], k.mean_of_4[:, :], context[:, f, b * S:(b + 1) * S], start=(f == 0), stop=(f == 3))
                        last.then_inc(sig("context_mean").sem, 1)
                        if b < 1:
                            continue
                        variances(pe, b - 1)
                    variances(pe, B - 1)
                    with pe.Fori(0, B) as b:
                        cols = bass.ts(b, S)
                        for g in range(2):
                            pe.wait_ge(sig("gelus").sem, sig("gelus").at(b * 2 + g - 1))
                            for f in range(4):
                                pe.wait_ge(sig("context_normed").sem, sig("context_normed").at(b * 4 + f + 1))
                                last = pe.matmul(h_ps[:, g, :], mats("W1", f * 2 + g), context[:, f, cols], start=(f == 0), stop=(f == 3))
                            last.then_inc(sig("hidden_product").sem, 1)
                        pe.wait_ge(sig("residual").sem, sig("residual").at(b))
                        for g in range(2):
                            pe.wait_ge(sig("gelus").sem, sig("gelus").at(b * 2 + g + 1))
                            last = pe.matmul(o_ps[:, 0, :], mats("W2", g), hidden[:, g, :], start=(g == 0), stop=(g == 1))
                        last.then_inc(sig("mlp_out").sem, 1)

                @block.scalar
                def _(act):
                    for b in range(B):
                        cols = slice(b * S, (b + 1) * S)
                        act.wait_ge(sig("variance").sem, sig("variance").at(b))
                        for f in range(4):
                            act.wait_ge(sig("context_centred").sem, sig("context_centred").at(b * 4 + f + 1))
                            act.activation(sqr[:, f, :], context[:, f, cols], ACT.Square).then_inc(sig("squared").sem, 1)
                        act.wait_ge(sig("variance").sem, sig("variance").at(b + 1))
                        act.activation(rs[:, cols], var[:, b % 2, :], ACT.Ln, bias=k.eps[:, 0:1]).then_inc(sig("rstd").sem, 1)
                        act.wait_ge(sig("rstd").sem, sig("rstd").at(b * 2 + 1))
                        act.activation(rs[:, cols], rs[:, cols], ACT.Exp, scale=-0.5).then_inc(sig("rstd").sem, 1)
                    with act.Fori(0, B) as b:
                        for g in range(2):
                            act.wait_ge(sig("hidden_product").sem, sig("hidden_product").at(b * 2 + g + 1))
                            act.wait_ge(sig("mlp_out").sem, sig("mlp_out").at(b))
                            act.activation(hidden[:, g, :], h_ps[:, g, :], ACT.Gelu, bias=vec("b1", g)).then_inc(sig("gelus").sem, 1)

                @block.vector
                def _(dve):
                    def centre(b):
                        cols = slice(b * S, (b + 1) * S)
                        dve.wait_ge(sig("context_mean").sem, sig("context_mean").at(b + 1))
                        for f in range(4):
                            dve.tensor_tensor(context[:, f, cols], context[:, f, cols], mu[:, b % 2, :], ALU.subtract).then_inc(sig("context_centred").sem, 1)

                    def norm(b):
                        cols = slice(b * S, (b + 1) * S)
                        dve.wait_ge(sig("rstd").sem, sig("rstd").at(b * 2 + 2))
                        for f in range(4):
                            dve.tensor_tensor(context[:, f, cols], context[:, f, cols], rs[:, cols], ALU.mult).then_inc(sig("dve_step").sem, 1)
                        for f in range(4):
                            dve.wait_ge(sig("dve_step").sem, sig("dve_step").at(b * 4 + f + 1))
                            dve.tensor_scalar(context[:, f, cols], context[:, f, cols], vec("ln_g", f), vec("ln_b", f), ALU.mult, ALU.add).then_inc(sig("context_normed").sem, 1)

                    centre(0)
                    for b in range(B):
                        if b + 1 < B:
                            centre(b + 1)
                        norm(b)
                    with dve.Fori(0, B) as b:
                        cols = bass.ts(b, S)
                        dve.tensor_tensor(k.X[:, cols], k.X[:, cols], x[:, cols], ALU.add).then_inc(sig("normed").sem, 1)
                        dve.wait_ge(sig("mlp_out").sem, sig("mlp_out").at(b + 1))
                        dve.wait_ge(sig("normed").sem, sig("normed").at(b + 1))
                        dve.scalar_tensor_tensor(out=k.X[:, cols], in0=o_ps[:, 0, :], scalar=vec("b2"), in1=k.X[:, cols],
                                                 op0=ALU.add, op1=ALU.add).then_inc(sig("residual").sem, 1)
            for name, n in (("context_mean", B), ("context_centred", 4 * B), ("squared", 4 * B), ("variance", B), ("rstd", 2 * B), ("dve_step", 4 * B),
                            ("context_normed", 4 * B), ("hidden_product", 2 * B), ("gelus", 2 * B), ("mlp_out", B), ("normed", B), ("residual", B)):
                sig(name).advance(n)


PARTS = 3
PAIRS = PARTS * PARTS
STACK = PAIRS * HD
HALF = HEADS // 2
VCOLS = HALF * HD + HALF
VWIDE = HALF * (VCOLS + 1) + HALF * HD
SOFTMAX_SCALE = float(HD) ** -0.5


def attention(k, x, ctx, seq, chunks, chunk, weight, bias, rope=None, residual=False):
    nc = k.nc
    sig = k.count_of
    tile = min(P, seq)
    per = chunk // tile
    assert per == 4 and chunks * chunk == x.shape[1]
    tokens = chunks * chunk

    def keys_of(t):
        g = t * tile // seq
        return slice(g * seq, (g + 1) * seq)

    parts_dram = k.scratch("parts", [2, PARTS, P, tokens])
    peaks_dram = k.scratch("peaks", [2, PARTS * HALF, chunk])

    with ExitStack() as st:
        values = k.sb("values", [P, chunks * per, P], stack=st)
        sums = k.sb("sums", [32 + HALF, tokens], stack=st)

        with ExitStack() as st2:
            proj = k.ps("proj", [P, 3, 512], stack=st2)
            rot = k.ps("rot", [P, 2, 512], stack=st2)
            vt = k.ps("vt", [P, 512], stack=st2)
            biased = k.sb("biased", [P, 3, chunk], stack=st2)
            turned = k.sb("turned", [P, 2, chunk], stack=st2)
            parts = k.sb("parts", [P, chunks, 2 * PARTS, chunk], BF16, stack=st2)
            with nc.Block() as block:

                @block.tensor
                def _(pe):
                    with pe.Fori(0, chunks) as c:
                        for w in range(3):
                            pe.wait_ge(sig("projected").sem, sig("projected").at(c * 3 + w - 2))
                            pe.matmul(proj[:, w, 0:chunk], weight(w), x[:, bass.ts(c, chunk)], start=True, stop=True).then_inc(sig("projection").sem, 1)
                        if rope:
                            for w in range(2):
                                pe.wait_ge(sig("projected").sem, sig("projected").at(c * 3 + w + 1))
                                pe.wait_ge(sig("rotated").sem, sig("rotated").at(c * 2 + w - 1))
                                pe.matmul(rot[:, w, 0:chunk], rope[0], biased[:, w, :], start=True, stop=True).then_inc(sig("rotation").sem, 1)
                        pe.wait_ge(sig("projected").sem, sig("projected").at(c * 3 + 3))
                        pe.wait_ge(sig("values_kept").sem, sig("values_kept").at(c))
                        for t in range(per):
                            last = pe.transpose(vt[0:tile, t * P:(t + 1) * P], biased[:, 2, t * tile:(t + 1) * tile], k.ident)
                        last.then_inc(sig("values_turned").sem, 1)

                @block.scalar
                def _(act):
                    with act.Fori(0, chunks) as c:
                        for w in range(3):
                            act.wait_ge(sig("projection").sem, sig("projection").at(c * 3 + w + 1))
                            if w < 2:
                                act.wait_ge(sig("parts_made").sem, sig("parts_made").at(c * 2 + w - 1))
                            else:
                                act.wait_ge(sig("values_turned").sem, sig("values_turned").at(c))
                            act.activation(biased[:, w, :], proj[:, w, 0:chunk], ACT.Identity, bias=bias(w)).then_inc(sig("projected").sem, 1)

                @block.vector
                def _(dve):
                    steps = 2 * (3 + (2 if rope else 0))
                    with dve.Fori(0, chunks) as c:
                        chain = Chain(dve, sig("dve_step"), c, steps)
                        for w in range(2):
                            src = biased[:, w, :]
                            dve.wait_ge(sig("projected").sem, sig("projected").at(c * 3 + w + 1))
                            if rope:
                                chain.link(dve.tensor_tensor(turned[:, w, :], biased[:, w, :], rope[1], ALU.mult))
                                dve.wait_ge(sig("rotation").sem, sig("rotation").at(c * 2 + w + 1))
                                dve.tensor_tensor(biased[:, w, :], rot[:, w, 0:chunk], rope[2], ALU.mult).then_inc(sig("rotated").sem, 1)
                                dve.wait_ge(sig("rotated").sem, sig("rotated").at(c * 2 + w + 1))
                                chain.link(dve.tensor_tensor(biased[:, w, :], biased[:, w, :], turned[:, w, :], ALU.add))
                            at = [parts[:, c, w * PARTS + n, :] for n in range(PARTS)]
                            chain.link(dve.tensor_copy(at[0], src))
                            chain.link(dve.tensor_tensor(turned[:, w, :], src, at[0], ALU.subtract))
                            chain.link(dve.tensor_copy(at[1], turned[:, w, :]))
                            dve.tensor_tensor(at[2], turned[:, w, :], at[1], ALU.subtract).then_inc(sig("parts_made").sem, 1)
                        assert chain.n == steps
                        dve.wait_ge(sig("values_turned").sem, sig("values_turned").at(c + 1))
                        dve.tensor_copy(values[0:tile, bass.ts(c, per), :], vt[0:tile, :].rearrange("p (t n) -> p t n", n=P)).then_inc(sig("values_kept").sem, 1)
                    sig("dve_step").advance(chunks * steps)

                @block.gpsimd
                def _(pool):
                    pool.memset(sums[:, :], 0.0)

                @block.sync
                def _(sp):
                    with sp.Fori(0, chunks) as c:
                        for w in range(2):
                            sp.wait_ge(sig("parts_made").sem, sig("parts_made").at(c * 2 + w + 1))
                            sp.dma_start(parts_dram[w, :, :, bass.ts(c, chunk)].rearrange("n p t -> p n t"),
                                         parts[:, c, w * PARTS:(w + 1) * PARTS, :]).then_inc(sig("parts_stored").sem, 16)
                    sp.wait_ge(sig("parts_stored").sem, sig("parts_stored").at(2 * chunks))
            for name, n in (("projection", 3 * chunks), ("projected", 3 * chunks), ("rotation", 2 * chunks if rope else 0),
                            ("rotated", 2 * chunks if rope else 0), ("values_turned", chunks), ("values_kept", chunks),
                            ("parts_made", 2 * chunks), ("parts_stored", 2 * chunks)):
                sig(name).advance(n)

        with ExitStack() as st2:
            s_ps = k.ps("s_ps", [P, per, 512], stack=st2)
            m_ps = k.ps("m_ps", [P, 2, 512], stack=st2)
            o_ps = k.ps("o_ps", [P, 512], stack=st2)
            t_ps = k.ps("t_ps", [P, 1024], BF16, stack=st2)
            queries = k.sb("queries", [P, 2, HALF, chunk], BF16, stack=st2)
            keys = k.sb("keys", [P, 2, HALF, chunk], BF16, stack=st2)
            spread = k.sb("spread", [P, 2 * per, VWIDE], stack=st2)
            probs = k.sb("probs", [P, 2, per, seq], stack=st2)
            peak = k.sb("peak", [P, per, HALF], stack=st2)
            peak_parts = k.sb("peak_parts", [P, per, PARTS * HALF], BF16, stack=st2)
            peak_rows = k.sb("peak_rows", [PARTS * HALF, chunk], BF16, stack=st2)
            last_unit = 2 * chunks - 1
            SCORES = 2 * HALF
            BLOCKS = per * HALF
            DMAS = 2 * PAIRS
            FIRST, LAST = 2, 7

            def units(eng, body):
                if chunks > 1:
                    with eng.Fori(0, chunks - 1) as c:
                        body(c, 0, True)
                        body(c, 1, True)
                body(chunks - 1, 0, True)
                body(chunks - 1, 1, False)

            with nc.Block() as block:

                @block.tensor
                def _(pe):
                    def peaks(u, slot, first, last):
                        for block_ in range(first, last):
                            h, t = divmod(block_, per)
                            n = u * BLOCKS + block_
                            pe.wait_ge(sig("peak_found").sem, sig("peak_found").at(n - 1))
                            if block_ == 0:
                                stack_in = sig(f"stack_in_{slot}")
                                pe.wait_ge(stack_in.sem, stack_in.at((u - slot) * (DMAS // 2) + DMAS) if isinstance(u, int)
                                           else stack_in.at(u * (DMAS // 2) + (DMAS if slot == 0 else DMAS // 2)))
                            pe.matmul(m_ps[0:tile, t % 2, 0:seq], queries[0:STACK, slot, h, t * tile:(t + 1) * tile],
                                      keys[0:STACK, slot, h, keys_of(t)], start=True, stop=True).then_inc(sig("peak_scores").sem, 1)

                    def peaks_turned(u):
                        pe.wait_ge(sig("peaks_split").sem, sig("peaks_split").at(u + 1))
                        for t in range(per):
                            last = pe.transpose(t_ps[0:PARTS * HALF, t * tile:(t + 1) * tile], peak_parts[0:tile, t, :], k.ident_bf[0:tile, 0:tile])
                        last.then_inc(sig("peaks_turned").sem, 1)

                    def scores(u, slot, h):
                        if h == 0:
                            pe.wait_ge(sig("peaks_in").sem, sig("peaks_in").at(u + 1))
                        for t in range(per):
                            n = u * SCORES + h * 2 + t // 2
                            if t % 2 == 0:
                                pe.wait_ge(sig("probs").sem, sig("probs").at(n - 1))
                            last = pe.matmul(s_ps[0:tile, t, 0:seq], keys[0:STACK + PARTS, slot, h, t * tile:(t + 1) * tile],
                                             queries[0:STACK + PARTS, slot, h, keys_of(t)], start=True, stop=True)
                            if t % 2 == 1:
                                last.then_inc(sig("scores").sem, 1)

                    def context(u, half, h, between=None):
                        if h == 0:
                            pe.wait_ge(sig("values_spread").sem, sig("values_spread").at(u + 1))
                            pe.wait_ge(sig("context_kept").sem, sig("context_kept").at(u * 2))
                        for t in range(per):
                            if t % 2 == 0:
                                pe.wait_ge(sig("probs").sem, sig("probs").at(u * SCORES + h * 2 + t // 2 + 1))
                            last = pe.matmul(o_ps[0:VCOLS, keys_of(t)], spread[0:tile, half * per + t, h * VCOLS:(h + 1) * VCOLS],
                                             probs[0:tile, h % 2, t, :], start=(h == 0 and t == 0), stop=(h == HALF - 1 and t == per - 1),
                                             skip_group_check=True)
                            if t == per - 1:
                                last.then_inc(sig("context_sums").sem, 1)
                            if between:
                                between()

                    def unit(c, half, more):
                        u = c * 2 + half
                        spots = (LAST - FIRST) * per
                        used = [0]

                        def between():
                            used[0] += 1
                            peaks(u + 1, 1 - half, -(-(used[0] - 1) * BLOCKS // spots), -(-used[0] * BLOCKS // spots))

                        for h in range(HALF):
                            scores(u, half, h)
                            if h > 0:
                                context(u, half, h - 1, between if more and FIRST <= h < LAST else None)
                            if more and h == HALF - 1:
                                peaks_turned(u + 1)
                        context(u, half, HALF - 1)

                    peaks(0, 0, 0, BLOCKS)
                    peaks_turned(0)
                    units(pe, unit)

                @block.scalar
                def _(act):
                    def peak_rows_kept(u):
                        act.wait_ge(sig("peaks_turned").sem, sig("peaks_turned").at(u + 1))
                        act.wait_ge(sig("peaks_out").sem, sig("peaks_out").at(u))
                        act.activation(peak_rows[:, :], t_ps[0:PARTS * HALF, 0:chunk], ACT.Copy).then_inc(sig("peak_rows").sem, 1)

                    def unit(c, half, more):
                        u = c * 2 + half
                        for h in range(HALF):
                            act.wait_ge(sig("context_sums").sem, sig("context_sums").at(u * HALF + h - 1))
                            for two in range(2):
                                act.wait_ge(sig("scores").sem, sig("scores").at(u * SCORES + h * 2 + two + 1))
                                act.activation(probs[0:tile, h % 2, two * 2:two * 2 + 2, :], s_ps[0:tile, two * 2:two * 2 + 2, 0:seq], ACT.Exp,
                                               scale=SOFTMAX_SCALE).then_inc(sig("probs").sem, 1)
                        if more:
                            peak_rows_kept(u + 1)
                        act.wait_ge(sig("context_sums").sem, sig("context_sums").at(u * HALF + HALF))
                        cols = bass.ts(c, chunk)
                        act.activation(ctx[half * 64:half * 64 + 64, cols], o_ps[0:HALF * HD, 0:chunk], ACT.Copy).then_inc(sig("context_kept").sem, 1)
                        act.activation(sums[half * 32:half * 32 + HALF, cols], o_ps[HALF * HD:VCOLS, 0:chunk], ACT.Copy).then_inc(sig("context_kept").sem, 1)

                    peak_rows_kept(0)
                    units(act, unit)

                @block.vector
                def _(dve):
                    steps = 4

                    def peaks(u):
                        for h in range(HALF):
                            for t in range(per):
                                n = u * BLOCKS + h * per + t
                                dve.wait_ge(sig("peak_scores").sem, sig("peak_scores").at(n + 1))
                                dve.tensor_reduce(peak[0:tile, t, h:h + 1], m_ps[0:tile, t % 2, 0:seq], AX.X, ALU.max).then_inc(sig("peak_found").sem, 1)
                        dve.wait_ge(sig("peak_found").sem, sig("peak_found").at(u * BLOCKS + BLOCKS))
                        dve.wait_ge(sig("peaks_turned").sem, sig("peaks_turned").at(u))
                        chain = Chain(dve, sig("dve_step"), u, steps)
                        at = [peak_parts[0:tile, :, n * HALF:(n + 1) * HALF] for n in range(PARTS)]
                        chain.link(dve.tensor_scalar(peak[0:tile, :, :], peak[0:tile, :, :], -1.0, None, ALU.mult))
                        chain.link(dve.tensor_copy(at[0], peak[0:tile, :, :]))
                        chain.link(dve.tensor_tensor(peak[0:tile, :, :], peak[0:tile, :, :], at[0], ALU.subtract))
                        chain.link(dve.tensor_copy(at[1], peak[0:tile, :, :]))
                        assert chain.n == steps
                        dve.tensor_tensor(at[2], peak[0:tile, :, :], at[1], ALU.subtract).then_inc(sig("peaks_split").sem, 1)

                    def unit(c, half, more):
                        u = c * 2 + half
                        if more:
                            peaks(u + 1)
                        cols = bass.ts(c, chunk)
                        dve.wait_ge(sig("context_kept").sem, sig("context_kept").at(u * 2 + 2))
                        dve.reciprocal(sums[half * 32:half * 32 + HALF, cols], sums[half * 32:half * 32 + HALF, cols])

                    dve.memset(keys[64:P, :, :, :], 1.0).then_inc(sig("stacks_set").sem, 1)
                    peaks(0)
                    units(dve, unit)
                    sig("dve_step").advance(2 * chunks * steps)

                @block.gpsimd
                def _(pool):
                    pool.memset(spread[0:tile, :, :], 0.0).then_inc(sig("pool_step").sem, 1)
                    pool.wait_ge(sig("pool_step").sem, sig("pool_step").at(1))
                    ones = spread[0:tile, :, HALF * HD:HALF * HD + HALF * (VCOLS + 1)].rearrange("p t (h w) -> p t h w", w=VCOLS + 1)[:, :, :, 0]
                    pool.memset(ones, 1.0).then_inc(sig("pool_step").sem, 1)
                    pool.wait_ge(sig("pool_step").sem, sig("pool_step").at(2))

                    def unit(c, half, more):
                        u = c * 2 + half
                        pool.wait_ge(sig("context_sums").sem, sig("context_sums").at(u * HALF - HALF))
                        to = spread[0:tile, half * per:(half + 1) * per, 0:HALF * (VCOLS + HD)].rearrange("p t (h w) -> p t h w", w=VCOLS + HD)[:, :, :, 0:HD]
                        of = values[0:tile, bass.ts(c, per), half * HALF * HD:(half + 1) * HALF * HD].rearrange("p t (h w) -> p t h w", w=HD)
                        pool.tensor_copy(to, of).then_inc(sig("values_spread").sem, 1)

                    units(pool, unit)

                @block.sync
                def _(sp):
                    def stack(c, slot):
                        u = c * 2 + slot
                        sp.wait_ge(sig("scores").sem, sig("scores").at(u * SCORES - SCORES))
                        for of, to, pick in ((0, queries, lambda i, j: i), (1, keys, lambda i, j: j)):
                            for i in range(PARTS):
                                for j in range(PARTS):
                                    row = (i * PARTS + j) * HD
                                    src = parts_dram[of, pick(i, j), slot * 64:slot * 64 + 64, bass.ts(c, chunk)].rearrange("(h d) t -> d h t", d=HD)
                                    sp.dma_start(to[row:row + HD, slot, :, :], src).then_inc(sig(f"stack_in_{slot}").sem, 16)

                    def peak_rows_in(u, slot):
                        sp.wait_ge(sig("peak_rows").sem, sig("peak_rows").at(u + 1))
                        sp.dma_start(peaks_dram[slot, :, :], peak_rows[:, :]).then_inc(sig("peaks_out").sem, 16)
                        sp.wait_ge(sig("peaks_out").sem, sig("peaks_out").at(u + 1))
                        sp.dma_start(queries[STACK:STACK + PARTS, slot, :, :], peaks_dram[slot, :, :].rearrange("(n h) t -> n h t", h=HALF)).then_inc(sig("peaks_in").sem, 16)

                    def unit(c, half, more):
                        if more:
                            stack(c + half, 1 - half)
                            peak_rows_in(c * 2 + half + 1, 1 - half)

                    sp.wait_ge(sig("stacks_set").sem, sig("stacks_set").at(1))
                    stack(0, 0)
                    peak_rows_in(0, 0)
                    units(sp, unit)
            n = 2 * chunks
            for name, total in (("peak_found", n * BLOCKS), ("peak_scores", n * BLOCKS), ("peaks_split", n), ("peaks_turned", n), ("peak_rows", n),
                                ("peaks_out", n), ("peaks_in", n), ("scores", n * SCORES), ("probs", n * SCORES), ("context_sums", n * HALF),
                                ("context_kept", 2 * n), ("values_spread", n), ("stacks_set", 1), ("pool_step", 2),
                                ("stack_in_0", chunks * DMAS), ("stack_in_1", chunks * DMAS)):
                sig(name).advance(total)

        with ExitStack() as st2:
            per_row = k.ps("per_row", [P, chunks, 512], stack=st2)
            with nc.Block() as block:

                @block.tensor
                def _(pe):
                    for c in range(chunks):
                        pe.matmul(per_row[:, c, 0:chunk], k.head_rows[:, :], sums[:, c * chunk:(c + 1) * chunk],
                                  start=True, stop=True).then_inc(sig("sums_spread").sem, 1)

                @block.vector
                def _(dve):
                    for c in range(chunks):
                        cols = slice(c * chunk, (c + 1) * chunk)
                        dve.wait_ge(sig("sums_spread").sem, sig("sums_spread").at(c + 1))
                        last = dve.tensor_tensor(ctx[:, cols], ctx[:, cols], per_row[:, c, 0:chunk], ALU.mult)
                        if residual:
                            last.then_inc(sig("normed").sem, 1)
                    if residual:
                        for c in range(chunks):
                            cols = slice(c * chunk, (c + 1) * chunk)
                            dve.wait_ge(sig("normed").sem, sig("normed").at(c + 1))
                            dve.tensor_tensor(k.X[:, cols], k.X[:, cols], ctx[:, cols], ALU.add)
                        sig("normed").advance(chunks)
            sig("sums_spread").advance(chunks)


def sampled(k, x, parts):
    with k.nc.Block() as block:

        @block.gpsimd
        def _(pool):
            for l, part in parts.items():
                whole = x.rearrange("p (n s) -> p n s", s=2 ** l)
                pool.tensor_copy(part, whole[:, :, 0])


def combine_levels(k, contexts, out_w, up_w, out_b, up_b):
    nc = k.nc
    sig = k.count_of
    with ExitStack() as st:
        ps = k.ps("level_ps", [P, 4, 512], stack=st)
        level = [k.sb(f"level{l}", [P, NT >> l], stack=st) for l in range(LEVELS)]
        quarter = k.sb("quarter", [P, NT // 2], stack=st)
        fine = [k.sb(f"fine{l}", [P, NT >> l], stack=st) for l in range(LEVELS - 1)]
        both = k.sb("both_b", [P, LEVELS], stack=st)
        work = []
        for l in range(LEVELS - 1, -1, -1):
            n = NT >> l
            work += [(l, at, min(CH, n - at)) for at in range(0, n, CH)]
        done = {l: sum(1 for w in work if w[0] >= l) for l in range(LEVELS)}
        with nc.Block() as block:

            @block.tensor
            def _(pe):
                for n, (l, at, size) in enumerate(work):
                    pe.wait_ge(sig("level_kept").sem, sig("level_kept").at(n - 3))
                    coarser = l < LEVELS - 1
                    last = pe.matmul(ps[:, n % 4, 0:size], out_w(l), contexts[l][:, at:at + size], start=True, stop=not coarser)
                    if coarser:
                        pe.wait_ge(sig("upsampled").sem, sig("upsampled").at(LEVELS - 1 - l))
                        last = pe.matmul(ps[:, n % 4, 0:size], up_w(l), fine[l][:, at:at + size], start=False, stop=True)
                    last.then_inc(sig("level_product").sem, 1)

            @block.scalar
            def _(act):
                act.wait_ge(sig("normed").sem, sig("normed").at(1))
                for n, (l, at, size) in enumerate(work):
                    act.wait_ge(sig("level_product").sem, sig("level_product").at(n + 1))
                    act.activation(level[l][:, at:at + size], ps[:, n % 4, 0:size], ACT.Identity, bias=both[:, l:l + 1]).then_inc(sig("level_kept").sem, 1)

            @block.vector
            def _(dve):
                chain = Chain(dve, sig("dve_step"))
                chain.link(dve.tensor_copy(both[:, :], out_b))
                dve.tensor_tensor(both[:, 0:LEVELS - 1], both[:, 0:LEVELS - 1], up_b, ALU.add).then_inc(sig("normed").sem, 1)
                for l in range(LEVELS - 2, -1, -1):
                    n = S >> (l + 1)
                    c = level[l + 1][:, :].rearrange("p (b n) -> p b n", n=n)
                    q = quarter[:, 0:B * n].rearrange("p (b n) -> p b n", n=n)
                    u = fine[l][:, :].rearrange("p (b n two) -> p b n two", n=n, two=2)
                    dve.wait_ge(sig("level_kept").sem, sig("level_kept").at(done[l + 1]))
                    chain.link(dve.tensor_scalar(q, c, 0.25, None, ALU.mult))
                    dve.scalar_tensor_tensor(out=u[:, :, 0:n - 1, 1], in0=c[:, :, 0:n - 1], scalar=0.75, in1=q[:, :, 1:n], op0=ALU.mult, op1=ALU.add)
                    dve.scalar_tensor_tensor(out=u[:, :, 1:n, 0], in0=c[:, :, 1:n], scalar=0.75, in1=q[:, :, 0:n - 1], op0=ALU.mult, op1=ALU.add)
                    dve.tensor_copy(u[:, :, 0, 0], c[:, :, 0])
                    dve.tensor_copy(u[:, :, n - 1, 1], c[:, :, n - 1]).then_inc(sig("upsampled").sem, 1)
                    if l > 0:
                        dve.wait_ge(sig("upsampled").sem, sig("upsampled").at(LEVELS - 1 - l))
                for c in range(NC):
                    cols = slice(c * CH, (c + 1) * CH)
                    dve.wait_ge(sig("level_kept").sem, sig("level_kept").at(done[1] + c + 1))
                    dve.tensor_tensor(k.X[:, cols], k.X[:, cols], level[0][:, cols], ALU.add)
                sig("dve_step").advance(chain.n)
        for name, n in (("level_kept", len(work)), ("level_product", len(work)), ("upsampled", LEVELS - 1), ("normed", 1)):
            sig(name).advance(n)


K_CLAMP = 60.0


def mixed(dve, sig, out, x, coef, b):
    n = sig("mix_step")

    def landed(step):
        dve.wait_ge(n.sem, n.at(b * 2 + step))

    dve.tensor_scalar(out[:, bass.ts(b, S)], x[:, bass.ts(b, S)], coef[:, 0:1], None, ALU.mult).then_inc(n.sem, 1)
    landed(1)
    dve.scalar_tensor_tensor(out=out[:, bass.ds(b * S + 1, S - 1)], in0=x[:, bass.ds(b * S, S - 1)], scalar=coef[:, 1:2], in1=out[:, bass.ds(b * S + 1, S - 1)],
                             op0=ALU.mult, op1=ALU.add).then_inc(n.sem, 1)
    landed(2)
    dve.scalar_tensor_tensor(out=out[:, bass.ds(b * S, S - 1)], in0=x[:, bass.ds(b * S + 1, S - 1)], scalar=coef[:, 2:3], in1=out[:, bass.ds(b * S, S - 1)],
                             op0=ALU.mult, op1=ALU.add).then_inc(sig("mixed").sem, 1)


def mix_coefficients(chain, dve, coef, time_mix, combined_mix, first_half, second_half):
    chain.link(dve.tensor_copy(coef[:, 0:1], time_mix))
    chain.link(dve.tensor_scalar(coef[:, 1:2], time_mix, -1.0, 1.0, ALU.mult, ALU.add))
    chain.link(dve.scalar_tensor_tensor(out=coef[:, 1:2], in0=combined_mix, scalar=first_half, in1=coef[:, 1:2], op0=ALU.mult, op1=ALU.add))
    chain.link(dve.tensor_scalar(coef[:, 2:3], combined_mix, second_half, None, ALU.mult))


def time_mix(k, x, out, mats, vec):
    nc = k.nc
    sig = k.count_of
    with ExitStack() as st:
        k_ps, v_ps, r_ps, o_ps = (k.ps(f"{n}_ps", [P, 2, S], stack=st) for n in "kvro")
        coef = k.sb("coef", [P, 3], stack=st)
        rates = k.sb("rates", [P, 3], stack=st)
        decay = k.sb("decay", [P, S], stack=st)
        xm = k.sb("xm", [P, NT], stack=st)
        key = k.sb("key", [P, NT], stack=st)
        kv = k.sb("kv", [P, NT], stack=st)
        val = k.sb("val", [P, NT], stack=st)
        gate = k.sb("gate", [P, NT], stack=st)
        a = k.sb("a", [P, B, S + 1], stack=st)
        d = k.sb("d", [P, B, S + 1], stack=st)
        with nc.Block() as block:

            @block.tensor
            def _(pe):
                for b in range(B):
                    cols = slice(b * S, (b + 1) * S)
                    pe.wait_ge(sig("mixed").sem, sig("mixed").at(b + 1))
                    pe.wait_ge(sig("key_clamped").sem, sig("key_clamped").at(b - 1))
                    pe.matmul(k_ps[:, b % 2, :], mats("Wk"), xm[:, cols], start=True, stop=True).then_inc(sig("projection").sem, 1)
                    pe.wait_ge(sig("values_copied").sem, sig("values_copied").at(b * 2 - 2))
                    pe.matmul(v_ps[:, b % 2, :], mats("Wv"), xm[:, cols], start=True, stop=True).then_inc(sig("projection").sem, 1)
                    pe.matmul(r_ps[:, b % 2, :], mats("Wr"), xm[:, cols], start=True, stop=True).then_inc(sig("projection").sem, 1)
                for b in range(B):
                    pe.wait_ge(sig("gated").sem, sig("gated").at(b + 1))
                    pe.wait_ge(sig("residual").sem, sig("residual").at(b - 1))
                    pe.matmul(o_ps[:, b % 2, :], mats("Wo"), gate[:, b * S:(b + 1) * S], start=True, stop=True).then_inc(sig("mlp_out").sem, 1)

            @block.scalar
            def _(act):
                r = sig("rstd")
                act.activation(rates[:, 0:1], vec("time_decay"), ACT.Exp).then_inc(r.sem, 1)
                act.activation(rates[:, 2:3], vec("time_first"), ACT.Exp).then_inc(r.sem, 1)
                act.wait_ge(r.sem, r.at(1))
                act.activation(rates[:, 1:2], rates[:, 0:1], ACT.Exp, scale=-1.0).then_inc(r.sem, 1)
                for b in range(B):
                    cols = slice(b * S, (b + 1) * S)
                    act.wait_ge(sig("projection").sem, sig("projection").at(b * 3 + 3))
                    act.activation(val[:, cols], v_ps[:, b % 2, :], ACT.Copy).then_inc(sig("values_copied").sem, 1)
                    act.activation(gate[:, cols], r_ps[:, b % 2, :], ACT.Copy).then_inc(sig("values_copied").sem, 1)
                    act.wait_ge(sig("key_clamped").sem, sig("key_clamped").at(b + 1))
                    act.activation(key[:, cols], key[:, cols], ACT.Exp).then_inc(sig("probs").sem, 1)
                for b in range(B):
                    cols = slice(b * S, (b + 1) * S)
                    act.wait_ge(sig("values_copied").sem, sig("values_copied").at(b * 2 + 2))
                    act.activation(gate[:, cols], gate[:, cols], ACT.Sigmoid).then_inc(sig("sigmoids").sem, 1)

            @block.vector
            def _(dve):
                chain = Chain(dve, sig("dve_step"))
                mix_coefficients(chain, dve, coef, vec("att_time_mix"), vec("att_combined_mix"), vec("first_half"), vec("second_half"))
                chain.link(dve.memset(a[:, :, 0:1], 0.0))
                chain.link(dve.memset(d[:, :, 0:1], 0.0))
                chain.link(dve.memset(decay[:, :], 1.0))
                with dve.Fori(0, B) as b:
                    mixed(dve, sig, xm, x, coef, b)
                dve.wait_ge(sig("rstd").sem, sig("rstd").at(3))
                chain.link(dve.tensor_scalar(decay[:, :], decay[:, :], rates[:, 1:2], None, ALU.mult))
                for b in range(B):
                    cols = slice(b * S, (b + 1) * S)
                    dve.wait_ge(sig("projection").sem, sig("projection").at(b * 3 + 1))
                    dve.tensor_scalar(key[:, cols], k_ps[:, b % 2, :], K_CLAMP, None, ALU.min).then_inc(sig("key_clamped").sem, 1)
                for b in range(B):
                    cols = slice(b * S, (b + 1) * S)
                    dve.wait_ge(sig("probs").sem, sig("probs").at(b + 1))
                    dve.tensor_tensor_scan(d[:, b, 1:S + 1], decay[:, :], key[:, cols], 0.0, ALU.mult, ALU.add).then_inc(sig("memories").sem, 1)
                    dve.wait_ge(sig("key_values").sem, sig("key_values").at(b + 1))
                    dve.tensor_tensor_scan(a[:, b, 1:S + 1], decay[:, :], kv[:, cols], 0.0, ALU.mult, ALU.add).then_inc(sig("memories").sem, 1)
                    dve.wait_ge(sig("memories").sem, sig("memories").at(b * 2 + 2))
                    chain.link(dve.scalar_tensor_tensor(out=key[:, cols], in0=key[:, cols], scalar=rates[:, 2:3], in1=d[:, b, 0:S], op0=ALU.mult, op1=ALU.add))
                    dve.reciprocal(key[:, cols], key[:, cols]).then_inc(sig("rotated").sem, 1)
                    chain.link(dve.scalar_tensor_tensor(out=kv[:, cols], in0=kv[:, cols], scalar=rates[:, 2:3], in1=a[:, b, 0:S], op0=ALU.mult, op1=ALU.add))
                    dve.wait_ge(sig("rotated").sem, sig("rotated").at(b + 1))
                    dve.tensor_tensor(kv[:, cols], kv[:, cols], key[:, cols], ALU.mult).then_inc(sig("averaged").sem, 1)
                for b in range(B):
                    cols = slice(b * S, (b + 1) * S)
                    dve.wait_ge(sig("mlp_out").sem, sig("mlp_out").at(b + 1))
                    dve.tensor_tensor(out[:, cols], x[:, cols], o_ps[:, b % 2, :], ALU.add).then_inc(sig("residual").sem, 1)
                sig("dve_step").advance(chain.n)

            @block.gpsimd
            def _(pool):
                for b in range(B):
                    cols = slice(b * S, (b + 1) * S)
                    pool.wait_ge(sig("probs").sem, sig("probs").at(b + 1))
                    pool.wait_ge(sig("values_copied").sem, sig("values_copied").at(b * 2 + 1))
                    pool.tensor_tensor(kv[:, cols], key[:, cols], val[:, cols], ALU.mult).then_inc(sig("key_values").sem, 1)
                for b in range(B):
                    cols = slice(b * S, (b + 1) * S)
                    pool.wait_ge(sig("sigmoids").sem, sig("sigmoids").at(b + 1))
                    pool.wait_ge(sig("averaged").sem, sig("averaged").at(b + 1))
                    pool.tensor_tensor(gate[:, cols], gate[:, cols], kv[:, cols], ALU.mult).then_inc(sig("gated").sem, 1)
        for name, n in (("mixed", B), ("mix_step", 2 * B), ("projection", 3 * B), ("key_clamped", B), ("values_copied", 2 * B), ("probs", B), ("sigmoids", B),
                        ("rstd", 3), ("memories", 2 * B), ("key_values", B), ("rotated", B), ("averaged", B), ("gated", B), ("mlp_out", B), ("residual", B)):
            sig(name).advance(n)


def channel_mix(k, x, mats, vec):
    nc = k.nc
    sig = k.count_of
    G = 4
    with ExitStack() as st:
        h_ps = k.ps("h_ps", [P, 2, S], stack=st)
        r_ps = k.ps("r_ps", [P, 2, S], stack=st)
        o_ps = k.ps("o_ps", [P, 2, S], stack=st)
        coef = k.sb("coef", [P, 3], stack=st)
        xm = k.sb("xm", [P, NT], stack=st)
        relu = k.sb("relu", [P, G, S], stack=st)
        hidden = k.sb("hidden", [P, G, S], stack=st)
        gate = k.sb("gate", [P, NT], stack=st)
        with nc.Block() as block:

            @block.tensor
            def _(pe):
                def down(n):
                    b, g = n // G, n % G
                    pe.wait_ge(sig("silu_up").sem, sig("silu_up").at(n + 1))
                    if g == 0:
                        pe.wait_ge(sig("residual").sem, sig("residual").at(b - 1))
                    last = pe.matmul(o_ps[:, b % 2, :], mats("Fv", g), hidden[:, g, :], start=(g == 0), stop=(g == G - 1))
                    if g == G - 1:
                        last.then_inc(sig("mlp_out").sem, 1)

                for b in range(B):
                    cols = slice(b * S, (b + 1) * S)
                    pe.wait_ge(sig("mixed").sem, sig("mixed").at(b + 1))
                    pe.wait_ge(sig("sigmoids").sem, sig("sigmoids").at(b - 1))
                    pe.matmul(r_ps[:, b % 2, :], mats("Fr"), xm[:, cols], start=True, stop=True).then_inc(sig("angle_product").sem, 1)
                    for g in range(G):
                        n = b * G + g
                        pe.wait_ge(sig("silu_up").sem, sig("silu_up").at(n - 1))
                        pe.matmul(h_ps[:, n % 2, :], mats("Fk", g), xm[:, cols], start=True, stop=True).then_inc(sig("hidden_product").sem, 1)
                        if n >= 2:
                            down(n - 2)
                down(B * G - 2)
                down(B * G - 1)

            @block.scalar
            def _(act):
                for b in range(B):
                    act.wait_ge(sig("angle_product").sem, sig("angle_product").at(b + 1))
                    act.activation(gate[:, b * S:(b + 1) * S], r_ps[:, b % 2, :], ACT.Sigmoid).then_inc(sig("sigmoids").sem, 1)
                    for g in range(G):
                        n = b * G + g
                        act.wait_ge(sig("hidden_product").sem, sig("hidden_product").at(n + 1))
                        act.wait_ge(sig("silu_up").sem, sig("silu_up").at(n - G + 1))
                        act.activation(relu[:, g, :], h_ps[:, n % 2, :], ACT.Relu).then_inc(sig("gelus").sem, 1)

            @block.vector
            def _(dve):
                chain = Chain(dve, sig("dve_step"))
                mix_coefficients(chain, dve, coef, vec("ffn_time_mix"), vec("ffn_combined_mix"), vec("first_half"), vec("second_half"))
                with dve.Fori(0, B) as b:
                    mixed(dve, sig, xm, x, coef, b)
                for b in range(B):
                    cols = slice(b * S, (b + 1) * S)
                    dve.tensor_tensor(k.X[:, cols], k.X[:, cols], x[:, cols], ALU.add).then_inc(sig("normed").sem, 1)
                    for g in range(G):
                        n = b * G + g
                        dve.wait_ge(sig("gelus").sem, sig("gelus").at(n + 1))
                        dve.wait_ge(sig("mlp_out").sem, sig("mlp_out").at(b))
                        dve.tensor_tensor(hidden[:, g, :], relu[:, g, :], h_ps[:, n % 2, :], ALU.mult).then_inc(sig("silu_up").sem, 1)
                    dve.wait_ge(sig("mlp_out").sem, sig("mlp_out").at(b + 1))
                    chain.link(dve.tensor_tensor(gate[:, cols], gate[:, cols], o_ps[:, b % 2, :], ALU.mult))
                    dve.wait_ge(sig("normed").sem, sig("normed").at(b + 1))
                    dve.tensor_tensor(k.X[:, cols], k.X[:, cols], gate[:, cols], ALU.add).then_inc(sig("residual").sem, 1)
                sig("dve_step").advance(chain.n)
        for name, n in (("mixed", B), ("mix_step", 2 * B), ("angle_product", B), ("hidden_product", B * G), ("silu_up", B * G), ("gelus", B * G),
                        ("mlp_out", B), ("sigmoids", B), ("normed", B), ("residual", B)):
            sig(name).advance(n)


MATS = ["centring", "ident", "rotation",
        "W_mag", "W_q", *[f"W1.{n}" for n in range(8)], "W2.0", "W2.1",
        "Wq", "Wk", "Wv",
        *[f"in.{l}.{w}" for l in range(LEVELS) for w in range(3)], *[f"out.{l}" for l in range(LEVELS)], *[f"up.{l}" for l in range(LEVELS - 1)],
        "rk", "rv", "rr", "ro", *[f"Fk.{g}" for g in range(4)], *[f"Fv.{g}" for g in range(4)], "Fr"]
VECS = ["phases", "b_mag", "b_q", "b1.0", "b1.1", "b2", *[f"ln_g.{f}" for f in range(4)], *[f"ln_b.{f}" for f in range(4)],
        "bq", "bk", "bv", *[f"in_b.{l}.{w}" for l in range(LEVELS) for w in range(3)], *[f"out_b.{l}" for l in range(LEVELS)],
        *[f"up_b.{l}" for l in range(LEVELS - 1)], "ln1_g", "ln1_b", "ln2_g", "ln2_b", "att_time_mix", "att_combined_mix",
        "time_decay", "time_first", "ffn_time_mix", "ffn_combined_mix", "first_half", "second_half"]


def build(nc, args):
    with ExitStack() as stack:
        k = Kernel(nc, args, stack)
        open_signals(k)
        sig = k.count_of
        k.X = k.sb("X", [P, NT])
        xn = k.sb("xn", [P, NT])
        vecs = k.sb("vecs", [P, len(VECS)])
        mats = k.sb("mats", [P, len(MATS), P])
        k.mean_of = k.sb("mean_of", [P, P])
        k.mean_of_4 = k.sb("mean_of_4", [P, P])
        k.ident_bf = k.sb("ident_bf", [P, P], BF16)
        k.head_rows = k.sb("head_rows", [32 + HALF, P])
        k.eps, k.tiny, k.half_pi = (k.sb(n, [P, 1]) for n in ("eps", "tiny", "half_pi"))
        gates = k.sb("gates", [P, EXPERTS0 + EXPERTS1])

        def mat(name):
            return mats[:, MATS.index(name), :]

        def vec(name):
            at = VECS.index(name)
            return vecs[:, at:at + 1]

        k.centring, k.ident = mat("centring"), mat("ident")
        with nc.Block() as block:

            @block.sync
            def _(sp):
                loads = [(k.X[:, :], args["x"]), (vecs[:, :], args["vecs"]), (mats[:, :, :], args["mats"]), (k.head_rows[:, :], args["head_rows"]),
                         (gates[:, :], args["gates"]), (k.ident_bf[:, :], args["ident_bf"].bitcast(BF16))]
                for to, of in loads:
                    sp.dma_start(to, of).then_inc(sig("inputs_in").sem, 16)
                sp.wait_ge(sig("inputs_in").sem, sig("inputs_in").at(len(loads)))
                sig("inputs_in").advance(len(loads))

            @block.vector
            def _(dve):
                for to, value in ((k.mean_of, 1 / P), (k.mean_of_4, 1 / (4 * P)), (k.eps, EPS), (k.tiny, 1e-8), (k.half_pi, float(np.pi / 2))):
                    dve.memset(to[:, :], value)

        def layer_weights(st, tiles):
            hi = k.sb("w_hi", [P, tiles * 3 * P], F32R, stack=st)
            lo = k.sb("w_lo", [P, tiles * 3 * P], F32R, stack=st)
            rows = k.sb("rows", [P, tiles, P], BF16, stack=st)
            return hi, lo, rows

        def mlp(w, tiles, experts, top, gate, load, softmax):
            hi, lo, rows = w
            with ExitStack() as st:
                x_hi = k.sb("x_hi", [P, NT], F32R, stack=st)
                x_lo = k.sb("x_lo", [P, NT], F32R, stack=st)
                k.route_rows = k.sb("route_rows", [P, NT], BF16, stack=st)
                if load:
                    with ExitStack() as st2:
                        k.raw_weights = k.sb("raw_weights", [P, RAW, 2 * 3 * P], stack=st2)
                        also, done = expert_loader(k, args[load], tiles, hi, lo)

                        def loads(sp):
                            sp.dma_start(rows[:, :, :], args[load + "_rows"].bitcast(BF16)).then_inc(sig("consts_in").sem, 16)
                            also["sync"](sp)
                            sp.wait_ge(sig("consts_in").sem, sig("consts_in").at(1))

                        layernorm(k, k.X, xn, parts=(x_hi, x_lo), also={**also, "sync": loads})
                        done()
                        sig("consts_in").advance(1)
                else:
                    layernorm(k, k.X, xn, parts=(x_hi, x_lo))
                routed_mlp(k, xn, x_hi, x_lo, hi, lo, tiles, experts, top, gate, rows, softmax)

        layernorm(k, k.X, xn)
        with ExitStack() as st:
            positions = k.sb("positions", [P, S], stack=st)
            load_table(k, positions[:, :], args["positions"])
            phase_memory(k, xn, lambda n, i=None: mat(n if i is None else f"{n}.{i}"), lambda n, i=None: vec(n if i is None else f"{n}.{i}"), positions[:, :])
        with ExitStack() as st:
            w = layer_weights(st, TILES0)
            gate = gates[:, 0:EXPERTS0]
            mlp(w, TILES0, EXPERTS0, TOP0, gate, "mlp0", False)
            layernorm(k, k.X, xn)
            with ExitStack() as st2:
                table = k.sb("rope", [P, 2, S], stack=st2)
                ctx = k.sb("ctx", [P, NT], stack=st2)
                load_table(k, table[:, :, :], args["rope"])
                attention(k, xn, ctx, S, B, S, lambda i: mat(("Wq", "Wk", "Wv")[i]), lambda i: vec(("bq", "bk", "bv")[i]),
                          rope=(mat("rotation"), table[:, 0, :], table[:, 1, :]), residual=True)
            mlp(w, TILES0, EXPERTS0, TOP0, gate, None, False)
        layernorm(k, k.X, xn)
        with ExitStack() as st:
            contexts = [k.sb(f"context{l}", [P, NT >> l], stack=st) for l in range(LEVELS)]
            with ExitStack() as st2:
                coarse = {l: k.sb(f"coarse{l}", [P, NT >> l], stack=st2) for l in range(1, LEVELS)}
                sampled(k, xn[:, :], {l: c[:, :] for l, c in coarse.items()})
                for l in range(LEVELS):
                    seq = S >> l
                    chunk = min(CH, B * seq)
                    attention(k, coarse[l] if l else xn, contexts[l], seq, B * seq // chunk, chunk,
                              lambda i, l=l: mat(f"in.{l}.{i}"), lambda i, l=l: vec(f"in_b.{l}.{i}"))
            at = VECS.index("out_b.0")
            combine_levels(k, contexts, lambda l: mat(f"out.{l}"), lambda l: mat(f"up.{l}"), vecs[:, at:at + LEVELS], vecs[:, at + LEVELS:at + 2 * LEVELS - 1])
        with ExitStack() as st:
            w = layer_weights(st, TILES1)
            gate = gates[:, EXPERTS0:]
            mlp(w, TILES1, EXPERTS1, TOP1, gate, "mlp1", True)
            layernorm(k, k.X, xn)
            with ExitStack() as st2:
                x1 = k.sb("x1", [P, NT], stack=st2)
                layernorm(k, xn, x1, gain=vec("ln1_g"), shift=vec("ln1_b"))
                names = {"Wk": "rk", "Wv": "rv", "Wr": "rr", "Wo": "ro"}
                time_mix(k, x1, xn, lambda n: mat(names[n]), vec)
                layernorm(k, xn, x1, gain=vec("ln2_g"), shift=vec("ln2_b"))
                channel_mix(k, x1, lambda n, i=None: mat(n if i is None else f"{n}.{i}"), vec)
            mlp(w, TILES1, EXPERTS1, TOP1, gate, None, True)

        with nc.Block() as block:

            @block.sync
            def _(sp):
                sp.dma_start(args["out"], k.X[:, :]).then_inc(sig("out_stored").sem, 16)
                sp.wait_ge(sig("out_stored").sem, sig("out_stored").at(1))


def load_table(k, to, of):
    with k.nc.Block() as block:

        @block.sync
        def _(sp):
            s = k.count_of("consts_in")
            sp.dma_start(to, of).then_inc(s.sem, 16)
            sp.wait_ge(s.sem, s.at(1))
            s.advance(1)


BF16_ONE = np.uint16(0x3F80)


def shape_constants():
    rotation = np.zeros((P, P), np.float32)
    for i in range(0, P, 2):
        rotation[i + 1, i] = -1.0
        rotation[i, i + 1] = 1.0
    inv = np.power(np.float32(10000.0), -2.0 * np.arange(HD // 2, dtype=np.float32) / HD).astype(np.float32)
    ang = np.arange(S, dtype=np.float32)[:, None] * inv[None, :]
    table = [np.tile(np.repeat(f(ang), 2, axis=-1).T, (HEADS, 1)) for f in (np.cos, np.sin)]
    head_rows = np.zeros((32 + HALF, P), np.float32)
    for h in range(HEADS):
        head_rows[32 * (h // HALF) + h % HALF, h * HD:(h + 1) * HD] = 1.0

    def rows(tiles, hidden, experts):
        out = np.zeros((P, tiles * P), np.uint16)
        for m in range(tiles * P):
            e = m // hidden
            out[[e, 32 + e, 64 + e] if e < experts else [96], m] = BF16_ONE
        return out.reshape(P, tiles, P)

    return {
        "centring": np.eye(P, dtype=np.float32) - np.float32(1 / P), "ident": np.eye(P, dtype=np.float32), "rotation": rotation,
        "first_half": (np.arange(P) < P // 2).astype(np.float32), "second_half": (np.arange(P) >= P // 2).astype(np.float32),
        "positions": np.tile(np.arange(S, dtype=np.float32), (P, 1)), "rope": np.stack(table, axis=1).astype(np.float32),
        "head_rows": head_rows, "ident_bf": np.eye(P, dtype=np.uint16) * BF16_ONE,
        "mlp0_rows": rows(TILES0, HIDDEN0, EXPERTS0), "mlp1_rows": rows(TILES1, HIDDEN1, EXPERTS1),
    }


def laid_out(inputs):
    d = {n: np.asarray(a) for n, a in inputs.items()}
    const = shape_constants()
    a, b = "L0_attn_a_", "L0_attn_b_"
    m, v = {n: const[n] for n in ("centring", "ident", "rotation")}, {n: const[n] for n in ("first_half", "second_half")}
    m["W_mag"], m["W_q"] = d[a + "W_mag"].T, d[a + "W_q"].T
    for f in range(4):
        for g in range(2):
            m[f"W1.{f * 2 + g}"] = d[a + "W1"][g * P:(g + 1) * P, f * P:(f + 1) * P].T
    for g in range(2):
        m[f"W2.{g}"] = d[a + "W2"][:, g * P:(g + 1) * P].T
        v[f"b1.{g}"] = d[a + "b1"][g * P:(g + 1) * P]
    v["phases"], v["b_mag"], v["b_q"], v["b2"] = d[a + "random_phases"], d[a + "b_mag"], d[a + "b_q"], d[a + "b2"]
    for f in range(4):
        v[f"ln_g.{f}"], v[f"ln_b.{f}"] = d[a + "ln_g"][f * P:(f + 1) * P], d[a + "ln_b"][f * P:(f + 1) * P]
    for w in "qkv":
        m["W" + w], v["b" + w] = d[b + "W" + w], d[b + "b" + w]
    c = "L1_attn_a_"
    for l in range(LEVELS):
        for w in range(3):
            m[f"in.{l}.{w}"] = d[c + "in_proj_w"][l, w * P:(w + 1) * P].T
            v[f"in_b.{l}.{w}"] = d[c + "in_proj_b"][l, w * P:(w + 1) * P]
        m[f"out.{l}"], v[f"out_b.{l}"] = d[c + "out_w"][l].T, d[c + "out_b"][l]
        if l < LEVELS - 1:
            m[f"up.{l}"], v[f"up_b.{l}"] = d[c + "up_w"][l].T, d[c + "up_b"][l]
    r = "L1_attn_b_"
    for n, w in (("rk", "Wk"), ("rv", "Wv"), ("rr", "Wr"), ("ro", "Wo"), ("Fr", "Fr")):
        m[n] = d[r + w].T
    for g in range(4):
        m[f"Fk.{g}"], m[f"Fv.{g}"] = d[r + "Fk"][g * P:(g + 1) * P].T, d[r + "Fv"][:, g * P:(g + 1) * P].T
    for n in ("ln1_g", "ln1_b", "ln2_g", "ln2_b", "att_time_mix", "att_combined_mix", "time_decay", "time_first", "ffn_time_mix", "ffn_combined_mix"):
        v[n] = d[r + n].reshape(P)

    def mlp(gate, up, down):
        n = gate.shape[1] // P
        parts = gate.reshape(P, n, P), up.reshape(P, n, P), down.reshape(n, P, P).transpose(1, 0, 2)
        return np.stack(parts, axis=2).reshape(P, n * 3 * P)

    f0, f1 = "L0_ffn_", "L1_ffn_"
    mlp0 = mlp(np.concatenate([d[f0 + "exp_wg"].transpose(1, 0, 2).reshape(P, -1), d[f0 + "shared_wg"]], 1),
               np.concatenate([d[f0 + "exp_wu"].transpose(1, 0, 2).reshape(P, -1), d[f0 + "shared_wu"]], 1),
               np.concatenate([d[f0 + "exp_wd"].reshape(-1, P), d[f0 + "shared_wd"]], 0))
    mlp1 = mlp(d[f1 + "w1"].reshape(-1, P).T, d[f1 + "w3"].reshape(-1, P).T, d[f1 + "w2"].transpose(0, 2, 1).reshape(-1, P))
    arrays = {"x": d[a + "x"].reshape(NT, P).T, "vecs": np.stack([v[n] for n in VECS], axis=1), "mats": np.stack([m[n] for n in MATS], axis=1),
              "gates": np.concatenate([d[f0 + "gate_w"].T, d[f1 + "gate_w"].T], axis=1), "mlp0": mlp0, "mlp1": mlp1,
              **{n: const[n] for n in ("positions", "rope", "head_rows", "ident_bf", "mlp0_rows", "mlp1_rows")}}
    return {n: np.ascontiguousarray(x) for n, x in arrays.items()}


def kernel(**inputs):
    import concourse.bacc as bacc
    from concourse.bass_utils import run_bass_kernel_spmd

    nc = bacc.Bacc("TRN2", target_bir_lowering=False, num_devices=1)
    arrays = {f"in_{n}": x for n, x in laid_out(inputs).items()}
    args = {n[3:]: nc.dram_tensor(n, x.shape, mybir.dt.from_np(x.dtype), kind="ExternalInput").ap() for n, x in arrays.items()}
    args["out"] = nc.dram_tensor("out_x", (P, NT), F32, kind="ExternalOutput").ap()
    build(nc, args)
    result = run_bass_kernel_spmd(nc, [arrays], core_ids=[0]).results[0]["out_x"]
    return np.ascontiguousarray(result.T).reshape(B, S, P)
```

```python
from contextlib import ExitStack

import numpy as np

import concourse.bass as bass
from concourse import mybir

F32 = mybir.dt.float32
F32R = mybir.dt.float32r
BF16 = mybir.dt.bfloat16
ACT = mybir.ActivationFunctionType
ALU = mybir.AluOpType
AX = mybir.AxisListType

P = 128
B = 4
S = 512
NT = B * S
CH = 512
NC = NT // CH
TILES = NT // P
HEADS = 16
HD = P // HEADS
EPS = 1e-5
HIDDEN0, EXPERTS0, TOP0, SHARED0 = 128, 16, 4, 256
HIDDEN1, EXPERTS1, TOP1 = 352, 8, 2
TILES0 = (HIDDEN0 * EXPERTS0 + SHARED0) // P
TILES1 = HIDDEN1 * EXPERTS1 // P
SCALE0 = 2.5
CREDIT = 32
LEVELS = 4


class Signal:

    def __init__(self, sem, step=1):
        self.sem, self.step, self.base = sem, step, CREDIT * step

    def at(self, n):
        return n * self.step + self.base

    def advance(self, n):
        self.base += n * self.step


class Chain:

    def __init__(self, eng, signal, it=0, per=0):
        self.eng, self.own, self.first, self.n = eng, signal, it * per, 0

    def link(self, ins):
        self.n += 1
        ins.then_inc(self.own.sem, 1)
        self.eng.wait_ge(self.own.sem, self.own.at(self.first + self.n))


class Kernel:

    def __init__(self, nc, args, stack):
        self.nc, self.args, self.stack = nc, args, stack
        self.counts = {}
        self.names = 0

    def sb(self, name, shape, dt=F32, stack=None):
        self.names += 1
        return (stack or self.stack).enter_context(self.nc.sbuf_tensor(f"{name}_{self.names}", shape, dt))

    def ps(self, name, shape, dt=F32, stack=None):
        self.names += 1
        return (stack or self.stack).enter_context(self.nc.psum_tensor(f"{name}_{self.names}", shape, dt))

    def scratch(self, name, shape):
        self.names += 1
        return self.nc.dram_tensor(f"{name}_{self.names}", shape, BF16).ap()

    def count_of(self, name):
        return self.counts[name]


SIGNALS = {
    "tensor": ["centred", "variance", "weights_turned", "gate_up", "routed_rows", "mlp_out", "magnitude_product", "angle_product", "context_mean", "hidden_product", "projection", "rotation", "values_turned", "peak_scores", "peaks_turned", "scores", "context_sums", "sums_spread", "level_product"],
    "scalar": ["squared", "weights_high", "logs", "rstd", "x_high", "gate_probs", "gate_exp", "silu", "h_hi", "sines", "sigmoids", "gelus", "projected", "values_copied", "peak_rows", "probs", "context_low", "sums_kept", "level_kept"],
    "vector": ["dve_step", "weights_low_odd", "normed", "routed", "weighted", "residual", "silu_up", "angles", "angle_reduced", "magnitudes", "magnitude_sum", "memories", "context_centred", "context_normed", "rotated", "values_kept", "parts_made", "peak_found", "peaks_split", "stacks_set", "upsampled", "mix_step", "mixed", "key_clamped", "averaged", "probs_low", "context_kept"],
    "gpsimd": ["pool_step", "weights_rounded", "weights_low_even", "h_lo", "probs_low_pool", "weighted_waves", "values_spread", "key_values", "gated"],
    "dma": ["inputs_in", "weights_in_0", "weights_in_1", "weights_in_2", "weights_in_3", "consts_in", "mats_in", "out_stored", "parts_stored", "stack_in_0", "stack_in_1", "stack_in_2", "stack_in_3", "peaks_out", "peaks_in"],
}


def open_signals(k):
    for owner, names in SIGNALS.items():
        for name in names:
            k.counts[name] = Signal(k.stack.enter_context(k.nc.semaphore(name)), 16 if owner == "dma" else 1)
    with k.nc.Block() as block:
        def opened(owner):
            def program(eng):
                for name in SIGNALS[owner]:
                    eng.sem_inc(k.counts[name].sem, k.counts[name].base)
            return program

        block.tensor(opened("tensor"))
        block.scalar(opened("scalar"))
        block.vector(opened("vector"))
        block.gpsimd(opened("gpsimd"))
        block.sync(opened("dma"))


def layernorm(k, src, dst, gain=None, shift=None, also=None, routing=None):
    nc = k.nc
    centred, variance, squared, logs, rstd = (k.count_of(n) for n in ("centred", "variance", "squared", "logs", "rstd"))
    normed, step = k.count_of("normed"), k.count_of("dve_step")
    with ExitStack() as st:
        xc = k.ps("xc", [P, NC, CH], stack=st)
        var = k.ps("var", [P, NC - 1, CH], stack=st)
        sq = k.sb("sq", [P, NC, CH], stack=st)
        rs = k.sb("rs", [P, NC, CH], stack=st)
        with nc.Block() as block:

            @block.tensor
            def _(pe):
                for c in range(NC):
                    pe.matmul(xc[:, c, :], k.centring, src[:, c * CH:(c + 1) * CH], start=True, stop=True).then_inc(centred.sem, 1)
                for c in range(NC):
                    pe.wait_ge(squared.sem, squared.at(c + 1))
                    if c == NC - 1:
                        pe.wait_ge(logs.sem, logs.at(1))
                    pe.matmul(var[:, c % (NC - 1), :], k.mean_of[:, :], sq[:, c, :], start=True, stop=True).then_inc(variance.sem, 1)
                for t in range(TILES if routing else 0):
                    pe.wait_ge(normed.sem, normed.at(t * P // CH + 1))
                    pe.matmul(routing[0][:, t, :], dst[:, t * P:(t + 1) * P], routing[1], start=(t == 0), stop=True, skip_group_check=True)

            @block.scalar
            def _(act):
                for c in range(NC):
                    act.wait_ge(centred.sem, centred.at(c + 1))
                    act.activation(sq[:, c, :], xc[:, c, :], ACT.Square).then_inc(squared.sem, 1)
                for c in range(NC):
                    act.wait_ge(variance.sem, variance.at(c + 1))
                    act.activation(rs[:, c, :], var[:, c % (NC - 1), :], ACT.Ln, bias=k.eps[:, 0:1]).then_inc(logs.sem, 1)
                for c in range(NC):
                    act.wait_ge(logs.sem, logs.at(c + 1))
                    act.activation(rs[:, c, :], rs[:, c, :], ACT.Exp, scale=-0.5).then_inc(rstd.sem, 1)
                if also and "scalar" in also:
                    also["scalar"](act)

            @block.vector
            def _(dve):
                for c in range(NC):
                    cols = slice(c * CH, (c + 1) * CH)
                    dve.wait_ge(rstd.sem, rstd.at(c + 1))
                    dve.tensor_tensor(dst[:, cols], xc[:, c, :], rs[:, c, :], ALU.mult).then_inc(normed.sem, 1)
                for c in range(NC if gain is not None else 0):
                    cols = slice(c * CH, (c + 1) * CH)
                    dve.wait_ge(normed.sem, normed.at(c + 1))
                    dve.tensor_scalar(dst[:, cols], dst[:, cols], gain, shift, ALU.mult, ALU.add).then_inc(step.sem, 1)
                if also and "vector" in also:
                    also["vector"](dve)

            if also and "gpsimd" in also:
                block.gpsimd(also["gpsimd"])
            if also:
                block.sync(also["sync"])
        for s, n in ((centred, NC), (variance, NC), (squared, NC), (logs, NC), (rstd, NC), (normed, NC),
                     (step, NC if gain is not None else 0)):
            s.advance(n)


RAW = 4


def expert_loader(k, weights, tiles, hi, lo, alone=False):
    weights_in = [k.count_of(f"weights_in_{n}") for n in range(RAW)]
    high, own_high = k.count_of("weights_high"), k.count_of("weights_rounded")
    low = k.count_of("weights_low_even"), k.count_of("weights_low_odd")
    raw = k.raw_weights
    width = 2 * 3 * P
    pieces = tiles // 2

    def part(n):
        return slice(n * width, (n + 1) * width)

    def round_high(act):
        for n in range(pieces):
            arrived = weights_in[n % RAW]
            act.wait_ge(arrived.sem, arrived.at(n // RAW + 1))
            act.activation(hi[:, part(n)], raw[:, n % RAW, :], ACT.Copy).then_inc(high.sem, 1)

    def rest_of(which):
        def program(eng):
            for n in range(which, pieces, 2):
                eng.wait_ge(high.sem, high.at(n + 1))
                eng.tensor_tensor(lo[:, part(n)], raw[:, n % RAW, :], hi[:, part(n)].bitcast(F32), ALU.subtract).then_inc(low[which].sem, 1)
        return program

    def both_parts(pool):
        for n in range(pieces):
            arrived = weights_in[n % RAW]
            pool.wait_ge(arrived.sem, arrived.at(n // RAW + 1))
            pool.tensor_copy(hi[:, part(n)], raw[:, n % RAW, :]).then_inc(own_high.sem, 1)
            pool.wait_ge(own_high.sem, own_high.at(n + 1))
            pool.tensor_tensor(lo[:, part(n)], raw[:, n % RAW, :], hi[:, part(n)].bitcast(F32), ALU.subtract).then_inc(low[0].sem, 1)

    def load(sp):
        for n in range(pieces):
            if n >= RAW:
                used, count = (low[0], n - RAW + 1) if alone else (low[n % 2], (n - RAW) // 2 + 1)
                sp.wait_ge(used.sem, used.at(count))
            sp.dma_start(raw[:, n % RAW, :], weights[:, part(n)]).then_inc(weights_in[n % RAW].sem, 16)

    def done():
        for n in range(RAW):
            weights_in[n].advance(len(range(n, pieces, RAW)))
        (own_high if alone else high).advance(pieces)
        low[0].advance(pieces if alone else len(range(0, pieces, 2)))
        low[1].advance(0 if alone else len(range(1, pieces, 2)))

    if alone:
        return {"gpsimd": both_parts, "sync": load}, done
    return {"scalar": round_high, "gpsimd": rest_of(0), "vector": rest_of(1), "sync": load}, done


def routed_mlp(k, x, logits, room, hi, lo, w_hi, w_lo, tiles, experts, top, rows, softmax):
    nc = k.nc
    turned, gate_up = k.count_of("weights_turned"), k.count_of("gate_up")
    rowsig, out_sum = k.count_of("routed_rows"), k.count_of("mlp_out")
    probs_ready, routed, step = k.count_of("gate_probs"), k.count_of("routed"), k.count_of("dve_step")
    x_high = k.count_of("x_high")
    silu, h_hi, h_lo, weighted, silu_up, residual = (k.count_of(n) for n in ("silu", "h_hi", "h_lo", "weighted", "silu_up", "residual"))

    wide = k.route_rows
    with ExitStack() as st:
        rowsT = k.ps("rowsT", [P, TILES, P], BF16, stack=st)
        sc = k.sb("sc", [P, TILES, experts], stack=st)
        rest = k.sb("rest", [P, TILES, experts], stack=st)
        best = k.sb("best", [P, TILES, 8], stack=st)
        peak = k.sb("peak", [P, TILES], stack=st)
        total = k.sb("total", [P, TILES], stack=st)
        wts = k.sb("wts", [P, TILES, experts], stack=st)
        split = k.sb("split", [P, TILES, P], BF16, stack=st)
        with nc.Block() as block:

            @block.tensor
            def _(pe):
                pe.wait_ge(routed.sem, routed.at(1))
                for t in range(TILES):
                    last = pe.transpose(rowsT[:, t, :], split[:, t, :], k.ident_bf[:, :])
                    if t % 8 == 7:
                        last.then_inc(turned.sem, 1)

            @block.scalar
            def _(act):
                if softmax:
                    act.wait_ge(k.count_of("silu_up").sem, k.count_of("silu_up").at(1))
                    act.activation(sc[:, :, :], rest[:, :, :], ACT.Exp).then_inc(probs_ready.sem, 1)
                else:
                    act.activation(sc[:, :, :], logits[:, :, :], ACT.Sigmoid).then_inc(probs_ready.sem, 1)
                for c in range(NC):
                    cols = slice(c * CH, (c + 1) * CH)
                    act.activation(hi[:, cols], x[:, cols], ACT.Copy).then_inc(x_high.sem, 1)
                for n in range(2):
                    act.wait_ge(turned.sem, turned.at(n + 1))
                    act.activation(wide[:, n * 8 * P:(n + 1) * 8 * P].rearrange("p (t n) -> p t n", n=P),
                                   rowsT[:, n * 8:(n + 1) * 8, :], ACT.Copy)

            @block.vector
            def _(dve):
                chain = Chain(dve, step)
                zeros = k.count_of("pool_step")

                def over(a):
                    return a[:, :].unsqueeze(2).to_broadcast([P, TILES, experts])

                if softmax:
                    chain.link(dve.tensor_reduce(peak[:, :], logits[:, :, :], AX.X, ALU.max))
                    dve.tensor_tensor(rest[:, :, :], logits[:, :, :], over(peak), ALU.subtract).then_inc(silu_up.sem, 1)
                    dve.wait_ge(probs_ready.sem, probs_ready.at(1))
                    chain.link(dve.tensor_reduce(total[:, :], sc[:, :, :], AX.X, ALU.add))
                    chain.link(dve.reciprocal(total[:, :], total[:, :]))
                    chain.link(dve.tensor_tensor(sc[:, :, :], sc[:, :, :], over(total), ALU.mult))
                dve.wait_ge(probs_ready.sem, probs_ready.at(1))
                for t in range(TILES):
                    last = dve.max(best[:, t, :], sc[:, t, :])
                chain.link(last)
                chain.link(dve.memset(best[:, :, top:8], -2.0))
                for t in range(TILES):
                    last = dve.match_replace(rest[:, t, :], best[:, t, :], sc[:, t, :], -1.0)
                chain.link(last)
                chain.link(dve.scalar_tensor_tensor(out=wts[:, :, :], in0=rest[:, :, :], scalar=0.0, in1=sc[:, :, :], op0=ALU.max, op1=ALU.subtract))
                chain.link(dve.tensor_reduce(total[:, :], wts[:, :, :], AX.X, ALU.add))
                if softmax:
                    chain.link(dve.reciprocal(total[:, :], total[:, :]))
                    chain.link(dve.tensor_tensor(wts[:, :, :], wts[:, :, :], over(total), ALU.mult))
                else:
                    chain.link(dve.tensor_scalar(total[:, :], total[:, :], -1e-20, None, ALU.add))
                    chain.link(dve.reciprocal(total[:, :], total[:, :]))
                    chain.link(dve.tensor_tensor(wts[:, :, :], wts[:, :, :], over(total), ALU.mult))
                    chain.link(dve.tensor_scalar(wts[:, :, :], wts[:, :, :], SCALE0, None, ALU.mult))
                dve.wait_ge(zeros.sem, zeros.at(2))
                chain.link(dve.tensor_copy(split[:, :, 0:experts], wts[:, :, :]))
                chain.link(dve.tensor_tensor(wts[:, :, :], wts[:, :, :], split[:, :, 0:experts], ALU.subtract))
                chain.link(dve.tensor_copy(split[:, :, 32:32 + experts], wts[:, :, :]))
                dve.tensor_tensor(split[:, :, 64:64 + experts], wts[:, :, :], split[:, :, 32:32 + experts], ALU.subtract).then_inc(routed.sem, 1)
                step.advance(chain.n)
            @block.gpsimd
            def _(pool):
                zeros = k.count_of("pool_step")
                pool.memset(split[:, :, :], 0.0).then_inc(zeros.sem, 1)
                pool.wait_ge(zeros.sem, zeros.at(1))
                pool.memset(split[:, :, 96:97], 1.0).then_inc(zeros.sem, 1)
                for c in range(NC):
                    cols = slice(c * CH, (c + 1) * CH)
                    pool.wait_ge(x_high.sem, x_high.at(c + 1))
                    pool.tensor_tensor(lo[:, cols], x[:, cols], hi[:, cols].bitcast(F32), ALU.subtract)
        k.count_of("pool_step").advance(2)
        for s, n in ((x_high, NC), (turned, 2), (probs_ready, 1), (routed, 1), (silu_up, 1 if softmax else 0)):
            s.advance(n)
    room.close()

    LAG, RING, PAIR = 3, 4, 2
    assert PAIR * tiles % RING == 0 and tiles % 2 == 0 and LAG < RING
    with ExitStack() as st:
        g_ps = k.ps("g_ps", [P, 2, CH], stack=st)
        u_ps = k.ps("u_ps", [P, 2, CH], stack=st)
        r_ps = k.ps("r_ps", [P, 2, CH], stack=st)
        o_ps = k.ps("o_ps", [P, PAIR, CH], stack=st)
        sg = k.sb("sg", [P, RING, CH], stack=st)
        hw = k.sb("hw", [P, RING, CH], stack=st)
        hh = k.sb("hh", [P, RING, CH], F32R, stack=st)
        hl = k.sb("hl", [P, RING, CH], F32R, stack=st)

        def weight(part, j, which):
            at = (j * 3 + which) * P
            return part[:, at:at + P]

        def number(i, half, j):
            m = half * tiles + j
            return i * (PAIR * tiles) + m, m % RING, m % 2

        with nc.Block() as block:

            @block.tensor
            def _(pe):
                def up(i, half, j):
                    n, _, bank = number(i, half, j)
                    cols = bass.ts(i * PAIR + half, CH)
                    pe.wait_ge(weighted.sem, weighted.at(n - 1))
                    for which, banks in ((0, g_ps), (1, u_ps)):
                        at = banks[:, bank, :]
                        pe.matmul(at, weight(w_hi, j, which), hi[:, cols], start=True, stop=False)
                        pe.matmul(at, weight(w_lo, j, which), hi[:, cols], start=False, stop=False)
                        last = pe.matmul(at, weight(w_hi, j, which), lo[:, cols], start=False, stop=True)
                        if which == 0:
                            last.then_inc(gate_up.sem, 1)
                    pe.matmul(r_ps[:, bank, :], rows[:, j, :], wide[:, cols], start=True, stop=True).then_inc(rowsig.sem, 1)

                def down(i, half, j):
                    n, slot, _ = number(i, half, j)
                    at = o_ps[:, half, :]
                    if j == 0:
                        pe.wait_ge(residual.sem, residual.at(i * PAIR + half - 1))
                    pe.wait_ge(h_hi.sem, h_hi.at(n + 1))
                    pe.matmul(at, weight(w_hi, j, 2), hh[:, slot, :], start=(j == 0), stop=False)
                    pe.matmul(at, weight(w_lo, j, 2), hh[:, slot, :], start=False, stop=False)
                    pe.wait_ge(h_lo.sem, h_lo.at(n + 1))
                    last = pe.matmul(at, weight(w_hi, j, 2), hl[:, slot, :], start=False, stop=(j == tiles - 1))
                    if j == tiles - 1:
                        last.then_inc(out_sum.sem, 1)

                def pair(i, more):
                    for half in range(PAIR):
                        for j in range(tiles):
                            down(i, half, j)
                            if j + LAG < tiles:
                                up(i, half, j + LAG)
                            elif half == 0:
                                up(i, 1, j + LAG - tiles)
                            elif more:
                                up(i + 1, 0, j + LAG - tiles)

                for j in range(LAG):
                    up(0, 0, j)
                with pe.Fori(0, NC // PAIR - 1) as i:
                    pair(i, True)
                pair(NC // PAIR - 1, False)

            def tiles_of(i):
                for half in range(PAIR):
                    for j in range(tiles):
                        yield half, j, *number(i, half, j)

            @block.scalar
            def _(act):
                def gates(n, slot, bank):
                    act.wait_ge(gate_up.sem, gate_up.at(n + 1))
                    act.activation(sg[:, slot, :], g_ps[:, bank, :], ACT.Silu).then_inc(silu.sem, 1)

                def high(n, slot):
                    act.wait_ge(weighted.sem, weighted.at(n + 1))
                    act.activation(hh[:, slot, :], hw[:, slot, :], ACT.Copy).then_inc(h_hi.sem, 1)

                def pair(i, more):
                    m = PAIR * tiles
                    for half, j, n, slot, bank in tiles_of(i):
                        if half * tiles + j + 1 < m or more:
                            gates(n + 1, (slot + 1) % RING, 1 - bank)
                        high(n, slot)

                gates(0, 0, 0)
                with act.Fori(0, NC // PAIR - 1) as i:
                    pair(i, True)
                pair(NC // PAIR - 1, False)

            @block.vector
            def _(dve):
                def add(chunk, bank):
                    cols = bass.ts(chunk, CH)
                    dve.wait_ge(out_sum.sem, out_sum.at(chunk + 1))
                    dve.tensor_tensor(k.X[:, cols], k.X[:, cols], o_ps[:, bank, :], ALU.add).then_inc(residual.sem, 1)

                def pair(i, after):
                    for half, j, n, slot, bank in tiles_of(i):
                        dve.wait_ge(silu.sem, silu.at(n + 1))
                        dve.wait_ge(rowsig.sem, rowsig.at(n + 1))
                        dve.tensor_tensor(hw[:, slot, :], sg[:, slot, :], u_ps[:, bank, :], ALU.mult).then_inc(silu_up.sem, 1)
                        dve.wait_ge(silu_up.sem, silu_up.at(n + 1))
                        dve.tensor_tensor(hw[:, slot, :], hw[:, slot, :], r_ps[:, bank, :], ALU.mult).then_inc(weighted.sem, 1)
                        if j == LAG and (half == 1 or after):
                            add(i * PAIR + half - 1, 1 - half)

                pair(0, False)
                with dve.Fori(0, NC // PAIR - 1) as i:
                    pair(i + 1, True)
                add(NC - 1, 1)

            @block.gpsimd
            def _(pool):
                with pool.Fori(0, NC // PAIR) as i:
                    for half, j, n, slot, bank in tiles_of(i):
                        pool.wait_ge(h_hi.sem, h_hi.at(n + 1))
                        pool.tensor_tensor(hl[:, slot, :], hw[:, slot, :], hh[:, slot, :].bitcast(F32), ALU.subtract).then_inc(h_lo.sem, 1)
        for s in (gate_up, rowsig, silu, silu_up, weighted, h_hi, h_lo):
            s.advance(NC * tiles)
        for s in (out_sum, residual):
            s.advance(NC)


TWO_PI = 2 * np.pi
TURN = (6.28125, float(np.float32(0.0019350051879882812)), float(TWO_PI - 6.28125 - 0.0019350051879882812))
ROUND = 1.5 * 2.0 ** 23
ALMOST_PI = 3.1415925


def turn_down(chain, dve, angle, turns):
    chain.link(dve.tensor_scalar(turns, angle, 1 / TWO_PI, ROUND, ALU.mult, ALU.add))
    chain.link(dve.tensor_scalar(turns, turns, ROUND, None, ALU.subtract))
    for part in TURN:
        chain.link(dve.scalar_tensor_tensor(out=angle, in0=turns, scalar=-part, in1=angle, op0=ALU.mult, op1=ALU.add))
    chain.link(dve.tensor_scalar(angle, angle, ALMOST_PI, -ALMOST_PI, ALU.min, ALU.max))


def phase_memory(k, x, mats, vec, positions, also):
    nc = k.nc
    sig = k.count_of
    with ExitStack() as st:
        phi = k.sb("phi", [P, S], stack=st)
        cos = k.sb("cos", [P, S], stack=st)
        sin = k.sb("sin", [P, S], stack=st)
        turns = k.sb("turns", [P, S], stack=st)
        ones = k.sb("ones_row", [P, S], stack=st)
        mem_r = k.sb("mem_r", [P, NT], stack=st)
        mem_i = k.sb("mem_i", [P, NT], stack=st)
        angle = k.sb("angle", [P, NT], stack=st)
        inv = k.sb("inv", [P, NT], stack=st)
        context = k.sb("context", [P, 4, NT], stack=st)

        with ExitStack() as st2:
            mag = k.sb("mag", [P, NT], stack=st2)
            wr = k.sb("wr", [P, NT], stack=st2)
            wi = k.sb("wi", [P, NT], stack=st2)
            wx = k.sb("wx", [P, NT], stack=st2)
            m_ps = k.ps("m_ps", [P, B, S], stack=st2)
            q_ps = k.ps("q_ps", [P, B, S], stack=st2)
            with nc.Block() as block:

                @block.tensor
                def _(pe):
                    with pe.Fori(0, B) as b:
                        cols = bass.ts(b, S)
                        pe.matmul(m_ps[:, b, :], mats("W_mag"), x[:, cols], start=True, stop=True).then_inc(sig("magnitude_product").sem, 1)
                        pe.matmul(q_ps[:, b, :], mats("W_q"), x[:, cols], start=True, stop=True).then_inc(sig("angle_product").sem, 1)

                @block.scalar
                def _(act):
                    act.wait_ge(sig("angle_reduced").sem, sig("angle_reduced").at(1))
                    act.activation(sin[:, :], phi[:, :], ACT.Sin).then_inc(sig("sines").sem, 1)
                    act.activation(cos[:, :], phi[:, :], ACT.Abs).then_inc(sig("sines").sem, 1)
                    act.wait_ge(sig("sines").sem, sig("sines").at(2))
                    act.activation(cos[:, :], cos[:, :], ACT.Sin, scale=-1.0, bias=k.half_pi[:, 0:1]).then_inc(sig("sines").sem, 1)
                    with act.Fori(0, B) as b:
                        act.wait_ge(sig("magnitude_product").sem, sig("magnitude_product").at(b + 1))
                        act.activation(mag[:, bass.ts(b, S)], m_ps[:, b, :], ACT.Sigmoid, bias=vec("b_mag")).then_inc(sig("sigmoids").sem, 1)
                    for b in range(B):
                        cols = bass.ts(b, S)
                        act.wait_ge(sig("magnitude_sum").sem, sig("magnitude_sum").at(b + 1))
                        act.activation(inv[:, cols], inv[:, cols], ACT.Ln, bias=k.tiny[:, 0:1]).then_inc(sig("logs").sem, 1)
                    for b in range(B):
                        cols = bass.ts(b, S)
                        act.wait_ge(sig("logs").sem, sig("logs").at(b + 1))
                        act.activation(inv[:, cols], inv[:, cols], ACT.Exp, scale=-0.5).then_inc(sig("rstd").sem, 1)

                @block.vector
                def _(dve):
                    chain = Chain(dve, sig("dve_step"))
                    chain.link(dve.memset(ones[:, :], 1.0))
                    chain.link(dve.tensor_scalar(phi[:, :], positions, vec("phases"), 0.01, ALU.mult, ALU.mult))
                    with dve.Fori(0, B) as b:
                        dve.wait_ge(sig("angle_product").sem, sig("angle_product").at(b + 1))
                        dve.scalar_tensor_tensor(out=angle[:, bass.ts(b, S)], in0=q_ps[:, b, :], scalar=vec("b_q"), in1=phi[:, :],
                                                 op0=ALU.add, op1=ALU.add).then_inc(sig("angles").sem, 1)
                    dve.wait_ge(sig("angles").sem, sig("angles").at(B))
                    turn_down(chain, dve, phi[:, :], turns[:, :])
                    dve.sem_inc(sig("angle_reduced").sem, 1)
                    sig("dve_step").advance(chain.n)
                    with dve.Fori(0, B) as b:
                        cols = bass.ts(b, S)
                        dve.wait_ge(sig("sigmoids").sem, sig("sigmoids").at(b + 1))
                        dve.tensor_scalar(mag[:, cols], mag[:, cols], 5.0, None, ALU.mult).then_inc(sig("magnitudes").sem, 1)
                        dve.wait_ge(sig("magnitudes").sem, sig("magnitudes").at(b + 1))
                        dve.tensor_tensor_scan(inv[:, cols], ones[:, :], mag[:, cols], 0.0, ALU.mult, ALU.add).then_inc(sig("magnitude_sum").sem, 1)
                        dve.wait_ge(sig("weighted_waves").sem, sig("weighted_waves").at(b * 2 + 1))
                        dve.tensor_tensor_scan(mem_r[:, cols], ones[:, :], wr[:, cols], 0.0, ALU.mult, ALU.add).then_inc(sig("memories").sem, 1)
                        dve.wait_ge(sig("weighted_waves").sem, sig("weighted_waves").at(b * 2 + 2))
                        dve.tensor_tensor_scan(mem_i[:, cols], ones[:, :], wi[:, cols], 0.0, ALU.mult, ALU.add).then_inc(sig("memories").sem, 1)
                    with dve.Fori(0, B) as b:
                        cols = bass.ts(b, S)
                        dve.wait_ge(sig("rstd").sem, sig("rstd").at(b + 1))
                        dve.wait_ge(sig("memories").sem, sig("memories").at(b * 2 + 2))
                        dve.tensor_tensor(mem_r[:, cols], mem_r[:, cols], inv[:, cols], ALU.mult)
                        dve.tensor_tensor(mem_i[:, cols], mem_i[:, cols], inv[:, cols], ALU.mult)

                @block.gpsimd
                def _(pool):
                    pool.wait_ge(sig("sines").sem, sig("sines").at(3))
                    with pool.Fori(0, B) as b:
                        cols = bass.ts(b, S)
                        pool.wait_ge(sig("magnitudes").sem, sig("magnitudes").at(b + 1))
                        pool.tensor_tensor(wx[:, cols], mag[:, cols], x[:, cols], ALU.mult).then_inc(sig("pool_step").sem, 1)
                        pool.wait_ge(sig("pool_step").sem, sig("pool_step").at(b + 1))
                        pool.tensor_tensor(wr[:, cols], wx[:, cols], cos[:, :], ALU.mult).then_inc(sig("weighted_waves").sem, 1)
                        pool.tensor_tensor(wi[:, cols], wx[:, cols], sin[:, :], ALU.mult).then_inc(sig("weighted_waves").sem, 1)
            for name, n in (("magnitude_product", B), ("angle_product", B), ("angle_reduced", 1), ("sines", 3), ("sigmoids", B), ("logs", B), ("rstd", B),
                            ("angles", B), ("magnitudes", B), ("magnitude_sum", B), ("memories", 2 * B), ("pool_step", B), ("weighted_waves", 2 * B)):
                sig(name).advance(n)

        with ExitStack() as st2:
            sq = k.sb("sq", [P, NT], stack=st2)
            cq = k.sb("cq", [P, NT], stack=st2)
            a = k.sb("a", [P, S], stack=st2)
            steps = 6
            with nc.Block() as block:

                @block.vector
                def _(dve):
                    with dve.Fori(0, B) as b:
                        chain = Chain(dve, sig("dve_step"), b, steps)
                        turn_down(chain, dve, angle[:, bass.ts(b, S)], turns[:, :])
                        assert chain.n == steps
                        dve.sem_inc(sig("angle_reduced").sem, 1)
                    sig("dve_step").advance(B * steps)
                    steps2 = 6
                    with dve.Fori(0, B) as b:
                        cols = bass.ts(b, S)
                        chain = Chain(dve, sig("dve_step"), b, steps2)
                        dve.wait_ge(sig("sines").sem, sig("sines").at(b * 3 + 3))
                        chain.link(dve.tensor_tensor(a[:, :], mem_i[:, cols], sq[:, cols], ALU.mult))
                        chain.link(dve.tensor_tensor(context[:, 2, cols], mem_r[:, cols], cq[:, cols], ALU.mult))
                        chain.link(dve.tensor_tensor(context[:, 2, cols], context[:, 2, cols], a[:, :], ALU.add))
                        chain.link(dve.tensor_tensor(a[:, :], mem_r[:, cols], sq[:, cols], ALU.mult))
                        chain.link(dve.tensor_tensor(context[:, 3, cols], mem_i[:, cols], cq[:, cols], ALU.mult))
                        chain.link(dve.tensor_tensor(context[:, 3, cols], context[:, 3, cols], a[:, :], ALU.subtract))
                        assert chain.n == steps2
                    sig("dve_step").advance(B * steps2)

                @block.scalar
                def _(act):
                    for b in range(B):
                        cols = bass.ts(b, S)
                        act.wait_ge(sig("angle_reduced").sem, sig("angle_reduced").at(b + 1))
                        act.activation(sq[:, cols], angle[:, cols], ACT.Sin).then_inc(sig("sines").sem, 1)
                        act.activation(cq[:, cols], angle[:, cols], ACT.Abs).then_inc(sig("sines").sem, 1)
                        act.wait_ge(sig("sines").sem, sig("sines").at(b * 3 + 2))
                        act.activation(cq[:, cols], cq[:, cols], ACT.Sin, scale=-1.0, bias=k.half_pi[:, 0:1]).then_inc(sig("sines").sem, 1)

                @block.gpsimd
                def _(pool):
                    with pool.Fori(0, B) as b:
                        cols = bass.ts(b, S)
                        pool.tensor_tensor(context[:, 0, cols], x[:, cols], cos[:, :], ALU.mult)
                        pool.tensor_tensor(context[:, 1, cols], x[:, cols], sin[:, :], ALU.mult)
            sig("angle_reduced").advance(B)
            sig("sines").advance(3 * B)

        with ExitStack() as st2:
            mu = k.ps("mu", [P, 2, S], stack=st2)
            var = k.ps("var", [P, 2, S], stack=st2)
            h_ps = k.ps("h_ps", [P, 2, S], stack=st2)
            o_ps = k.ps("o_ps", [P, 2, S], stack=st2)
            sqr = k.sb("sqr", [P, 4, S], stack=st2)
            rs = k.sb("rs", [P, NT], stack=st2)
            hidden = k.sb("hidden", [P, 2, S], stack=st2)
            with nc.Block() as block:

                def variances(pe, b):
                    for f in range(4):
                        pe.wait_ge(sig("squared").sem, sig("squared").at(b * 4 + f + 1))
                        last = pe.matmul(var[:, b % 2, :], k.mean_of_4[:, :], sqr[:, f, :], start=(f == 0), stop=(f == 3))
                    last.then_inc(sig("variance").sem, 1)

                @block.tensor
                def _(pe):
                    for b in range(B):
                        for f in range(4):
                            last = pe.matmul(mu[:, b % 2, :], k.mean_of_4[:, :], context[:, f, b * S:(b + 1) * S], start=(f == 0), stop=(f == 3))
                        last.then_inc(sig("context_mean").sem, 1)
                        if b < 1:
                            continue
                        variances(pe, b - 1)
                    variances(pe, B - 1)
                    with pe.Fori(0, B) as b:
                        cols = bass.ts(b, S)
                        for g in range(2):
                            pe.wait_ge(sig("gelus").sem, sig("gelus").at(b * 2 + g - 1))
                            for f in range(4):
                                pe.wait_ge(sig("context_normed").sem, sig("context_normed").at(b * 4 + f + 1))
                                last = pe.matmul(h_ps[:, g, :], mats("W1", f * 2 + g), context[:, f, cols], start=(f == 0), stop=(f == 3))
                            last.then_inc(sig("hidden_product").sem, 1)
                        pe.wait_ge(sig("residual").sem, sig("residual").at(b))
                        for g in range(2):
                            pe.wait_ge(sig("gelus").sem, sig("gelus").at(b * 2 + g + 1))
                            last = pe.matmul(o_ps[:, 0, :], mats("W2", g), hidden[:, g, :], start=(g == 0), stop=(g == 1))
                        last.then_inc(sig("mlp_out").sem, 1)

                @block.scalar
                def _(act):
                    for b in range(B):
                        cols = slice(b * S, (b + 1) * S)
                        act.wait_ge(sig("variance").sem, sig("variance").at(b))
                        for f in range(4):
                            act.wait_ge(sig("context_centred").sem, sig("context_centred").at(b * 4 + f + 1))
                            act.activation(sqr[:, f, :], context[:, f, cols], ACT.Square).then_inc(sig("squared").sem, 1)
                        act.wait_ge(sig("variance").sem, sig("variance").at(b + 1))
                        act.activation(rs[:, cols], var[:, b % 2, :], ACT.Ln, bias=k.eps[:, 0:1]).then_inc(sig("rstd").sem, 1)
                        act.wait_ge(sig("rstd").sem, sig("rstd").at(b * 2 + 1))
                        act.activation(rs[:, cols], rs[:, cols], ACT.Exp, scale=-0.5).then_inc(sig("rstd").sem, 1)
                    with act.Fori(0, B) as b:
                        for g in range(2):
                            act.wait_ge(sig("hidden_product").sem, sig("hidden_product").at(b * 2 + g + 1))
                            act.wait_ge(sig("mlp_out").sem, sig("mlp_out").at(b))
                            act.activation(hidden[:, g, :], h_ps[:, g, :], ACT.Gelu, bias=vec("b1", g)).then_inc(sig("gelus").sem, 1)

                @block.vector
                def _(dve):
                    def centre(b):
                        cols = slice(b * S, (b + 1) * S)
                        dve.wait_ge(sig("context_mean").sem, sig("context_mean").at(b + 1))
                        for f in range(4):
                            dve.tensor_tensor(context[:, f, cols], context[:, f, cols], mu[:, b % 2, :], ALU.subtract).then_inc(sig("context_centred").sem, 1)

                    def norm(b):
                        cols = slice(b * S, (b + 1) * S)
                        dve.wait_ge(sig("rstd").sem, sig("rstd").at(b * 2 + 2))
                        for f in range(4):
                            dve.tensor_tensor(context[:, f, cols], context[:, f, cols], rs[:, cols], ALU.mult).then_inc(sig("dve_step").sem, 1)
                        for f in range(4):
                            dve.wait_ge(sig("dve_step").sem, sig("dve_step").at(b * 4 + f + 1))
                            dve.tensor_scalar(context[:, f, cols], context[:, f, cols], vec("ln_g", f), vec("ln_b", f), ALU.mult, ALU.add).then_inc(sig("context_normed").sem, 1)

                    centre(0)
                    for b in range(B):
                        if b + 1 < B:
                            centre(b + 1)
                        norm(b)
                    with dve.Fori(0, B) as b:
                        cols = bass.ts(b, S)
                        dve.tensor_tensor(k.X[:, cols], k.X[:, cols], x[:, cols], ALU.add).then_inc(sig("normed").sem, 1)
                        dve.wait_ge(sig("mlp_out").sem, sig("mlp_out").at(b + 1))
                        dve.wait_ge(sig("normed").sem, sig("normed").at(b + 1))
                        dve.scalar_tensor_tensor(out=k.X[:, cols], in0=o_ps[:, 0, :], scalar=vec("b2"), in1=k.X[:, cols],
                                                 op0=ALU.add, op1=ALU.add).then_inc(sig("residual").sem, 1)

                block.gpsimd(also["gpsimd"])
                block.sync(also["sync"])
            for name, n in (("context_mean", B), ("context_centred", 4 * B), ("squared", 4 * B), ("variance", B), ("rstd", 2 * B), ("dve_step", 4 * B),
                            ("context_normed", 4 * B), ("hidden_product", 2 * B), ("gelus", 2 * B), ("mlp_out", B), ("normed", B), ("residual", B)):
                sig(name).advance(n)


PARTS = 3
PAIRS = PARTS * PARTS
STACK = PAIRS * HD
HALF = HEADS // 2
GROUP = HALF // 2
LOW, SUMS = GROUP * HD, 2 * GROUP * HD
VCOLS = SUMS + GROUP
VWIDE = HALF * VCOLS + SUMS + GROUP
RINGS = 4
SOFTMAX_SCALE = float(HD) ** -0.5


def attention(k, x, ctx, seq, chunks, chunk, weight, bias, rope=None, residual=False):
    nc = k.nc
    sig = k.count_of
    tile = min(P, seq)
    per = chunk // tile
    assert per == 4 and chunks * chunk == x.shape[1]
    tokens = chunks * chunk

    def keys_of(t):
        g = t * tile // seq
        return slice(g * seq, (g + 1) * seq)

    parts_dram = k.scratch("parts", [2, chunks * PARTS * HD, HEADS * chunk])
    peaks_dram = k.scratch("peaks", [2, PARTS * HALF, chunk])

    with ExitStack() as st:
        values = k.sb("values", [P, chunks * per, P], stack=st)
        sums = k.sb("sums", [P, tokens], stack=st)

        queries = k.sb("queries", [P, 2, HALF, chunk], BF16, stack=st)
        keys = k.sb("keys", [P, 2, HALF, chunk], BF16, stack=st)
        spread = k.sb("spread", [P, 2 * per, VWIDE], F32R, stack=st)

        def columns(slot, first, stride, width, bits=False):
            out = []
            for g in range(HALF // GROUP):
                at = g * GROUP * VCOLS + first
                a = spread[0:tile, slot, at:at + GROUP * stride]
                if bits:
                    a = a.bitcast(F32)
                out.append(a.rearrange("p t (h w) -> p t h w", w=stride)[:, :, :, 0:width])
            return out

        with ExitStack() as st2:
            proj = k.ps("proj", [P, 3, 512], stack=st2)
            rot = k.ps("rot", [P, 2, 512], stack=st2)
            vt = k.ps("vt", [P, 512], stack=st2)
            biased = k.sb("biased", [P, 3, chunk], stack=st2)
            turned = k.sb("turned", [P, 2, chunk], stack=st2)
            parts = k.sb("parts", [P, chunks, 2 * PARTS, chunk], BF16, stack=st2)
            with nc.Block() as block:

                @block.tensor
                def _(pe):
                    with pe.Fori(0, chunks) as c:
                        for w in range(3):
                            pe.wait_ge(sig("projected").sem, sig("projected").at(c * 3 + w - 2))
                            pe.matmul(proj[:, w, 0:chunk], weight(w), x[:, bass.ts(c, chunk)], start=True, stop=True).then_inc(sig("projection").sem, 1)
                        if rope:
                            for w in range(2):
                                pe.wait_ge(sig("projected").sem, sig("projected").at(c * 3 + w + 1))
                                pe.wait_ge(sig("rotated").sem, sig("rotated").at(c * 2 + w - 1))
                                pe.matmul(rot[:, w, 0:chunk], rope[0], biased[:, w, :], start=True, stop=True).then_inc(sig("rotation").sem, 1)
                        pe.wait_ge(sig("projected").sem, sig("projected").at(c * 3 + 3))
                        pe.wait_ge(sig("values_kept").sem, sig("values_kept").at(c))
                        for t in range(per):
                            last = pe.transpose(vt[0:tile, t * P:(t + 1) * P], biased[:, 2, t * tile:(t + 1) * tile], k.ident)
                        last.then_inc(sig("values_turned").sem, 1)

                @block.scalar
                def _(act):
                    with act.Fori(0, chunks) as c:
                        for w in range(3):
                            act.wait_ge(sig("projection").sem, sig("projection").at(c * 3 + w + 1))
                            if w < 2:
                                act.wait_ge(sig("parts_made").sem, sig("parts_made").at(c * 2 + w - 1))
                            else:
                                act.wait_ge(sig("values_turned").sem, sig("values_turned").at(c))
                            act.activation(biased[:, w, :], proj[:, w, 0:chunk], ACT.Identity, bias=bias(w)).then_inc(sig("projected").sem, 1)

                @block.vector
                def _(dve):
                    steps = 2 * (3 + (2 if rope else 0))
                    with dve.Fori(0, chunks) as c:
                        chain = Chain(dve, sig("dve_step"), c, steps)
                        for w in range(2):
                            src = biased[:, w, :]
                            dve.wait_ge(sig("projected").sem, sig("projected").at(c * 3 + w + 1))
                            if rope:
                                chain.link(dve.tensor_tensor(turned[:, w, :], biased[:, w, :], rope[1], ALU.mult))
                                dve.wait_ge(sig("rotation").sem, sig("rotation").at(c * 2 + w + 1))
                                dve.tensor_tensor(biased[:, w, :], rot[:, w, 0:chunk], rope[2], ALU.mult).then_inc(sig("rotated").sem, 1)
                                dve.wait_ge(sig("rotated").sem, sig("rotated").at(c * 2 + w + 1))
                                chain.link(dve.tensor_tensor(biased[:, w, :], biased[:, w, :], turned[:, w, :], ALU.add))
                            at = [parts[:, c, w * PARTS + n, :] for n in range(PARTS)]
                            chain.link(dve.tensor_copy(at[0], src))
                            chain.link(dve.tensor_tensor(turned[:, w, :], src, at[0], ALU.subtract))
                            chain.link(dve.tensor_copy(at[1], turned[:, w, :]))
                            dve.tensor_tensor(at[2], turned[:, w, :], at[1], ALU.subtract).then_inc(sig("parts_made").sem, 1)
                        assert chain.n == steps
                        dve.wait_ge(sig("values_turned").sem, sig("values_turned").at(c + 1))
                        dve.tensor_copy(values[0:tile, bass.ts(c, per), :], vt[0:tile, :].rearrange("p (t n) -> p t n", n=P)).then_inc(sig("values_kept").sem, 1)
                    sig("dve_step").advance(chunks * steps)

                @block.gpsimd
                def _(pool):
                    chain = Chain(pool, sig("pool_step"))
                    chain.link(pool.memset(keys[64:P, :, :, :], 1.0))
                    chain.link(pool.memset(sums[:, :], 1.0))
                    chain.link(pool.memset(spread[0:tile, :, :].bitcast(F32), 0.0))
                    for ones in columns(slice(0, 2 * per), SUMS, VCOLS + 1, 1):
                        chain.link(pool.memset(ones.bitcast(F32), 1.0))
                    sig("pool_step").advance(chain.n)

                @block.sync
                def _(sp):
                    with sp.Fori(0, chunks) as c:
                        for w in range(2):
                            sp.wait_ge(sig("parts_made").sem, sig("parts_made").at(c * 2 + w + 1))
                            for n in range(PARTS):
                                to = parts_dram[w, bass.ds((c * PARTS + n) * HD, HD), :].rearrange("d (h t) -> h d t", t=chunk)
                                sp.dma_start(to, parts[:, c, w * PARTS + n, :]).then_inc(sig("parts_stored").sem, 16)
                    sp.wait_ge(sig("parts_stored").sem, sig("parts_stored").at(2 * PARTS * chunks))
            for name, n in (("projection", 3 * chunks), ("projected", 3 * chunks), ("rotation", 2 * chunks if rope else 0),
                            ("rotated", 2 * chunks if rope else 0), ("values_turned", chunks), ("values_kept", chunks),
                            ("parts_made", 2 * chunks), ("parts_stored", 2 * PARTS * chunks)):
                sig(name).advance(n)

        with ExitStack() as st2:
            banks = k.ps("banks", [P, 8, 512], stack=st2)
            s_ps, m_ps, o_ps = banks[:, 0:4, :], banks[:, 4:6, :], banks[:, 6:8, :]
            peaks_as_rows = m_ps[0:PARTS * HALF, 0, :].bitcast(BF16)
            p_hi = k.sb("p_hi", [P, RINGS, 2, seq], F32R, stack=st2)
            p_lo = k.sb("p_lo", [P, RINGS, 2, seq], F32R, stack=st2)
            probs = k.sb("probs", [P, RINGS, 2, seq], stack=st2)
            unit_values = k.sb("unit_values", [P, per, HALF * HD], stack=st2)
            by_low = k.sb("by_low", [GROUP * HD, 2, chunk], stack=st2)
            peak = k.sb("peak", [P, per, HALF], stack=st2)
            peak_parts = k.sb("peak_parts", [P, per, PARTS * HALF], BF16, stack=st2)
            peak_rows = k.sb("peak_rows", [PARTS * HALF, chunk], BF16, stack=st2)
            HALVES = 2 * HALF
            BANK = HALVES // 2
            BLOCKS = per * HALF
            DMAS = PARTS + 1
            LAG = 3
            PEAKS_FROM, PEAKS_BY = 10, 7
            ROWS_AT = 8

            def first_bank(u, h):
                return 4 * (h % 2) if u == 0 else 4

            def on_pool(m, tile_):
                return tile_ == 1 or m in (0, 3)

            made = {"pool": [0], "dve": [0]}
            for m in range(HALVES):
                for who in made:
                    made[who].append(made[who][-1] + sum(on_pool(m, t) == (who == "pool") for t in range(2)))

            def units(eng, body):
                if chunks > 1:
                    with eng.Fori(0, chunks - 1) as c:
                        body(c, 0, 2)
                        body(c, 1, 2)
                body(chunks - 1, 0, 1)
                body(chunks - 1, 1, 0)

            def ahead(u, half, more, n, by):
                if n + by < HALVES:
                    return u, half, n + by
                return (u + 1, 1 - half, n + by - HALVES) if more else None

            def peak_blocks(n, more):
                half_ = BLOCKS // 2
                if n < PEAKS_BY and more >= 1:
                    return [(1, half_ + b) for b in range(n * half_ // PEAKS_BY, (n + 1) * half_ // PEAKS_BY)]
                if n >= PEAKS_FROM and more >= 2:
                    steps, n = HALVES - PEAKS_FROM, n - PEAKS_FROM
                    return [(2, b) for b in range(n * half_ // steps, (n + 1) * half_ // steps)]
                return []

            with nc.Block() as block:

                @block.tensor
                def _(pe):
                    def peak_scores(u, slot, block_):
                        h, t = divmod(block_, per)
                        pe.wait_ge(sig("peak_found").sem, sig("peak_found").at(u * BLOCKS + block_ - 1))
                        if block_ % (BLOCKS // 2) == 0:
                            stack_in = sig(f"stack_in_{slot * 2 + h // GROUP}")
                            pe.wait_ge(stack_in.sem, stack_in.at((u - slot + 2) * (DMAS // 2)))
                        if block_ == 0:
                            pe.wait_ge(sig("peak_rows").sem, sig("peak_rows").at(u))
                        pe.matmul(m_ps[0:tile, t % 2, 0:seq], queries[0:STACK, slot, h, t * tile:(t + 1) * tile],
                                  keys[0:STACK, slot, h, keys_of(t)], start=True, stop=True).then_inc(sig("peak_scores").sem, 1)

                    def first_peaks(u, h):
                        pe.wait_ge(sig("peak_found").sem, sig("peak_found").at((u * HALF + h - (1 - u)) * per))
                        if h % GROUP == 0:
                            stack_in = sig(f"stack_in_{u * 2 + h // GROUP}")
                            pe.wait_ge(stack_in.sem, stack_in.at(DMAS))
                        if h == 0:
                            pe.wait_ge(sig("peak_rows").sem, sig("peak_rows").at(u))
                        for t in range(per):
                            last = pe.matmul(banks[0:tile, first_bank(u, h) + t, 0:seq], queries[0:STACK, u, h, t * tile:(t + 1) * tile],
                                             keys[0:STACK, u, h, keys_of(t)], start=True, stop=True)
                        last.then_inc(sig("peak_scores").sem, per)

                    def peaks_turned(u):
                        pe.wait_ge(sig("peaks_split").sem, sig("peaks_split").at(u + 1))
                        for t in range(per):
                            last = pe.transpose(peaks_as_rows[:, t * tile:(t + 1) * tile], peak_parts[0:tile, t, :], k.ident_bf[0:tile, 0:tile])
                        last.then_inc(sig("peaks_turned").sem, 1)

                    def scores(u, slot, m):
                        if m == 0:
                            pe.wait_ge(sig("peaks_in").sem, sig("peaks_in").at(u + 1))
                        pe.wait_ge(sig("probs").sem, sig("probs").at(u * HALVES + m - 1))
                        for t in (m % 2 * 2, m % 2 * 2 + 1):
                            last = pe.matmul(s_ps[0:tile, t, 0:seq], keys[0:STACK + PARTS, slot, m // 2, t * tile:(t + 1) * tile],
                                             queries[0:STACK + PARTS, slot, m // 2, keys_of(t)], start=True, stop=True)
                        last.then_inc(sig("scores").sem, 1)

                    def context(u, half, m, between):
                        bank, first = divmod(m, BANK)
                        if m == 0:
                            pe.wait_ge(sig("values_spread").sem, sig("values_spread").at(u + 1))
                        if first == 0:
                            pe.wait_ge(sig("context_kept").sem, sig("context_kept").at(u * 2 + bank - 1))
                            pe.wait_ge(sig("sums_kept").sem, sig("sums_kept").at(u * 2 + bank - 1))
                        pe.wait_ge(sig("probs_low").sem, sig("probs_low").at(u * made["dve"][-1] + made["dve"][m + 1]))
                        pe.wait_ge(sig("probs_low_pool").sem, sig("probs_low_pool").at(u * made["pool"][-1] + made["pool"][m + 1]))
                        for two in range(2):
                            t = m % 2 * 2 + two
                            for part in (p_hi, p_lo):
                                last = pe.matmul(o_ps[0:VCOLS, bank, keys_of(t)], spread[0:tile, half * per + t, m // 2 * VCOLS:(m // 2 + 1) * VCOLS],
                                                 part[0:tile, m % RINGS, two, :], start=(first == 0 and two == 0 and part is p_hi),
                                                 stop=(first == BANK - 1 and two == 1 and part is p_lo), skip_group_check=True)
                                if two == 1 and part is p_lo:
                                    last.then_inc(sig("context_sums").sem, 1)
                                between()

                    def unit(c, half, more):
                        u = c * 2 + half
                        for n in range(HALVES):
                            blocks = peak_blocks(n, more)
                            spots = [4]

                            def between():
                                for _ in range(-(-len(blocks) // spots[0]) if spots[0] else 0):
                                    on, block_ = blocks.pop(0)
                                    peak_scores(u + on, (half + on) % 2, block_)
                                spots[0] -= 1

                            step = ahead(u, half, more, n, LAG)
                            if step:
                                scores(*step)
                            context(u, half, n, between)
                            if more and n == PEAKS_BY:
                                peaks_turned(u + 1)

                    for h in range(HALF):
                        first_peaks(0, h)
                    peaks_turned(0)
                    first_peaks(1, 0)
                    for m in range(LAG):
                        first_peaks(1, m + 1)
                        scores(0, 0, m)
                    pe.wait_ge(sig("peak_found").sem, sig("peak_found").at(BLOCKS + BLOCKS // 2))
                    units(pe, unit)

                @block.scalar
                def _(act):
                    def peak_rows_kept(u):
                        act.wait_ge(sig("peaks_turned").sem, sig("peaks_turned").at(u + 1))
                        act.wait_ge(sig("peaks_out").sem, sig("peaks_out").at(u))
                        act.activation(peak_rows[:, :], peaks_as_rows[:, 0:chunk], ACT.Copy).then_inc(sig("peak_rows").sem, 1)

                    def exponentials(u, _, m):
                        act.wait_ge(sig("context_sums").sem, sig("context_sums").at(u * HALVES + m + 1 - RINGS))
                        act.wait_ge(sig("scores").sem, sig("scores").at(u * HALVES + m + 1))
                        of = s_ps[0:tile, m % 2 * 2:m % 2 * 2 + 2, 0:seq]
                        act.activation(probs[0:tile, m % RINGS, :, :], of, ACT.Exp, scale=SOFTMAX_SCALE)
                        act.activation(p_hi[0:tile, m % RINGS, :, :], of, ACT.Exp, scale=SOFTMAX_SCALE).then_inc(sig("probs").sem, 1)

                    def kept(c, half, bank):
                        u = c * 2 + half
                        cols = bass.ts(c, chunk)
                        at = (half * 2 + bank) * 32
                        act.wait_ge(sig("context_kept").sem, sig("context_kept").at(u * 2 + bank - 1))
                        act.wait_ge(sig("context_sums").sem, sig("context_sums").at(u * HALVES + (bank + 1) * BANK))
                        act.activation(by_low[:, bank, :], o_ps[LOW:SUMS, bank, 0:chunk], ACT.Copy).then_inc(sig("context_low").sem, 1)
                        act.activation(sums[at:at + GROUP, cols], o_ps[SUMS:VCOLS, bank, 0:chunk], ACT.Copy).then_inc(sig("sums_kept").sem, 1)

                    def unit(c, half, more):
                        u = c * 2 + half
                        for n in range(HALVES):
                            if n % BANK == BANK - 1:
                                kept(c, half, n // BANK)
                            step = ahead(u, half, more, n, RINGS)
                            if step:
                                exponentials(*step)
                            if more and n == ROWS_AT:
                                peak_rows_kept(u + 1)

                    peak_rows_kept(0)
                    for m in range(RINGS):
                        exponentials(0, 0, m)
                    units(act, unit)

                @block.vector
                def _(dve):
                    steps = 4

                    def found(u, block_):
                        h, t = divmod(block_, per)
                        dve.wait_ge(sig("peak_scores").sem, sig("peak_scores").at(u * BLOCKS + block_ + 1))
                        dve.tensor_reduce(peak[0:tile, t, h:h + 1], m_ps[0:tile, t % 2, 0:seq], AX.X, ALU.max).then_inc(sig("peak_found").sem, 1)

                    def first_found(u, h):
                        dve.wait_ge(sig("peak_scores").sem, sig("peak_scores").at(u * BLOCKS + (h + 1) * per))
                        of = banks[0:tile, first_bank(u, h):first_bank(u, h) + per, 0:seq]
                        dve.tensor_reduce(peak[0:tile, :, h], of, AX.X, ALU.max).then_inc(sig("peak_found").sem, per)

                    def split(u):
                        dve.wait_ge(sig("peak_found").sem, sig("peak_found").at(u * BLOCKS + BLOCKS))
                        dve.wait_ge(sig("peaks_turned").sem, sig("peaks_turned").at(u))
                        chain = Chain(dve, sig("dve_step"), u, steps)
                        at = [peak_parts[0:tile, :, n * HALF:(n + 1) * HALF] for n in range(PARTS)]
                        chain.link(dve.tensor_scalar(peak[0:tile, :, :], peak[0:tile, :, :], -1.0, None, ALU.mult))
                        chain.link(dve.tensor_copy(at[0], peak[0:tile, :, :]))
                        chain.link(dve.tensor_tensor(peak[0:tile, :, :], peak[0:tile, :, :], at[0], ALU.subtract))
                        chain.link(dve.tensor_copy(at[1], peak[0:tile, :, :]))
                        assert chain.n == steps
                        dve.tensor_tensor(at[2], peak[0:tile, :, :], at[1], ALU.subtract).then_inc(sig("peaks_split").sem, 1)

                    def low(u, _, m):
                        dve.wait_ge(sig("probs").sem, sig("probs").at(u * HALVES + m + 1))
                        for t in range(2):
                            if not on_pool(m, t):
                                dve.tensor_tensor(p_lo[0:tile, m % RINGS, t, :], probs[0:tile, m % RINGS, t, :], p_hi[0:tile, m % RINGS, t, :].bitcast(F32),
                                                  ALU.subtract).then_inc(sig("probs_low").sem, 1)

                    def unit(c, half, more):
                        u = c * 2 + half
                        for n in range(HALVES):
                            for on, block_ in peak_blocks(n, more):
                                found(u + on, block_)
                            if more and n == PEAKS_BY - 1:
                                split(u + 1)
                            step = ahead(u, half, more, n, LAG)
                            if step:
                                low(*step)
                            if n in (BANK, HALVES - 1):
                                bank = n // BANK - (n == BANK)
                                at = (half * 2 + bank) * 32
                                dve.wait_ge(sig("context_low").sem, sig("context_low").at(u * 2 + bank + 1))
                                dve.tensor_tensor(ctx[at:at + GROUP * HD, bass.ts(c, chunk)], o_ps[0:LOW, bank, 0:chunk], by_low[:, bank, :],
                                                  ALU.add).then_inc(sig("context_kept").sem, 1)

                    for h in range(HALF):
                        first_found(0, h)
                    split(0)
                    first_found(1, 0)
                    for m in range(LAG):
                        first_found(1, m + 1)
                        if m > 0:
                            low(0, 0, m - 1)
                    low(0, 0, LAG - 1)
                    units(dve, unit)
                    sig("dve_step").advance(2 * chunks * steps)

                @block.gpsimd
                def _(pool):
                    def values_spread(c, half):
                        u = c * 2 + half
                        pool.wait_ge(sig("context_sums").sem, sig("context_sums").at(u * HALVES - HALVES))
                        slot = slice(half * per, (half + 1) * per)
                        def split_heads(a):
                            return [a[:, :, g * GROUP * HD:(g + 1) * GROUP * HD].rearrange("p t (h w) -> p t h w", w=HD) for g in range(HALF // GROUP)]

                        of = values[0:tile, bass.ts(c, per), half * HALF * HD:(half + 1) * HALF * HD]
                        pool.tensor_copy(unit_values[0:tile, :, :], of).then_inc(sig("pool_step").sem, 1)
                        for to, v in zip(columns(slot, 0, VCOLS + HD, HD), split_heads(of)):
                            pool.tensor_copy(to, v).then_inc(sig("pool_step").sem, 1)
                        pool.wait_ge(sig("pool_step").sem, sig("pool_step").at(u * 3 + 3))
                        for to, v, hi in zip(columns(slot, LOW, VCOLS + HD, HD), split_heads(unit_values[0:tile, :, :]), columns(slot, 0, VCOLS + HD, HD, bits=True)):
                            last = pool.tensor_tensor(to, v, hi, ALU.subtract)
                        last.then_inc(sig("values_spread").sem, 1)

                    def low(u, _, m):
                        for t in range(2):
                            if on_pool(m, t):
                                pool.wait_ge(sig("probs").sem, sig("probs").at(u * HALVES + m + 1))
                                pool.tensor_tensor(p_lo[0:tile, m % RINGS, t, :], probs[0:tile, m % RINGS, t, :], p_hi[0:tile, m % RINGS, t, :].bitcast(F32),
                                                   ALU.subtract).then_inc(sig("probs_low_pool").sem, 1)

                    def unit(c, half, more):
                        u = c * 2 + half
                        for n in range(HALVES):
                            low(u, half, n)
                            if more and n == BANK:
                                values_spread(c + half, 1 - half)

                    values_spread(0, 0)
                    units(pool, unit)

                @block.sync
                def _(sp):
                    def stack(c, slot, group):
                        u = c * 2 + slot
                        sp.wait_ge(sig("scores").sem, sig("scores").at(u * HALVES - 2 * HALVES + (group + 1) * BANK))
                        came = sig(f"stack_in_{slot * 2 + group}")
                        heads = slice(group * GROUP, (group + 1) * GROUP)
                        first = (slot * HALF + group * GROUP) * chunk
                        cols = slice(first, first + GROUP * chunk)
                        every = PARTS * HD
                        for i in range(PARTS):
                            of = parts_dram[0, bass.ds((c * PARTS + i) * HD, HD), cols]
                            sp.dma_start(queries[i * every:(i + 1) * every, slot, heads, :], of.unsqueeze(0).to_broadcast([PARTS, HD, GROUP * chunk])).then_inc(came.sem, 16)
                        of = parts_dram[1, bass.ds(c * every, every), cols]
                        sp.dma_start(keys[0:STACK, slot, heads, :], of.unsqueeze(0).to_broadcast([PARTS, every, GROUP * chunk])).then_inc(came.sem, 16)

                    def peak_rows_in(u, slot):
                        sp.wait_ge(sig("peak_rows").sem, sig("peak_rows").at(u + 1))
                        sp.dma_start(peaks_dram[slot, :, :], peak_rows[:, :]).then_inc(sig("peaks_out").sem, 16)
                        sp.wait_ge(sig("peaks_out").sem, sig("peaks_out").at(u + 1))
                        sp.dma_start(queries[STACK:STACK + PARTS, slot, :, :], peaks_dram[slot, :, :].rearrange("(n h) t -> n h t", h=HALF)).then_inc(sig("peaks_in").sem, 16)

                    def unit(c, half, more):
                        if more == 2:
                            stack(c + 1, half, 0)
                        if more:
                            peak_rows_in(c * 2 + half + 1, 1 - half)
                        if more == 2:
                            stack(c + 1, half, 1)

                    for slot in range(2):
                        for group in range(2):
                            stack(0, slot, group)
                    peak_rows_in(0, 0)
                    units(sp, unit)
            n = 2 * chunks
            for name, total in (("peak_found", n * BLOCKS), ("peak_scores", n * BLOCKS), ("peaks_split", n), ("peaks_turned", n), ("peak_rows", n),
                                ("peaks_out", n), ("peaks_in", n), ("scores", n * HALVES), ("probs", n * HALVES), ("context_sums", n * HALVES),
                                ("probs_low", n * made["dve"][-1]), ("probs_low_pool", n * made["pool"][-1]), ("context_low", 2 * n),
                                ("context_kept", 2 * n), ("sums_kept", 2 * n), ("values_spread", n), ("pool_step", 3 * n),
                                *[(f"stack_in_{s}", chunks * DMAS) for s in range(4)]):
                sig(name).advance(total)

        with ExitStack() as st2:
            per_row = k.ps("per_row", [P, chunks, 512], stack=st2)
            with nc.Block() as block:

                @block.tensor
                def _(pe):
                    for c in range(chunks):
                        pe.wait_ge(sig("memories").sem, sig("memories").at(c + 1))
                        pe.matmul(per_row[:, c, 0:chunk], k.head_rows[:, :], sums[:, c * chunk:(c + 1) * chunk],
                                  start=True, stop=True).then_inc(sig("sums_spread").sem, 1)

                @block.vector
                def _(dve):
                    for c in range(chunks):
                        cols = slice(c * chunk, (c + 1) * chunk)
                        dve.reciprocal(sums[:, cols], sums[:, cols]).then_inc(sig("memories").sem, 1)
                    for c in range(chunks):
                        cols = slice(c * chunk, (c + 1) * chunk)
                        dve.wait_ge(sig("sums_spread").sem, sig("sums_spread").at(c + 1))
                        last = dve.tensor_tensor(ctx[:, cols], ctx[:, cols], per_row[:, c, 0:chunk], ALU.mult)
                        if residual:
                            last.then_inc(sig("normed").sem, 1)
                    if residual:
                        for c in range(chunks):
                            cols = slice(c * chunk, (c + 1) * chunk)
                            dve.wait_ge(sig("normed").sem, sig("normed").at(c + 1))
                            dve.tensor_tensor(k.X[:, cols], k.X[:, cols], ctx[:, cols], ALU.add)
                        sig("normed").advance(chunks)
            sig("sums_spread").advance(chunks)
            sig("memories").advance(chunks)


def sampled(k, x, parts):
    with k.nc.Block() as block:

        @block.gpsimd
        def _(pool):
            for l, part in parts.items():
                whole = x.rearrange("p (n s) -> p n s", s=2 ** l)
                pool.tensor_copy(part, whole[:, :, 0])


def combine_levels(k, contexts, out_w, up_w, out_b, up_b, also):
    nc = k.nc
    sig = k.count_of
    with ExitStack() as st:
        ps = k.ps("level_ps", [P, 4, 512], stack=st)
        level = [k.sb(f"level{l}", [P, NT >> l], stack=st) for l in range(LEVELS)]
        quarter = k.sb("quarter", [P, NT // 2], stack=st)
        fine = [k.sb(f"fine{l}", [P, NT >> l], stack=st) for l in range(LEVELS - 1)]
        both = k.sb("both_b", [P, LEVELS], stack=st)
        work = []
        for l in range(LEVELS - 1, -1, -1):
            n = NT >> l
            work += [(l, at, min(CH, n - at)) for at in range(0, n, CH)]
        done = {l: sum(1 for w in work if w[0] >= l) for l in range(LEVELS)}
        with nc.Block() as block:

            @block.tensor
            def _(pe):
                for n, (l, at, size) in enumerate(work):
                    pe.wait_ge(sig("level_kept").sem, sig("level_kept").at(n - 3))
                    coarser = l < LEVELS - 1
                    last = pe.matmul(ps[:, n % 4, 0:size], out_w(l), contexts[l][:, at:at + size], start=True, stop=not coarser)
                    if coarser:
                        pe.wait_ge(sig("upsampled").sem, sig("upsampled").at(LEVELS - 1 - l))
                        last = pe.matmul(ps[:, n % 4, 0:size], up_w(l), fine[l][:, at:at + size], start=False, stop=True)
                    last.then_inc(sig("level_product").sem, 1)

            @block.scalar
            def _(act):
                act.wait_ge(sig("normed").sem, sig("normed").at(1))
                for n, (l, at, size) in enumerate(work):
                    act.wait_ge(sig("level_product").sem, sig("level_product").at(n + 1))
                    act.activation(level[l][:, at:at + size], ps[:, n % 4, 0:size], ACT.Identity, bias=both[:, l:l + 1]).then_inc(sig("level_kept").sem, 1)
                also["scalar"](act)

            @block.vector
            def _(dve):
                chain = Chain(dve, sig("dve_step"))
                chain.link(dve.tensor_copy(both[:, :], out_b))
                dve.tensor_tensor(both[:, 0:LEVELS - 1], both[:, 0:LEVELS - 1], up_b, ALU.add).then_inc(sig("normed").sem, 1)
                for l in range(LEVELS - 2, -1, -1):
                    n = S >> (l + 1)
                    c = level[l + 1][:, :].rearrange("p (b n) -> p b n", n=n)
                    q = quarter[:, 0:B * n].rearrange("p (b n) -> p b n", n=n)
                    u = fine[l][:, :].rearrange("p (b n two) -> p b n two", n=n, two=2)
                    dve.wait_ge(sig("level_kept").sem, sig("level_kept").at(done[l + 1]))
                    chain.link(dve.tensor_scalar(q, c, 0.25, None, ALU.mult))
                    dve.scalar_tensor_tensor(out=u[:, :, 0:n - 1, 1], in0=c[:, :, 0:n - 1], scalar=0.75, in1=q[:, :, 1:n], op0=ALU.mult, op1=ALU.add)
                    dve.scalar_tensor_tensor(out=u[:, :, 1:n, 0], in0=c[:, :, 1:n], scalar=0.75, in1=q[:, :, 0:n - 1], op0=ALU.mult, op1=ALU.add)
                    dve.tensor_copy(u[:, :, 0, 0], c[:, :, 0])
                    dve.tensor_copy(u[:, :, n - 1, 1], c[:, :, n - 1]).then_inc(sig("upsampled").sem, 1)
                    if l > 0:
                        dve.wait_ge(sig("upsampled").sem, sig("upsampled").at(LEVELS - 1 - l))
                for c in range(NC):
                    cols = slice(c * CH, (c + 1) * CH)
                    dve.wait_ge(sig("level_kept").sem, sig("level_kept").at(done[1] + c + 1))
                    dve.tensor_tensor(k.X[:, cols], k.X[:, cols], level[0][:, cols], ALU.add)
                sig("dve_step").advance(chain.n)
                also["vector"](dve)

            block.gpsimd(also["gpsimd"])
            block.sync(also["sync"])
        for name, n in (("level_kept", len(work)), ("level_product", len(work)), ("upsampled", LEVELS - 1), ("normed", 1)):
            sig(name).advance(n)


K_CLAMP = 60.0


def mixed(dve, sig, out, x, coef, b):
    n = sig("mix_step")

    def landed(step):
        dve.wait_ge(n.sem, n.at(b * 2 + step))

    dve.tensor_scalar(out[:, bass.ts(b, S)], x[:, bass.ts(b, S)], coef[:, 0:1], None, ALU.mult).then_inc(n.sem, 1)
    landed(1)
    dve.scalar_tensor_tensor(out=out[:, bass.ds(b * S + 1, S - 1)], in0=x[:, bass.ds(b * S, S - 1)], scalar=coef[:, 1:2], in1=out[:, bass.ds(b * S + 1, S - 1)],
                             op0=ALU.mult, op1=ALU.add).then_inc(n.sem, 1)
    landed(2)
    dve.scalar_tensor_tensor(out=out[:, bass.ds(b * S, S - 1)], in0=x[:, bass.ds(b * S + 1, S - 1)], scalar=coef[:, 2:3], in1=out[:, bass.ds(b * S, S - 1)],
                             op0=ALU.mult, op1=ALU.add).then_inc(sig("mixed").sem, 1)


def mix_coefficients(chain, dve, coef, time_mix, combined_mix, first_half, second_half):
    chain.link(dve.tensor_copy(coef[:, 0:1], time_mix))
    chain.link(dve.tensor_scalar(coef[:, 1:2], time_mix, -1.0, 1.0, ALU.mult, ALU.add))
    chain.link(dve.scalar_tensor_tensor(out=coef[:, 1:2], in0=combined_mix, scalar=first_half, in1=coef[:, 1:2], op0=ALU.mult, op1=ALU.add))
    chain.link(dve.tensor_scalar(coef[:, 2:3], combined_mix, second_half, None, ALU.mult))


def time_mix(k, x, out, mats, vec):
    nc = k.nc
    sig = k.count_of
    with ExitStack() as st:
        k_ps, v_ps, r_ps, o_ps = (k.ps(f"{n}_ps", [P, 2, S], stack=st) for n in "kvro")
        coef = k.sb("coef", [P, 3], stack=st)
        rates = k.sb("rates", [P, 3], stack=st)
        decay = k.sb("decay", [P, S], stack=st)
        xm = k.sb("xm", [P, NT], stack=st)
        key = k.sb("key", [P, NT], stack=st)
        kv = k.sb("kv", [P, NT], stack=st)
        val = k.sb("val", [P, NT], stack=st)
        gate = k.sb("gate", [P, NT], stack=st)
        a = k.sb("a", [P, B, S + 1], stack=st)
        d = k.sb("d", [P, B, S + 1], stack=st)
        with nc.Block() as block:

            @block.tensor
            def _(pe):
                for b in range(B):
                    cols = slice(b * S, (b + 1) * S)
                    pe.wait_ge(sig("mixed").sem, sig("mixed").at(b + 1))
                    pe.wait_ge(sig("key_clamped").sem, sig("key_clamped").at(b - 1))
                    pe.matmul(k_ps[:, b % 2, :], mats("Wk"), xm[:, cols], start=True, stop=True).then_inc(sig("projection").sem, 1)
                    pe.wait_ge(sig("values_copied").sem, sig("values_copied").at(b * 2 - 2))
                    pe.matmul(v_ps[:, b % 2, :], mats("Wv"), xm[:, cols], start=True, stop=True).then_inc(sig("projection").sem, 1)
                    pe.matmul(r_ps[:, b % 2, :], mats("Wr"), xm[:, cols], start=True, stop=True).then_inc(sig("projection").sem, 1)
                for b in range(B):
                    pe.wait_ge(sig("gated").sem, sig("gated").at(b + 1))
                    pe.wait_ge(sig("residual").sem, sig("residual").at(b - 1))
                    pe.matmul(o_ps[:, b % 2, :], mats("Wo"), gate[:, b * S:(b + 1) * S], start=True, stop=True).then_inc(sig("mlp_out").sem, 1)

            @block.scalar
            def _(act):
                r = sig("rstd")
                act.activation(rates[:, 0:1], vec("time_decay"), ACT.Exp).then_inc(r.sem, 1)
                act.activation(rates[:, 2:3], vec("time_first"), ACT.Exp).then_inc(r.sem, 1)
                act.wait_ge(r.sem, r.at(1))
                act.activation(rates[:, 1:2], rates[:, 0:1], ACT.Exp, scale=-1.0).then_inc(r.sem, 1)
                for b in range(B):
                    cols = slice(b * S, (b + 1) * S)
                    act.wait_ge(sig("projection").sem, sig("projection").at(b * 3 + 3))
                    act.activation(val[:, cols], v_ps[:, b % 2, :], ACT.Copy).then_inc(sig("values_copied").sem, 1)
                    act.activation(gate[:, cols], r_ps[:, b % 2, :], ACT.Copy).then_inc(sig("values_copied").sem, 1)
                    act.wait_ge(sig("key_clamped").sem, sig("key_clamped").at(b + 1))
                    act.activation(key[:, cols], key[:, cols], ACT.Exp).then_inc(sig("probs").sem, 1)
                for b in range(B):
                    cols = slice(b * S, (b + 1) * S)
                    act.wait_ge(sig("values_copied").sem, sig("values_copied").at(b * 2 + 2))
                    act.activation(gate[:, cols], gate[:, cols], ACT.Sigmoid).then_inc(sig("sigmoids").sem, 1)

            @block.vector
            def _(dve):
                chain = Chain(dve, sig("dve_step"))
                mix_coefficients(chain, dve, coef, vec("att_time_mix"), vec("att_combined_mix"), vec("first_half"), vec("second_half"))
                chain.link(dve.memset(a[:, :, 0:1], 0.0))
                chain.link(dve.memset(d[:, :, 0:1], 0.0))
                chain.link(dve.memset(decay[:, :], 1.0))
                with dve.Fori(0, B) as b:
                    mixed(dve, sig, xm, x, coef, b)
                dve.wait_ge(sig("rstd").sem, sig("rstd").at(3))
                chain.link(dve.tensor_scalar(decay[:, :], decay[:, :], rates[:, 1:2], None, ALU.mult))
                for b in range(B):
                    cols = slice(b * S, (b + 1) * S)
                    dve.wait_ge(sig("projection").sem, sig("projection").at(b * 3 + 1))
                    dve.tensor_scalar(key[:, cols], k_ps[:, b % 2, :], K_CLAMP, None, ALU.min).then_inc(sig("key_clamped").sem, 1)
                for b in range(B):
                    cols = slice(b * S, (b + 1) * S)
                    dve.wait_ge(sig("probs").sem, sig("probs").at(b + 1))
                    dve.tensor_tensor_scan(d[:, b, 1:S + 1], decay[:, :], key[:, cols], 0.0, ALU.mult, ALU.add).then_inc(sig("memories").sem, 1)
                    dve.wait_ge(sig("key_values").sem, sig("key_values").at(b + 1))
                    dve.tensor_tensor_scan(a[:, b, 1:S + 1], decay[:, :], kv[:, cols], 0.0, ALU.mult, ALU.add).then_inc(sig("memories").sem, 1)
                    dve.wait_ge(sig("memories").sem, sig("memories").at(b * 2 + 2))
                    chain.link(dve.scalar_tensor_tensor(out=key[:, cols], in0=key[:, cols], scalar=rates[:, 2:3], in1=d[:, b, 0:S], op0=ALU.mult, op1=ALU.add))
                    dve.reciprocal(key[:, cols], key[:, cols]).then_inc(sig("rotated").sem, 1)
                    chain.link(dve.scalar_tensor_tensor(out=kv[:, cols], in0=kv[:, cols], scalar=rates[:, 2:3], in1=a[:, b, 0:S], op0=ALU.mult, op1=ALU.add))
                    dve.wait_ge(sig("rotated").sem, sig("rotated").at(b + 1))
                    dve.tensor_tensor(kv[:, cols], kv[:, cols], key[:, cols], ALU.mult).then_inc(sig("averaged").sem, 1)
                for b in range(B):
                    cols = slice(b * S, (b + 1) * S)
                    dve.wait_ge(sig("mlp_out").sem, sig("mlp_out").at(b + 1))
                    dve.tensor_tensor(out[:, cols], x[:, cols], o_ps[:, b % 2, :], ALU.add).then_inc(sig("residual").sem, 1)
                sig("dve_step").advance(chain.n)

            @block.gpsimd
            def _(pool):
                for b in range(B):
                    cols = slice(b * S, (b + 1) * S)
                    pool.wait_ge(sig("probs").sem, sig("probs").at(b + 1))
                    pool.wait_ge(sig("values_copied").sem, sig("values_copied").at(b * 2 + 1))
                    pool.tensor_tensor(kv[:, cols], key[:, cols], val[:, cols], ALU.mult).then_inc(sig("key_values").sem, 1)
                for b in range(B):
                    cols = slice(b * S, (b + 1) * S)
                    pool.wait_ge(sig("sigmoids").sem, sig("sigmoids").at(b + 1))
                    pool.wait_ge(sig("averaged").sem, sig("averaged").at(b + 1))
                    pool.tensor_tensor(gate[:, cols], gate[:, cols], kv[:, cols], ALU.mult).then_inc(sig("gated").sem, 1)
        for name, n in (("mixed", B), ("mix_step", 2 * B), ("projection", 3 * B), ("key_clamped", B), ("values_copied", 2 * B), ("probs", B), ("sigmoids", B),
                        ("rstd", 3), ("memories", 2 * B), ("key_values", B), ("rotated", B), ("averaged", B), ("gated", B), ("mlp_out", B), ("residual", B)):
            sig(name).advance(n)


def channel_mix(k, x, mats, vec):
    nc = k.nc
    sig = k.count_of
    G = 4
    with ExitStack() as st:
        h_ps = k.ps("h_ps", [P, 2, S], stack=st)
        r_ps = k.ps("r_ps", [P, 2, S], stack=st)
        o_ps = k.ps("o_ps", [P, 2, S], stack=st)
        coef = k.sb("coef", [P, 3], stack=st)
        xm = k.sb("xm", [P, NT], stack=st)
        relu = k.sb("relu", [P, G, S], stack=st)
        hidden = k.sb("hidden", [P, G, S], stack=st)
        gate = k.sb("gate", [P, NT], stack=st)
        with nc.Block() as block:

            @block.tensor
            def _(pe):
                def down(n):
                    b, g = n // G, n % G
                    pe.wait_ge(sig("silu_up").sem, sig("silu_up").at(n + 1))
                    if g == 0:
                        pe.wait_ge(sig("residual").sem, sig("residual").at(b - 1))
                    last = pe.matmul(o_ps[:, b % 2, :], mats("Fv", g), hidden[:, g, :], start=(g == 0), stop=(g == G - 1))
                    if g == G - 1:
                        last.then_inc(sig("mlp_out").sem, 1)

                for b in range(B):
                    cols = slice(b * S, (b + 1) * S)
                    pe.wait_ge(sig("mixed").sem, sig("mixed").at(b + 1))
                    pe.wait_ge(sig("sigmoids").sem, sig("sigmoids").at(b - 1))
                    pe.matmul(r_ps[:, b % 2, :], mats("Fr"), xm[:, cols], start=True, stop=True).then_inc(sig("angle_product").sem, 1)
                    for g in range(G):
                        n = b * G + g
                        pe.wait_ge(sig("silu_up").sem, sig("silu_up").at(n - 1))
                        pe.matmul(h_ps[:, n % 2, :], mats("Fk", g), xm[:, cols], start=True, stop=True).then_inc(sig("hidden_product").sem, 1)
                        if n >= 2:
                            down(n - 2)
                down(B * G - 2)
                down(B * G - 1)

            @block.scalar
            def _(act):
                for b in range(B):
                    act.wait_ge(sig("angle_product").sem, sig("angle_product").at(b + 1))
                    act.activation(gate[:, b * S:(b + 1) * S], r_ps[:, b % 2, :], ACT.Sigmoid).then_inc(sig("sigmoids").sem, 1)
                    for g in range(G):
                        n = b * G + g
                        act.wait_ge(sig("hidden_product").sem, sig("hidden_product").at(n + 1))
                        act.wait_ge(sig("silu_up").sem, sig("silu_up").at(n - G + 1))
                        act.activation(relu[:, g, :], h_ps[:, n % 2, :], ACT.Relu).then_inc(sig("gelus").sem, 1)

            @block.vector
            def _(dve):
                chain = Chain(dve, sig("dve_step"))
                mix_coefficients(chain, dve, coef, vec("ffn_time_mix"), vec("ffn_combined_mix"), vec("first_half"), vec("second_half"))
                with dve.Fori(0, B) as b:
                    mixed(dve, sig, xm, x, coef, b)
                for b in range(B):
                    cols = slice(b * S, (b + 1) * S)
                    dve.tensor_tensor(k.X[:, cols], k.X[:, cols], x[:, cols], ALU.add).then_inc(sig("normed").sem, 1)
                    for g in range(G):
                        n = b * G + g
                        dve.wait_ge(sig("gelus").sem, sig("gelus").at(n + 1))
                        dve.wait_ge(sig("mlp_out").sem, sig("mlp_out").at(b))
                        dve.tensor_tensor(hidden[:, g, :], relu[:, g, :], h_ps[:, n % 2, :], ALU.mult).then_inc(sig("silu_up").sem, 1)
                    dve.wait_ge(sig("mlp_out").sem, sig("mlp_out").at(b + 1))
                    chain.link(dve.tensor_tensor(gate[:, cols], gate[:, cols], o_ps[:, b % 2, :], ALU.mult))
                    dve.wait_ge(sig("normed").sem, sig("normed").at(b + 1))
                    dve.tensor_tensor(k.X[:, cols], k.X[:, cols], gate[:, cols], ALU.add).then_inc(sig("residual").sem, 1)
                sig("dve_step").advance(chain.n)
        for name, n in (("mixed", B), ("mix_step", 2 * B), ("angle_product", B), ("hidden_product", B * G), ("silu_up", B * G), ("gelus", B * G),
                        ("mlp_out", B), ("sigmoids", B), ("normed", B), ("residual", B)):
            sig(name).advance(n)


MATS = {
    "kept": ["centring", "ident", "rotation", "Wq", "Wk", "Wv"],
    "first": ["W_mag", "W_q", *[f"W1.{n}" for n in range(8)], "W2.0", "W2.1"],
    "levels": [*[f"in.{l}.{w}" for l in range(LEVELS) for w in range(3)], *[f"out.{l}" for l in range(LEVELS)], *[f"up.{l}" for l in range(LEVELS - 1)]],
    "mixing": ["rk", "rv", "rr", "ro", *[f"Fk.{g}" for g in range(4)], *[f"Fv.{g}" for g in range(4)], "Fr"],
}
VECS = ["phases", "b_mag", "b_q", "b1.0", "b1.1", "b2", *[f"ln_g.{f}" for f in range(4)], *[f"ln_b.{f}" for f in range(4)],
        "bq", "bk", "bv", *[f"in_b.{l}.{w}" for l in range(LEVELS) for w in range(3)], *[f"out_b.{l}" for l in range(LEVELS)],
        *[f"up_b.{l}" for l in range(LEVELS - 1)], "ln1_g", "ln1_b", "ln2_g", "ln2_b", "att_time_mix", "att_combined_mix",
        "time_decay", "time_first", "ffn_time_mix", "ffn_combined_mix", "first_half", "second_half"]


def build(nc, args):
    with ExitStack() as stack:
        k = Kernel(nc, args, stack)
        open_signals(k)
        sig = k.count_of
        k.X = k.sb("X", [P, NT])
        xn = k.sb("xn", [P, NT])
        vecs = k.sb("vecs", [P, len(VECS)])
        mats = {"kept": k.sb("mats", [P, len(MATS["kept"]), P])}
        k.mean_of = k.sb("mean_of", [P, P])
        k.mean_of_4 = k.sb("mean_of_4", [P, P])
        k.ident_bf = k.sb("ident_bf", [P, P], BF16)
        k.head_rows = k.sb("head_rows", [P, P])
        k.eps, k.tiny, k.half_pi = (k.sb(n, [P, 1]) for n in ("eps", "tiny", "half_pi"))
        gates = k.sb("gates", [P, EXPERTS0 + EXPERTS1])

        def mat(name):
            group = next(g for g, names in MATS.items() if name in names)
            return mats[group][:, MATS[group].index(name), :]

        def load_mats(group, st):
            mats[group] = k.sb(f"mats_{group}", [P, len(MATS[group]), P], stack=st)

            def load(sp):
                arrived = sig("mats_in")
                sp.dma_start(mats[group][:, :, :], args["mats_" + group]).then_inc(arrived.sem, 16)
                sp.wait_ge(arrived.sem, arrived.at(1))
                arrived.advance(1)
            return {"sync": load}

        def vec(name):
            at = VECS.index(name)
            return vecs[:, at:at + 1]

        k.centring, k.ident = mat("centring"), mat("ident")
        with nc.Block() as block:

            @block.sync
            def _(sp):
                loads = [(k.X[:, :], args["x"]), (vecs[:, :], args["vecs"]), (mats["kept"][:, :, :], args["mats_kept"]), (k.head_rows[:, :], args["head_rows"]),
                         (gates[:, :], args["gates"]), (k.ident_bf[:, :], args["ident_bf"].bitcast(BF16))]
                for to, of in loads:
                    sp.dma_start(to, of).then_inc(sig("inputs_in").sem, 16)
                sp.wait_ge(sig("inputs_in").sem, sig("inputs_in").at(len(loads)))
                sig("inputs_in").advance(len(loads))

            @block.vector
            def _(dve):
                for to, value in ((k.mean_of, 1 / P), (k.mean_of_4, 1 / (4 * P)), (k.eps, EPS), (k.tiny, 1e-8), (k.half_pi, float(np.pi / 2))):
                    dve.memset(to[:, :], value)

        def layer_weights(st, tiles):
            hi = k.sb("w_hi", [P, tiles * 3 * P], F32R, stack=st)
            lo = k.sb("w_lo", [P, tiles * 3 * P], F32R, stack=st)
            rows = k.sb("rows", [P, tiles, P], BF16, stack=st)
            return hi, lo, rows

        def loader(st, w, tiles, name, alone=False):
            hi, lo, rows = w
            k.raw_weights = k.sb("raw_weights", [P, RAW, 2 * 3 * P], stack=st)
            also, done = expert_loader(k, args[name], tiles, hi, lo, alone)

            def loads(sp):
                sp.dma_start(rows[:, :, :], args[name + "_rows"].bitcast(BF16)).then_inc(sig("consts_in").sem, 16)
                also["sync"](sp)
                sp.wait_ge(sig("consts_in").sem, sig("consts_in").at(1))
                sig("consts_in").advance(1)
            return {**also, "sync": loads}, done

        def mlp(w, tiles, experts, top, gate, softmax):
            hi, lo, rows = w
            with ExitStack() as st:
                room = ExitStack()
                logits = k.ps("logits", [P, TILES, experts], stack=room)
                layernorm(k, k.X, xn, routing=(logits, gate))
                x_hi = k.sb("x_hi", [P, NT], F32R, stack=st)
                x_lo = k.sb("x_lo", [P, NT], F32R, stack=st)
                k.route_rows = k.sb("route_rows", [P, NT], BF16, stack=st)
                routed_mlp(k, xn, logits, room, x_hi, x_lo, hi, lo, tiles, experts, top, rows, softmax)

        def table_in(to, of):
            def load(sp):
                arrived = sig("consts_in")
                sp.dma_start(to, of).then_inc(arrived.sem, 16)
                sp.wait_ge(arrived.sem, arrived.at(1))
                arrived.advance(1)
            return load

        with ExitStack() as st:
            w = layer_weights(st, TILES0)
            gate = gates[:, 0:EXPERTS0]
            with ExitStack() as st2:
                positions = k.sb("positions", [P, S], stack=st2)
                load_first = load_mats("first", st2)["sync"]
                load_positions = table_in(positions[:, :], args["positions"])

                def loads(sp):
                    load_first(sp)
                    load_positions(sp)

                layernorm(k, k.X, xn, also={"sync": loads})
                also, done = loader(st2, w, TILES0, "mlp0", alone=True)
                phase_memory(k, xn, lambda n, i=None: mat(n if i is None else f"{n}.{i}"), lambda n, i=None: vec(n if i is None else f"{n}.{i}"), positions[:, :], also)
                done()
            mlp(w, TILES0, EXPERTS0, TOP0, gate, False)
            with ExitStack() as st2:
                turns = k.sb("turns", [P, 2, S], stack=st2)
                layernorm(k, k.X, xn, also={"sync": table_in(turns[:, :, :], args["rope"])})
                attention(k, xn, xn, S, B, S, lambda i: mat(("Wq", "Wk", "Wv")[i]), lambda i: vec(("bq", "bk", "bv")[i]),
                          rope=(mat("rotation"), turns[:, 0, :], turns[:, 1, :]), residual=True)
            mlp(w, TILES0, EXPERTS0, TOP0, gate, False)
        with ExitStack() as st:
            layernorm(k, k.X, xn, also=load_mats("levels", st))
            contexts = [xn, *[k.sb(f"context{l}", [P, NT >> l], stack=st) for l in range(1, LEVELS)]]
            with ExitStack() as st2:
                coarse = {l: k.sb(f"coarse{l}", [P, NT >> l], stack=st2) for l in range(1, LEVELS)}
                sampled(k, xn[:, :], {l: c[:, :] for l, c in coarse.items()})
                for l in range(LEVELS):
                    seq = S >> l
                    chunk = min(CH, B * seq)
                    attention(k, coarse[l] if l else xn, contexts[l], seq, B * seq // chunk, chunk,
                              lambda i, l=l: mat(f"in.{l}.{i}"), lambda i, l=l: vec(f"in_b.{l}.{i}"))
            w = layer_weights(st, TILES1)
            also, done = loader(st, w, TILES1, "mlp1")
            at = VECS.index("out_b.0")
            combine_levels(k, contexts, lambda l: mat(f"out.{l}"), lambda l: mat(f"up.{l}"), vecs[:, at:at + LEVELS], vecs[:, at + LEVELS:at + 2 * LEVELS - 1], also)
            done()
            gate = gates[:, EXPERTS0:]
            mlp(w, TILES1, EXPERTS1, TOP1, gate, True)
            with ExitStack() as st2:
                layernorm(k, k.X, xn, also=load_mats("mixing", st2))
                x1 = k.sb("x1", [P, NT], stack=st2)
                layernorm(k, xn, x1, gain=vec("ln1_g"), shift=vec("ln1_b"))
                names = {"Wk": "rk", "Wv": "rv", "Wr": "rr", "Wo": "ro"}
                time_mix(k, x1, xn, lambda n: mat(names[n]), vec)
                layernorm(k, xn, x1, gain=vec("ln2_g"), shift=vec("ln2_b"))
                channel_mix(k, x1, lambda n, i=None: mat(n if i is None else f"{n}.{i}"), vec)
            mlp(w, TILES1, EXPERTS1, TOP1, gate, True)

        with nc.Block() as block:

            @block.sync
            def _(sp):
                sp.dma_start(args["out"], k.X[:, :]).then_inc(sig("out_stored").sem, 16)
                sp.wait_ge(sig("out_stored").sem, sig("out_stored").at(1))


BF16_ONE = np.uint16(0x3F80)


def shape_constants():
    rotation = np.zeros((P, P), np.float32)
    for i in range(0, P, 2):
        rotation[i + 1, i] = -1.0
        rotation[i, i + 1] = 1.0
    inv = np.power(np.float32(10000.0), -2.0 * np.arange(HD // 2, dtype=np.float32) / HD).astype(np.float32)
    ang = np.arange(S, dtype=np.float32)[:, None] * inv[None, :]
    table = [np.tile(np.repeat(f(ang), 2, axis=-1).T, (HEADS, 1)) for f in (np.cos, np.sin)]
    head_rows = np.zeros((P, P), np.float32)
    for h in range(HEADS):
        head_rows[32 * (h // GROUP) + h % GROUP, h * HD:(h + 1) * HD] = 1.0

    def rows(tiles, hidden, experts):
        out = np.zeros((P, tiles * P), np.uint16)
        for m in range(tiles * P):
            e = m // hidden
            out[[e, 32 + e, 64 + e] if e < experts else [96], m] = BF16_ONE
        return out.reshape(P, tiles, P)

    return {
        "centring": np.eye(P, dtype=np.float32) - np.float32(1 / P), "ident": np.eye(P, dtype=np.float32), "rotation": rotation,
        "first_half": (np.arange(P) < P // 2).astype(np.float32), "second_half": (np.arange(P) >= P // 2).astype(np.float32),
        "positions": np.tile(np.arange(S, dtype=np.float32), (P, 1)), "rope": np.stack(table, axis=1).astype(np.float32),
        "head_rows": head_rows, "ident_bf": np.eye(P, dtype=np.uint16) * BF16_ONE,
        "mlp0_rows": rows(TILES0, HIDDEN0, EXPERTS0), "mlp1_rows": rows(TILES1, HIDDEN1, EXPERTS1),
    }


def laid_out(inputs):
    d = {n: np.asarray(a) for n, a in inputs.items()}
    const = shape_constants()
    a, b = "L0_attn_a_", "L0_attn_b_"
    m, v = {n: const[n] for n in ("centring", "ident", "rotation")}, {n: const[n] for n in ("first_half", "second_half")}
    m["W_mag"], m["W_q"] = d[a + "W_mag"].T, d[a + "W_q"].T
    for f in range(4):
        for g in range(2):
            m[f"W1.{f * 2 + g}"] = d[a + "W1"][g * P:(g + 1) * P, f * P:(f + 1) * P].T
    for g in range(2):
        m[f"W2.{g}"] = d[a + "W2"][:, g * P:(g + 1) * P].T
        v[f"b1.{g}"] = d[a + "b1"][g * P:(g + 1) * P]
    v["phases"], v["b_mag"], v["b_q"], v["b2"] = d[a + "random_phases"], d[a + "b_mag"], d[a + "b_q"], d[a + "b2"]
    for f in range(4):
        v[f"ln_g.{f}"], v[f"ln_b.{f}"] = d[a + "ln_g"][f * P:(f + 1) * P], d[a + "ln_b"][f * P:(f + 1) * P]
    for w in "qkv":
        m["W" + w], v["b" + w] = d[b + "W" + w], d[b + "b" + w]
    c = "L1_attn_a_"
    for l in range(LEVELS):
        for w in range(3):
            m[f"in.{l}.{w}"] = d[c + "in_proj_w"][l, w * P:(w + 1) * P].T
            v[f"in_b.{l}.{w}"] = d[c + "in_proj_b"][l, w * P:(w + 1) * P]
        m[f"out.{l}"], v[f"out_b.{l}"] = d[c + "out_w"][l].T, d[c + "out_b"][l]
        if l < LEVELS - 1:
            m[f"up.{l}"], v[f"up_b.{l}"] = d[c + "up_w"][l].T, d[c + "up_b"][l]
    r = "L1_attn_b_"
    for n, w in (("rk", "Wk"), ("rv", "Wv"), ("rr", "Wr"), ("ro", "Wo"), ("Fr", "Fr")):
        m[n] = d[r + w].T
    for g in range(4):
        m[f"Fk.{g}"], m[f"Fv.{g}"] = d[r + "Fk"][g * P:(g + 1) * P].T, d[r + "Fv"][:, g * P:(g + 1) * P].T
    for n in ("ln1_g", "ln1_b", "ln2_g", "ln2_b", "att_time_mix", "att_combined_mix", "time_decay", "time_first", "ffn_time_mix", "ffn_combined_mix"):
        v[n] = d[r + n].reshape(P)

    def mlp(gate, up, down):
        n = gate.shape[1] // P
        parts = gate.reshape(P, n, P), up.reshape(P, n, P), down.reshape(n, P, P).transpose(1, 0, 2)
        return np.stack(parts, axis=2).reshape(P, n * 3 * P)

    f0, f1 = "L0_ffn_", "L1_ffn_"
    mlp0 = mlp(np.concatenate([d[f0 + "exp_wg"].transpose(1, 0, 2).reshape(P, -1), d[f0 + "shared_wg"]], 1),
               np.concatenate([d[f0 + "exp_wu"].transpose(1, 0, 2).reshape(P, -1), d[f0 + "shared_wu"]], 1),
               np.concatenate([d[f0 + "exp_wd"].reshape(-1, P), d[f0 + "shared_wd"]], 0))
    mlp1 = mlp(d[f1 + "w1"].reshape(-1, P).T, d[f1 + "w3"].reshape(-1, P).T, d[f1 + "w2"].transpose(0, 2, 1).reshape(-1, P))
    arrays = {"x": d[a + "x"].reshape(NT, P).T, "vecs": np.stack([v[n] for n in VECS], axis=1), **{"mats_" + g: np.stack([m[n] for n in names], axis=1) for g, names in MATS.items()},
              "gates": np.concatenate([d[f0 + "gate_w"].T, d[f1 + "gate_w"].T], axis=1), "mlp0": mlp0, "mlp1": mlp1,
              **{n: const[n] for n in ("positions", "rope", "head_rows", "ident_bf", "mlp0_rows", "mlp1_rows")}}
    return {n: np.ascontiguousarray(x) for n, x in arrays.items()}


def kernel(**inputs):
    import concourse.bacc as bacc
    from concourse.bass_utils import run_bass_kernel_spmd

    nc = bacc.Bacc("TRN2", target_bir_lowering=False, num_devices=1)
    arrays = {f"in_{n}": x for n, x in laid_out(inputs).items()}
    args = {n[3:]: nc.dram_tensor(n, x.shape, mybir.dt.from_np(x.dtype), kind="ExternalInput").ap() for n, x in arrays.items()}
    args["out"] = nc.dram_tensor("out_x", (P, NT), F32, kind="ExternalOutput").ap()
    build(nc, args)
    result = run_bass_kernel_spmd(nc, [arrays], core_ids=[0]).results[0]["out_x"]
    return np.ascontiguousarray(result.T).reshape(B, S, P)
```

```python
from contextlib import ExitStack

import numpy as np

import concourse.bass as bass
from concourse import mybir

F32 = mybir.dt.float32
F32R = mybir.dt.float32r
BF16 = mybir.dt.bfloat16
ACT = mybir.ActivationFunctionType
ALU = mybir.AluOpType
AX = mybir.AxisListType

P = 128
B = 4
S = 512
NT = B * S
CH = 512
NC = NT // CH
TILES = NT // P
HEADS = 16
HD = P // HEADS
EPS = 1e-5
HIDDEN0, EXPERTS0, TOP0, SHARED0 = 128, 16, 4, 256
HIDDEN1, EXPERTS1, TOP1 = 352, 8, 2
TILES0 = (HIDDEN0 * EXPERTS0 + SHARED0) // P
TILES1 = HIDDEN1 * EXPERTS1 // P
SCALE0 = 2.5
CREDIT = 32
LEVELS = 4


class Signal:

    def __init__(self, sem, step=1):
        self.sem, self.step, self.base = sem, step, CREDIT * step

    def at(self, n):
        return n * self.step + self.base

    def advance(self, n):
        self.base += n * self.step


class Chain:

    def __init__(self, eng, signal, it=0, per=0):
        self.eng, self.own, self.first, self.n = eng, signal, it * per, 0

    def link(self, ins):
        self.n += 1
        ins.then_inc(self.own.sem, 1)
        self.eng.wait_ge(self.own.sem, self.own.at(self.first + self.n))


class Kernel:

    def __init__(self, nc, args, stack):
        self.nc, self.args, self.stack = nc, args, stack
        self.counts = {}
        self.names = 0

    def sb(self, name, shape, dt=F32, stack=None):
        self.names += 1
        return (stack or self.stack).enter_context(self.nc.sbuf_tensor(f"{name}_{self.names}", shape, dt))

    def ps(self, name, shape, dt=F32, stack=None):
        self.names += 1
        return (stack or self.stack).enter_context(self.nc.psum_tensor(f"{name}_{self.names}", shape, dt))

    def scratch(self, name, shape):
        self.names += 1
        return self.nc.dram_tensor(f"{name}_{self.names}", shape, BF16).ap()

    def count_of(self, name):
        return self.counts[name]


SIGNALS = {
    "tensor": ["centred", "variance", "weights_turned", "gate_up", "routed_rows", "mlp_out", "magnitude_product", "angle_product", "context_mean", "hidden_product", "projection", "rotation", "values_turned", "peak_scores", "peaks_turned", "scores", "context_sums", "sums_spread", "level_product"],
    "scalar": ["squared", "weights_high", "logs", "rstd", "x_high", "gate_probs", "silu", "h_hi", "sines", "sigmoids", "gelus", "projected", "values_copied", "peak_rows", "probs", "context_low", "sums_kept", "level_kept"],
    "vector": ["dve_step", "weights_low_odd", "normed", "routed", "weighted", "residual", "silu_up", "angles", "angle_reduced", "magnitudes", "magnitude_sum", "memories", "context_centred", "context_normed", "rotated", "values_kept", "parts_made", "biased_used", "peak_found", "peaks_split", "upsampled", "mix_step", "mixed", "key_clamped", "averaged", "probs_low", "context_kept"],
    "gpsimd": ["pool_step", "weights_rounded", "weights_low_even", "h_lo", "probs_low_pool", "weighted_waves", "values_spread", "key_values", "gated"],
    "dma": ["inputs_in", "weights_in_0", "weights_in_1", "weights_in_2", "weights_in_3", "weights_in_4", "weights_in_5", "weights_in_6", "weights_in_7", "first_parts_stored", "consts_in", "mats_in", "out_stored", "parts_stored", "stack_in_0", "stack_in_1", "stack_in_2", "stack_in_3", "peaks_out", "peaks_in"],
}


def open_signals(k):
    for owner, names in SIGNALS.items():
        for name in names:
            k.counts[name] = Signal(k.stack.enter_context(k.nc.semaphore(name)), 16 if owner == "dma" else 1)
    with k.nc.Block() as block:
        def opened(owner):
            def program(eng):
                for name in SIGNALS[owner]:
                    eng.sem_inc(k.counts[name].sem, k.counts[name].base)
            return program

        block.tensor(opened("tensor"))
        block.scalar(opened("scalar"))
        block.vector(opened("vector"))
        block.gpsimd(opened("gpsimd"))
        block.sync(opened("dma"))


def layernorm(k, src, dst, gain=None, shift=None, also=None, routing=None, sigmoid_next=False):
    nc = k.nc
    centred, variance, squared, logs, rstd = (k.count_of(n) for n in ("centred", "variance", "squared", "logs", "rstd"))
    normed, step = k.count_of("normed"), k.count_of("dve_step")
    with ExitStack() as st:
        xc = k.ps("xc", [P, NC, CH], stack=st)
        var = k.ps("var", [P, NC - 1, CH], stack=st)
        sq = k.sb("sq", [P, NC, CH], stack=st)
        rs = k.sb("rs", [P, NC, CH], stack=st)
        with nc.Block() as block:

            @block.tensor
            def _(pe):
                for c in range(NC):
                    pe.matmul(xc[:, c, :], k.centring, src[:, c * CH:(c + 1) * CH], start=True, stop=True).then_inc(centred.sem, 1)
                for c in range(NC):
                    pe.wait_ge(squared.sem, squared.at(c + 1))
                    if c == NC - 1:
                        pe.wait_ge(logs.sem, logs.at(1))
                    pe.matmul(var[:, c % (NC - 1), :], k.mean_of[:, :], sq[:, c, :], start=True, stop=True).then_inc(variance.sem, 1)
                for t in range(TILES if routing else 0):
                    pe.wait_ge(normed.sem, normed.at(t * P // CH + 1))
                    pe.matmul(routing[0][:, t, :], dst[:, t * P:(t + 1) * P], routing[1], start=(t == 0), stop=True, skip_group_check=True)

            @block.scalar
            def _(act):
                act.preload_act_table(ACT.Ln)
                for c in range(NC):
                    act.wait_ge(centred.sem, centred.at(c + 1))
                    act.activation(sq[:, c, :], xc[:, c, :], ACT.Square).then_inc(squared.sem, 1)
                for c in range(NC):
                    act.wait_ge(variance.sem, variance.at(c + 1))
                    act.activation(rs[:, c, :], var[:, c % (NC - 1), :], ACT.Ln, bias=k.eps[:, 0:1]).then_inc(logs.sem, 1)
                for c in range(NC):
                    act.wait_ge(logs.sem, logs.at(c + 1))
                    act.activation(rs[:, c, :], rs[:, c, :], ACT.Exp, scale=-0.5).then_inc(rstd.sem, 1)
                if sigmoid_next:
                    act.preload_act_table(ACT.Sigmoid)
                if also and "scalar" in also:
                    also["scalar"](act)

            @block.vector
            def _(dve):
                for c in range(NC):
                    cols = slice(c * CH, (c + 1) * CH)
                    dve.wait_ge(rstd.sem, rstd.at(c + 1))
                    dve.tensor_tensor(dst[:, cols], xc[:, c, :], rs[:, c, :], ALU.mult).then_inc(normed.sem, 1)
                for c in range(NC if gain is not None else 0):
                    cols = slice(c * CH, (c + 1) * CH)
                    dve.wait_ge(normed.sem, normed.at(c + 1))
                    dve.tensor_scalar(dst[:, cols], dst[:, cols], gain, shift, ALU.mult, ALU.add).then_inc(step.sem, 1)
                if also and "vector" in also:
                    also["vector"](dve)

            if also and "gpsimd" in also:
                block.gpsimd(also["gpsimd"])
            if also:
                block.sync(also["sync"])
        for s, n in ((centred, NC), (variance, NC), (squared, NC), (logs, NC), (rstd, NC), (normed, NC),
                     (step, NC if gain is not None else 0)):
            s.advance(n)


RAW, RAW_ALONE = 8, 4


def expert_loader(k, weights, tiles, hi, lo, alone=False):
    buffers = RAW_ALONE if alone else RAW
    weights_in = [k.count_of(f"weights_in_{n}") for n in range(buffers)]
    high, own_high = k.count_of("weights_high"), k.count_of("weights_rounded")
    low = k.count_of("weights_low_even"), k.count_of("weights_low_odd")
    raw = k.raw_weights
    width = 2 * 3 * P
    pieces = tiles // 2

    def part(n):
        return slice(n * width, (n + 1) * width)

    def round_high(act):
        for n in range(pieces):
            arrived = weights_in[n % buffers]
            act.wait_ge(arrived.sem, arrived.at(n // buffers + 1))
            act.activation(hi[:, part(n)], raw[:, n % buffers, :], ACT.Copy).then_inc(high.sem, 1)

    def rest_of(which):
        def program(eng):
            for n in range(which, pieces, 2):
                eng.wait_ge(high.sem, high.at(n + 1))
                eng.tensor_tensor(lo[:, part(n)], raw[:, n % buffers, :], hi[:, part(n)].bitcast(F32), ALU.subtract).then_inc(low[which].sem, 1)
        return program

    def both_parts(pool):
        for n in range(pieces):
            arrived = weights_in[n % buffers]
            pool.wait_ge(arrived.sem, arrived.at(n // buffers + 1))
            pool.tensor_copy(hi[:, part(n)], raw[:, n % buffers, :]).then_inc(own_high.sem, 1)
            pool.wait_ge(own_high.sem, own_high.at(n + 1))
            pool.tensor_tensor(lo[:, part(n)], raw[:, n % buffers, :], hi[:, part(n)].bitcast(F32), ALU.subtract).then_inc(low[0].sem, 1)

    def load(sp):
        for n in range(pieces):
            if n >= buffers:
                used, count = (low[0], n - buffers + 1) if alone else (low[n % 2], (n - buffers) // 2 + 1)
                sp.wait_ge(used.sem, used.at(count))
            sp.dma_start(raw[:, n % buffers, :], weights[:, part(n)]).then_inc(weights_in[n % buffers].sem, 16)

    def done():
        for n in range(buffers):
            weights_in[n].advance(len(range(n, pieces, buffers)))
        (own_high if alone else high).advance(pieces)
        low[0].advance(pieces if alone else len(range(0, pieces, 2)))
        low[1].advance(0 if alone else len(range(1, pieces, 2)))

    if alone:
        return {"gpsimd": both_parts, "sync": load}, done
    return {"scalar": round_high, "gpsimd": rest_of(0), "vector": rest_of(1), "sync": load}, done


def routed_mlp(k, x, logits, room, hi, lo, w_hi, w_lo, tiles, experts, top, rows, softmax):
    nc = k.nc
    turned, gate_up = k.count_of("weights_turned"), k.count_of("gate_up")
    rowsig, out_sum = k.count_of("routed_rows"), k.count_of("mlp_out")
    probs_ready, routed, step = k.count_of("gate_probs"), k.count_of("routed"), k.count_of("dve_step")
    x_high = k.count_of("x_high")
    silu, h_hi, h_lo, weighted, silu_up, residual = (k.count_of(n) for n in ("silu", "h_hi", "h_lo", "weighted", "silu_up", "residual"))

    wide = k.route_rows
    with ExitStack() as st:
        rowsT = k.ps("rowsT", [P, TILES, P], BF16, stack=st)
        sc = k.sb("sc", [P, TILES, experts], stack=st)
        rest = k.sb("rest", [P, TILES, experts], stack=st)
        best = k.sb("best", [P, TILES, 8], stack=st)
        peak = k.sb("peak", [P, TILES], stack=st)
        total = k.sb("total", [P, TILES], stack=st)
        wts = k.sb("wts", [P, TILES, experts], stack=st)
        split = k.sb("split", [P, TILES, P], BF16, stack=st)
        with nc.Block() as block:

            @block.tensor
            def _(pe):
                pe.wait_ge(routed.sem, routed.at(1))
                for t in range(TILES):
                    last = pe.transpose(rowsT[:, t, :], split[:, t, :], k.ident_bf[:, :])
                    if t % 8 == 7:
                        last.then_inc(turned.sem, 1)

            @block.scalar
            def _(act):
                if softmax:
                    act.wait_ge(k.count_of("silu_up").sem, k.count_of("silu_up").at(1))
                    act.activation(sc[:, :, :], rest[:, :, :], ACT.Exp).then_inc(probs_ready.sem, 1)
                else:
                    act.activation(sc[:, :, :], logits[:, :, :], ACT.Sigmoid).then_inc(probs_ready.sem, 1)
                for c in range(NC):
                    cols = slice(c * CH, (c + 1) * CH)
                    act.activation(hi[:, cols], x[:, cols], ACT.Copy).then_inc(x_high.sem, 1)
                for n in range(2):
                    act.wait_ge(turned.sem, turned.at(n + 1))
                    act.activation(wide[:, n * 8 * P:(n + 1) * 8 * P].rearrange("p (t n) -> p t n", n=P),
                                   rowsT[:, n * 8:(n + 1) * 8, :], ACT.Copy)

            @block.vector
            def _(dve):
                chain = Chain(dve, step)
                zeros = k.count_of("pool_step")

                def over(a):
                    return a[:, :].unsqueeze(2).to_broadcast([P, TILES, experts])

                if softmax:
                    chain.link(dve.tensor_reduce(peak[:, :], logits[:, :, :], AX.X, ALU.max))
                    dve.tensor_tensor(rest[:, :, :], logits[:, :, :], over(peak), ALU.subtract).then_inc(silu_up.sem, 1)
                    dve.wait_ge(probs_ready.sem, probs_ready.at(1))
                    chain.link(dve.tensor_reduce(total[:, :], sc[:, :, :], AX.X, ALU.add))
                    chain.link(dve.reciprocal(total[:, :], total[:, :]))
                    chain.link(dve.tensor_tensor(sc[:, :, :], sc[:, :, :], over(total), ALU.mult))
                dve.wait_ge(probs_ready.sem, probs_ready.at(1))
                for t in range(TILES):
                    last = dve.max(best[:, t, :], sc[:, t, :])
                chain.link(last)
                chain.link(dve.memset(best[:, :, top:8], -2.0))
                for t in range(TILES):
                    last = dve.match_replace(rest[:, t, :], best[:, t, :], sc[:, t, :], -1.0)
                chain.link(last)
                chain.link(dve.scalar_tensor_tensor(out=wts[:, :, :], in0=rest[:, :, :], scalar=0.0, in1=sc[:, :, :], op0=ALU.max, op1=ALU.subtract))
                chain.link(dve.tensor_reduce(total[:, :], wts[:, :, :], AX.X, ALU.add))
                if softmax:
                    chain.link(dve.reciprocal(total[:, :], total[:, :]))
                    chain.link(dve.tensor_tensor(wts[:, :, :], wts[:, :, :], over(total), ALU.mult))
                else:
                    chain.link(dve.tensor_scalar(total[:, :], total[:, :], -1e-20, None, ALU.add))
                    chain.link(dve.reciprocal(total[:, :], total[:, :]))
                    chain.link(dve.tensor_tensor(wts[:, :, :], wts[:, :, :], over(total), ALU.mult))
                    chain.link(dve.tensor_scalar(wts[:, :, :], wts[:, :, :], SCALE0, None, ALU.mult))
                dve.wait_ge(zeros.sem, zeros.at(2))
                chain.link(dve.tensor_copy(split[:, :, 0:experts], wts[:, :, :]))
                chain.link(dve.tensor_tensor(wts[:, :, :], wts[:, :, :], split[:, :, 0:experts], ALU.subtract))
                chain.link(dve.tensor_copy(split[:, :, 32:32 + experts], wts[:, :, :]))
                dve.tensor_tensor(split[:, :, 64:64 + experts], wts[:, :, :], split[:, :, 32:32 + experts], ALU.subtract).then_inc(routed.sem, 1)
                step.advance(chain.n)
            @block.gpsimd
            def _(pool):
                zeros = k.count_of("pool_step")
                pool.memset(split[:, :, :], 0.0).then_inc(zeros.sem, 1)
                pool.wait_ge(zeros.sem, zeros.at(1))
                pool.memset(split[:, :, 96:97], 1.0).then_inc(zeros.sem, 1)
                for c in range(NC):
                    cols = slice(c * CH, (c + 1) * CH)
                    pool.wait_ge(x_high.sem, x_high.at(c + 1))
                    pool.tensor_tensor(lo[:, cols], x[:, cols], hi[:, cols].bitcast(F32), ALU.subtract)
        k.count_of("pool_step").advance(2)
        for s, n in ((x_high, NC), (turned, 2), (probs_ready, 1), (routed, 1), (silu_up, 1 if softmax else 0)):
            s.advance(n)
    room.close()

    LAG, RING, PAIR = 3, 4, 2
    assert PAIR * tiles % RING == 0 and tiles % 2 == 0 and LAG < RING
    with ExitStack() as st:
        g_ps = k.ps("g_ps", [P, 2, CH], stack=st)
        u_ps = k.ps("u_ps", [P, 2, CH], stack=st)
        r_ps = k.ps("r_ps", [P, 2, CH], stack=st)
        o_ps = k.ps("o_ps", [P, PAIR, CH], stack=st)
        sg = k.sb("sg", [P, RING, CH], stack=st)
        hw = k.sb("hw", [P, RING, CH], stack=st)
        hh = k.sb("hh", [P, RING, CH], F32R, stack=st)
        hl = k.sb("hl", [P, RING, CH], F32R, stack=st)

        def weight(part, j, which):
            at = (j * 3 + which) * P
            return part[:, at:at + P]

        def number(i, half, j):
            m = half * tiles + j
            return i * (PAIR * tiles) + m, m % RING, m % 2

        with nc.Block() as block:

            @block.tensor
            def _(pe):
                def up(i, half, j):
                    n, _, bank = number(i, half, j)
                    cols = bass.ts(i * PAIR + half, CH)
                    pe.wait_ge(weighted.sem, weighted.at(n - 1))
                    for which, banks in ((0, g_ps), (1, u_ps)):
                        at = banks[:, bank, :]
                        pe.matmul(at, weight(w_hi, j, which), hi[:, cols], start=True, stop=False)
                        pe.matmul(at, weight(w_lo, j, which), hi[:, cols], start=False, stop=False)
                        last = pe.matmul(at, weight(w_hi, j, which), lo[:, cols], start=False, stop=True)
                        if which == 0:
                            last.then_inc(gate_up.sem, 1)
                    pe.matmul(r_ps[:, bank, :], rows[:, j, :], wide[:, cols], start=True, stop=True).then_inc(rowsig.sem, 1)

                def down(i, half, j):
                    n, slot, _ = number(i, half, j)
                    at = o_ps[:, half, :]
                    if j == 0:
                        pe.wait_ge(residual.sem, residual.at(i * PAIR + half - 1))
                    pe.wait_ge(h_hi.sem, h_hi.at(n + 1))
                    pe.matmul(at, weight(w_hi, j, 2), hh[:, slot, :], start=(j == 0), stop=False)
                    pe.matmul(at, weight(w_lo, j, 2), hh[:, slot, :], start=False, stop=False)
                    pe.wait_ge(h_lo.sem, h_lo.at(n + 1))
                    last = pe.matmul(at, weight(w_hi, j, 2), hl[:, slot, :], start=False, stop=(j == tiles - 1))
                    if j == tiles - 1:
                        last.then_inc(out_sum.sem, 1)

                def pair(i, more):
                    for half in range(PAIR):
                        for j in range(tiles):
                            down(i, half, j)
                            if j + LAG < tiles:
                                up(i, half, j + LAG)
                            elif half == 0:
                                up(i, 1, j + LAG - tiles)
                            elif more:
                                up(i + 1, 0, j + LAG - tiles)

                for j in range(LAG):
                    up(0, 0, j)
                with pe.Fori(0, NC // PAIR - 1) as i:
                    pair(i, True)
                pair(NC // PAIR - 1, False)

            def tiles_of(i):
                for half in range(PAIR):
                    for j in range(tiles):
                        yield half, j, *number(i, half, j)

            @block.scalar
            def _(act):
                def gates(n, slot, bank):
                    act.wait_ge(gate_up.sem, gate_up.at(n + 1))
                    act.activation(sg[:, slot, :], g_ps[:, bank, :], ACT.Silu).then_inc(silu.sem, 1)

                def high(n, slot):
                    act.wait_ge(weighted.sem, weighted.at(n + 1))
                    act.activation(hh[:, slot, :], hw[:, slot, :], ACT.Copy).then_inc(h_hi.sem, 1)

                def pair(i, more):
                    m = PAIR * tiles
                    for half, j, n, slot, bank in tiles_of(i):
                        if half * tiles + j + 1 < m or more:
                            gates(n + 1, (slot + 1) % RING, 1 - bank)
                        high(n, slot)

                gates(0, 0, 0)
                with act.Fori(0, NC // PAIR - 1) as i:
                    pair(i, True)
                pair(NC // PAIR - 1, False)

            @block.vector
            def _(dve):
                def add(chunk, bank):
                    cols = bass.ts(chunk, CH)
                    dve.wait_ge(out_sum.sem, out_sum.at(chunk + 1))
                    dve.tensor_tensor(k.X[:, cols], k.X[:, cols], o_ps[:, bank, :], ALU.add).then_inc(residual.sem, 1)

                def pair(i, after):
                    for half, j, n, slot, bank in tiles_of(i):
                        dve.wait_ge(silu.sem, silu.at(n + 1))
                        dve.wait_ge(rowsig.sem, rowsig.at(n + 1))
                        dve.tensor_tensor(hw[:, slot, :], sg[:, slot, :], u_ps[:, bank, :], ALU.mult).then_inc(silu_up.sem, 1)
                        dve.wait_ge(silu_up.sem, silu_up.at(n + 1))
                        dve.tensor_tensor(hw[:, slot, :], hw[:, slot, :], r_ps[:, bank, :], ALU.mult).then_inc(weighted.sem, 1)
                        if j == LAG and (half == 1 or after):
                            add(i * PAIR + half - 1, 1 - half)

                pair(0, False)
                with dve.Fori(0, NC // PAIR - 1) as i:
                    pair(i + 1, True)
                add(NC - 1, 1)

            @block.gpsimd
            def _(pool):
                with pool.Fori(0, NC // PAIR) as i:
                    for half, j, n, slot, bank in tiles_of(i):
                        pool.wait_ge(h_hi.sem, h_hi.at(n + 1))
                        pool.tensor_tensor(hl[:, slot, :], hw[:, slot, :], hh[:, slot, :].bitcast(F32), ALU.subtract).then_inc(h_lo.sem, 1)
        for s in (gate_up, rowsig, silu, silu_up, weighted, h_hi, h_lo):
            s.advance(NC * tiles)
        for s in (out_sum, residual):
            s.advance(NC)


TWO_PI = 2 * np.pi
TURN = (6.28125, float(np.float32(0.0019350051879882812)), float(TWO_PI - 6.28125 - 0.0019350051879882812))
ROUND = 1.5 * 2.0 ** 23
ALMOST_PI = 3.1415925


def turn_down(chain, dve, angle, turns):
    chain.link(dve.tensor_scalar(turns, angle, 1 / TWO_PI, ROUND, ALU.mult, ALU.add))
    chain.link(dve.tensor_scalar(turns, turns, ROUND, None, ALU.subtract))
    for part in TURN:
        chain.link(dve.scalar_tensor_tensor(out=angle, in0=turns, scalar=-part, in1=angle, op0=ALU.mult, op1=ALU.add))
    chain.link(dve.tensor_scalar(angle, angle, ALMOST_PI, -ALMOST_PI, ALU.min, ALU.max))


def phase_memory(k, x, mats, vec, positions, also):
    nc = k.nc
    sig = k.count_of
    with ExitStack() as st:
        phi = k.sb("phi", [P, S], stack=st)
        cos = k.sb("cos", [P, S], stack=st)
        sin = k.sb("sin", [P, S], stack=st)
        turns = k.sb("turns", [P, S], stack=st)
        ones = k.sb("ones_row", [P, S], stack=st)
        mem_r = k.sb("mem_r", [P, NT], stack=st)
        mem_i = k.sb("mem_i", [P, NT], stack=st)
        angle = k.sb("angle", [P, NT], stack=st)
        inv = k.sb("inv", [P, NT], stack=st)
        context = k.sb("context", [P, 4, NT], stack=st)

        with ExitStack() as st2:
            mag = k.sb("mag", [P, NT], stack=st2)
            wr = k.sb("wr", [P, NT], stack=st2)
            wi = k.sb("wi", [P, NT], stack=st2)
            wx = k.sb("wx", [P, NT], stack=st2)
            m_ps = k.ps("m_ps", [P, B, S], stack=st2)
            q_ps = k.ps("q_ps", [P, B, S], stack=st2)
            with nc.Block() as block:

                @block.tensor
                def _(pe):
                    with pe.Fori(0, B) as b:
                        cols = bass.ts(b, S)
                        pe.matmul(m_ps[:, b, :], mats("W_mag"), x[:, cols], start=True, stop=True).then_inc(sig("magnitude_product").sem, 1)
                        pe.matmul(q_ps[:, b, :], mats("W_q"), x[:, cols], start=True, stop=True).then_inc(sig("angle_product").sem, 1)

                @block.scalar
                def _(act):
                    act.wait_ge(sig("angle_reduced").sem, sig("angle_reduced").at(1))
                    act.activation(sin[:, :], phi[:, :], ACT.Sin).then_inc(sig("sines").sem, 1)
                    act.activation(cos[:, :], phi[:, :], ACT.Abs).then_inc(sig("sines").sem, 1)
                    act.wait_ge(sig("sines").sem, sig("sines").at(2))
                    act.activation(cos[:, :], cos[:, :], ACT.Sin, scale=-1.0, bias=k.half_pi[:, 0:1]).then_inc(sig("sines").sem, 1)
                    with act.Fori(0, B) as b:
                        act.wait_ge(sig("magnitude_product").sem, sig("magnitude_product").at(b + 1))
                        act.activation(mag[:, bass.ts(b, S)], m_ps[:, b, :], ACT.Sigmoid, bias=vec("b_mag")).then_inc(sig("sigmoids").sem, 1)
                    act.preload_act_table(ACT.Ln)
                    for b in range(B):
                        cols = bass.ts(b, S)
                        act.wait_ge(sig("magnitude_sum").sem, sig("magnitude_sum").at(b + 1))
                        act.activation(inv[:, cols], inv[:, cols], ACT.Ln, bias=k.tiny[:, 0:1]).then_inc(sig("logs").sem, 1)
                    for b in range(B):
                        cols = bass.ts(b, S)
                        act.wait_ge(sig("logs").sem, sig("logs").at(b + 1))
                        act.activation(inv[:, cols], inv[:, cols], ACT.Exp, scale=-0.5).then_inc(sig("rstd").sem, 1)

                @block.vector
                def _(dve):
                    chain = Chain(dve, sig("dve_step"))
                    chain.link(dve.memset(ones[:, :], 1.0))
                    chain.link(dve.tensor_scalar(phi[:, :], positions, vec("phases"), 0.01, ALU.mult, ALU.mult))
                    with dve.Fori(0, B) as b:
                        dve.wait_ge(sig("angle_product").sem, sig("angle_product").at(b + 1))
                        dve.scalar_tensor_tensor(out=angle[:, bass.ts(b, S)], in0=q_ps[:, b, :], scalar=vec("b_q"), in1=phi[:, :],
                                                 op0=ALU.add, op1=ALU.add).then_inc(sig("angles").sem, 1)
                    dve.wait_ge(sig("angles").sem, sig("angles").at(B))
                    turn_down(chain, dve, phi[:, :], turns[:, :])
                    dve.sem_inc(sig("angle_reduced").sem, 1)
                    sig("dve_step").advance(chain.n)
                    with dve.Fori(0, B) as b:
                        cols = bass.ts(b, S)
                        dve.wait_ge(sig("sigmoids").sem, sig("sigmoids").at(b + 1))
                        dve.tensor_scalar(mag[:, cols], mag[:, cols], 5.0, None, ALU.mult).then_inc(sig("magnitudes").sem, 1)
                        dve.wait_ge(sig("magnitudes").sem, sig("magnitudes").at(b + 1))
                        dve.tensor_tensor_scan(inv[:, cols], ones[:, :], mag[:, cols], 0.0, ALU.mult, ALU.add).then_inc(sig("magnitude_sum").sem, 1)
                        dve.wait_ge(sig("weighted_waves").sem, sig("weighted_waves").at(b * 2 + 1))
                        dve.tensor_tensor_scan(mem_r[:, cols], ones[:, :], wr[:, cols], 0.0, ALU.mult, ALU.add).then_inc(sig("memories").sem, 1)
                        dve.wait_ge(sig("weighted_waves").sem, sig("weighted_waves").at(b * 2 + 2))
                        dve.tensor_tensor_scan(mem_i[:, cols], ones[:, :], wi[:, cols], 0.0, ALU.mult, ALU.add).then_inc(sig("memories").sem, 1)
                    with dve.Fori(0, B) as b:
                        cols = bass.ts(b, S)
                        dve.wait_ge(sig("rstd").sem, sig("rstd").at(b + 1))
                        dve.wait_ge(sig("memories").sem, sig("memories").at(b * 2 + 2))
                        dve.tensor_tensor(mem_r[:, cols], mem_r[:, cols], inv[:, cols], ALU.mult)
                        dve.tensor_tensor(mem_i[:, cols], mem_i[:, cols], inv[:, cols], ALU.mult)

                @block.gpsimd
                def _(pool):
                    pool.wait_ge(sig("sines").sem, sig("sines").at(3))
                    with pool.Fori(0, B) as b:
                        cols = bass.ts(b, S)
                        pool.wait_ge(sig("magnitudes").sem, sig("magnitudes").at(b + 1))
                        pool.tensor_tensor(wx[:, cols], mag[:, cols], x[:, cols], ALU.mult).then_inc(sig("pool_step").sem, 1)
                        pool.wait_ge(sig("pool_step").sem, sig("pool_step").at(b + 1))
                        pool.tensor_tensor(wr[:, cols], wx[:, cols], cos[:, :], ALU.mult).then_inc(sig("weighted_waves").sem, 1)
                        pool.tensor_tensor(wi[:, cols], wx[:, cols], sin[:, :], ALU.mult).then_inc(sig("weighted_waves").sem, 1)
            for name, n in (("magnitude_product", B), ("angle_product", B), ("angle_reduced", 1), ("sines", 3), ("sigmoids", B), ("logs", B), ("rstd", B),
                            ("angles", B), ("magnitudes", B), ("magnitude_sum", B), ("memories", 2 * B), ("pool_step", B), ("weighted_waves", 2 * B)):
                sig(name).advance(n)

        with ExitStack() as st2:
            sq = k.sb("sq", [P, NT], stack=st2)
            cq = k.sb("cq", [P, NT], stack=st2)
            a = k.sb("a", [P, S], stack=st2)
            a2 = k.sb("a2", [P, S], stack=st2)
            steps = 6
            with nc.Block() as block:

                @block.vector
                def _(dve):
                    with dve.Fori(0, B) as b:
                        chain = Chain(dve, sig("dve_step"), b, steps)
                        turn_down(chain, dve, angle[:, bass.ts(b, S)], turns[:, :])
                        assert chain.n == steps
                        dve.sem_inc(sig("angle_reduced").sem, 1)
                    sig("dve_step").advance(B * steps)
                    steps2 = 3
                    with dve.Fori(0, B) as b:
                        cols = bass.ts(b, S)
                        chain = Chain(dve, sig("dve_step"), b, steps2)
                        dve.wait_ge(sig("sines").sem, sig("sines").at(b * 3 + 3))
                        chain.link(dve.tensor_tensor(a[:, :], mem_i[:, cols], sq[:, cols], ALU.mult))
                        chain.link(dve.tensor_tensor(context[:, 2, cols], mem_r[:, cols], cq[:, cols], ALU.mult))
                        chain.link(dve.tensor_tensor(context[:, 2, cols], context[:, 2, cols], a[:, :], ALU.add))
                        assert chain.n == steps2
                    sig("dve_step").advance(B * steps2)

                @block.scalar
                def _(act):
                    for b in range(B):
                        cols = bass.ts(b, S)
                        act.wait_ge(sig("angle_reduced").sem, sig("angle_reduced").at(b + 1))
                        act.activation(sq[:, cols], angle[:, cols], ACT.Sin).then_inc(sig("sines").sem, 1)
                        act.activation(cq[:, cols], angle[:, cols], ACT.Abs).then_inc(sig("sines").sem, 1)
                        act.wait_ge(sig("sines").sem, sig("sines").at(b * 3 + 2))
                        act.activation(cq[:, cols], cq[:, cols], ACT.Sin, scale=-1.0, bias=k.half_pi[:, 0:1]).then_inc(sig("sines").sem, 1)

                @block.gpsimd
                def _(pool):
                    with pool.Fori(0, B) as b:
                        cols = bass.ts(b, S)
                        pool.tensor_tensor(context[:, 0, cols], x[:, cols], cos[:, :], ALU.mult)
                        pool.tensor_tensor(context[:, 1, cols], x[:, cols], sin[:, :], ALU.mult)
                    steps3 = 3
                    for b in range(B):
                        cols = slice(b * S, (b + 1) * S)
                        chain = Chain(pool, sig("pool_step"), b, steps3)
                        pool.wait_ge(sig("sines").sem, sig("sines").at(b * 3 + 3))
                        chain.link(pool.tensor_tensor(a2[:, :], mem_r[:, cols], sq[:, cols], ALU.mult))
                        chain.link(pool.tensor_tensor(context[:, 3, cols], mem_i[:, cols], cq[:, cols], ALU.mult))
                        chain.link(pool.tensor_tensor(context[:, 3, cols], context[:, 3, cols], a2[:, :], ALU.subtract))
                        assert chain.n == steps3
                    sig("pool_step").advance(B * steps3)
            sig("angle_reduced").advance(B)
            sig("sines").advance(3 * B)

        with ExitStack() as st2:
            mu = k.ps("mu", [P, 2, S], stack=st2)
            var = k.ps("var", [P, 2, S], stack=st2)
            h_ps = k.ps("h_ps", [P, 2, S], stack=st2)
            o_ps = k.ps("o_ps", [P, 2, S], stack=st2)
            sqr = k.sb("sqr", [P, 4, S], stack=st2)
            rs = k.sb("rs", [P, NT], stack=st2)
            hidden = k.sb("hidden", [P, 2, S], stack=st2)
            with nc.Block() as block:

                def variances(pe, b):
                    for f in range(4):
                        pe.wait_ge(sig("squared").sem, sig("squared").at(b * 4 + f + 1))
                        last = pe.matmul(var[:, b % 2, :], k.mean_of_4[:, :], sqr[:, f, :], start=(f == 0), stop=(f == 3))
                    last.then_inc(sig("variance").sem, 1)

                @block.tensor
                def _(pe):
                    for b in range(B):
                        for f in range(4):
                            last = pe.matmul(mu[:, b % 2, :], k.mean_of_4[:, :], context[:, f, b * S:(b + 1) * S], start=(f == 0), stop=(f == 3))
                        last.then_inc(sig("context_mean").sem, 1)
                        if b < 1:
                            continue
                        variances(pe, b - 1)
                    variances(pe, B - 1)
                    with pe.Fori(0, B) as b:
                        cols = bass.ts(b, S)
                        for g in range(2):
                            pe.wait_ge(sig("gelus").sem, sig("gelus").at(b * 2 + g - 1))
                            for f in range(4):
                                pe.wait_ge(sig("context_normed").sem, sig("context_normed").at(b * 4 + f + 1))
                                last = pe.matmul(h_ps[:, g, :], mats("W1", f * 2 + g), context[:, f, cols], start=(f == 0), stop=(f == 3))
                            last.then_inc(sig("hidden_product").sem, 1)
                        pe.wait_ge(sig("residual").sem, sig("residual").at(b))
                        for g in range(2):
                            pe.wait_ge(sig("gelus").sem, sig("gelus").at(b * 2 + g + 1))
                            last = pe.matmul(o_ps[:, 0, :], mats("W2", g), hidden[:, g, :], start=(g == 0), stop=(g == 1))
                        last.then_inc(sig("mlp_out").sem, 1)

                @block.scalar
                def _(act):
                    act.preload_act_table(ACT.Ln)
                    for b in range(B):
                        cols = slice(b * S, (b + 1) * S)
                        act.wait_ge(sig("variance").sem, sig("variance").at(b))
                        for f in range(4):
                            act.wait_ge(sig("context_centred").sem, sig("context_centred").at(b * 4 + f + 1))
                            act.activation(sqr[:, f, :], context[:, f, cols], ACT.Square).then_inc(sig("squared").sem, 1)
                        act.wait_ge(sig("variance").sem, sig("variance").at(b + 1))
                        act.activation(rs[:, cols], var[:, b % 2, :], ACT.Ln, bias=k.eps[:, 0:1]).then_inc(sig("logs").sem, 1)
                        if b % 2 == 1:
                            act.wait_ge(sig("logs").sem, sig("logs").at(b + 1))
                            for two in (b - 1, b):
                                cols = slice(two * S, (two + 1) * S)
                                act.activation(rs[:, cols], rs[:, cols], ACT.Exp, scale=-0.5).then_inc(sig("rstd").sem, 1)
                    with act.Fori(0, B) as b:
                        for g in range(2):
                            act.wait_ge(sig("hidden_product").sem, sig("hidden_product").at(b * 2 + g + 1))
                            act.wait_ge(sig("mlp_out").sem, sig("mlp_out").at(b))
                            act.activation(hidden[:, g, :], h_ps[:, g, :], ACT.Gelu, bias=vec("b1", g)).then_inc(sig("gelus").sem, 1)

                @block.vector
                def _(dve):
                    def centre(b):
                        cols = slice(b * S, (b + 1) * S)
                        dve.wait_ge(sig("context_mean").sem, sig("context_mean").at(b + 1))
                        for f in range(4):
                            dve.tensor_tensor(context[:, f, cols], context[:, f, cols], mu[:, b % 2, :], ALU.subtract).then_inc(sig("context_centred").sem, 1)

                    def norm(b):
                        cols = slice(b * S, (b + 1) * S)
                        dve.wait_ge(sig("rstd").sem, sig("rstd").at(b + 1))
                        for f in range(4):
                            dve.tensor_tensor(context[:, f, cols], context[:, f, cols], rs[:, cols], ALU.mult).then_inc(sig("dve_step").sem, 1)
                        for f in range(4):
                            dve.wait_ge(sig("dve_step").sem, sig("dve_step").at(b * 4 + f + 1))
                            dve.tensor_scalar(context[:, f, cols], context[:, f, cols], vec("ln_g", f), vec("ln_b", f), ALU.mult, ALU.add).then_inc(sig("context_normed").sem, 1)

                    centre(0)
                    for b in range(B):
                        if b + 1 < B:
                            centre(b + 1)
                        norm(b)
                    with dve.Fori(0, B) as b:
                        cols = bass.ts(b, S)
                        dve.tensor_tensor(k.X[:, cols], k.X[:, cols], x[:, cols], ALU.add).then_inc(sig("normed").sem, 1)
                        dve.wait_ge(sig("mlp_out").sem, sig("mlp_out").at(b + 1))
                        dve.wait_ge(sig("normed").sem, sig("normed").at(b + 1))
                        dve.scalar_tensor_tensor(out=k.X[:, cols], in0=o_ps[:, 0, :], scalar=vec("b2"), in1=k.X[:, cols],
                                                 op0=ALU.add, op1=ALU.add).then_inc(sig("residual").sem, 1)

                block.gpsimd(also["gpsimd"])
                block.sync(also["sync"])
            for name, n in (("context_mean", B), ("context_centred", 4 * B), ("squared", 4 * B), ("variance", B), ("logs", B), ("rstd", B), ("dve_step", 4 * B),
                            ("context_normed", 4 * B), ("hidden_product", 2 * B), ("gelus", 2 * B), ("mlp_out", B), ("normed", B), ("residual", B)):
                sig(name).advance(n)


PARTS = 3
PAIRS = PARTS * PARTS
STACK = PAIRS * HD
HALF = HEADS // 2
GROUP = HALF // 2
LOW, SUMS = GROUP * HD, 2 * GROUP * HD
VCOLS = SUMS + GROUP
VWIDE = HALF * VCOLS + SUMS + GROUP
PER = 4
RINGS = 4
SOFTMAX_SCALE = float(HD) ** -0.5


class Level:

    def __init__(self, x, ctx, seq, chunks, chunk, weight, bias):
        self.x, self.ctx, self.seq, self.chunks, self.chunk, self.weight, self.bias = x, ctx, seq, chunks, chunk, weight, bias
        self.tile = min(P, seq)
        self.tokens = chunks * chunk
        self.after, self.first = None, 0
        assert chunk // self.tile == PER

    def keys_of(self, t):
        g = t * self.tile // self.seq
        return slice(g * self.seq, (g + 1) * self.seq)


class Unit:

    def __init__(self, level, c, half, looped=False):
        self.level, self.c, self.half, self.looped = level, c, half, looped
        self.number = (level.first + c) * 2 + half
        self.cols = bass.ts(c, level.chunk)

    def following(self, by):
        over, half = divmod(self.half + by, 2)
        c = self.c + over if over else self.c
        if self.looped or c < self.level.chunks:
            return Unit(self.level, c, half)
        return Unit(self.level.after, c - self.level.chunks, half) if self.level.after else None


def attention(k, levels, rope=None, residual=False):
    nc = k.nc
    sig = k.count_of
    per = PER
    for level, after in zip(levels, levels[1:]):
        level.after, after.first = after, level.first + level.chunks
    chunks = levels[-1].first + levels[-1].chunks
    big = max(level.chunk for level in levels)
    longest = max(level.seq for level in levels)
    peaks_dram = k.scratch("peaks", [2, PARTS * HALF, big])
    for level in levels:
        level.parts_dram = k.scratch("parts", [2, level.chunks * PARTS * HD, HEADS * level.chunk])

    with ExitStack() as st:
        for level in levels:
            level.values = k.sb("values", [P, level.chunks * per, P], stack=st)
            level.sums = k.sb("sums", [P, level.tokens], stack=st)
        queries = k.sb("queries", [P, 2, HALF * big], BF16, stack=st)
        keys = k.sb("keys", [P, 2, HALF * big], BF16, stack=st)
        spread = k.sb("spread", [P, 2 * per, VWIDE], F32R, stack=st)
        for level in levels:
            level.queries, level.keys = (a[:, :, 0:HALF * level.chunk].rearrange("p s (h t) -> p s h t", t=level.chunk) for a in (queries, keys))

        def columns(tile, slot, first, stride, width, bits=False):
            out = []
            for g in range(HALF // GROUP):
                at = g * GROUP * VCOLS + first
                a = spread[0:tile, slot, at:at + GROUP * stride]
                if bits:
                    a = a.bitcast(F32)
                out.append(a.rearrange("p t (h w) -> p t h w", w=stride)[:, :, :, 0:width])
            return out

        HALVES = 2 * HALF
        BANK = HALVES // 2
        DMAS = PARTS + 1
        start = Unit(levels[0], 0, 0), Unit(levels[0], 0, 1)

        def stack(sp, unit, group):
            g, slot = unit.level, unit.half
            came = sig(f"stack_in_{slot * 2 + group}")
            heads = slice(group * GROUP, (group + 1) * GROUP)
            first = (slot * HALF + group * GROUP) * g.chunk
            cols = slice(first, first + GROUP * g.chunk)
            every = PARTS * HD
            for i in range(PARTS):
                of = g.parts_dram[0, bass.ds((unit.c * PARTS + i) * HD, HD), cols]
                sp.dma_start(g.queries[i * every:(i + 1) * every, slot, heads, :], of.unsqueeze(0).to_broadcast([PARTS, HD, GROUP * g.chunk])).then_inc(came.sem, 16)
            of = g.parts_dram[1, bass.ds(unit.c * every, every), cols]
            sp.dma_start(g.keys[0:STACK, slot, heads, :], of.unsqueeze(0).to_broadcast([PARTS, every, GROUP * g.chunk])).then_inc(came.sem, 16)

        with ExitStack() as st2:
            proj = k.ps("proj", [P, 3, 512], stack=st2)
            rot = k.ps("rot", [P, 2, 512], stack=st2)
            vt = k.ps("vt", [P, 512], stack=st2)
            biased = k.sb("biased", [P, 3, big], stack=st2)
            turned = k.sb("turned", [P, 2, big], stack=st2)
            for level in levels:
                level.parts = k.sb("parts", [P, level.chunks, 2 * PARTS, level.chunk], BF16, stack=st2)

            def every_chunk(eng, body, skipped=0):
                for level in levels:
                    first = skipped if level is levels[0] else 0
                    with eng.Fori(0, level.chunks - first) as c:
                        body(level, c + first, level.first + first + c)

            fills = 2 + len(levels) + HALF // GROUP
            with nc.Block() as block:

                @block.tensor
                def _(pe):
                    def project(level, c, n):
                        chunk, tile = level.chunk, level.tile
                        for w in range(3):
                            pe.wait_ge(sig("projected").sem, sig("projected").at(n * 3 + w - 2))
                            pe.matmul(proj[:, w, 0:chunk], level.weight(w), level.x[:, bass.ts(c, chunk)], start=True, stop=True).then_inc(sig("projection").sem, 1)
                        if rope:
                            for w in range(2):
                                pe.wait_ge(sig("projected").sem, sig("projected").at(n * 3 + w + 1))
                                pe.wait_ge(sig("rotated").sem, sig("rotated").at(n))
                                pe.matmul(rot[:, w, 0:chunk], rope[0], biased[:, w, 0:chunk], start=True, stop=True).then_inc(sig("rotation").sem, 1)
                        pe.wait_ge(sig("projected").sem, sig("projected").at(n * 3 + 3))
                        pe.wait_ge(sig("values_kept").sem, sig("values_kept").at(n))
                        for t in range(per):
                            last = pe.transpose(vt[0:tile, t * P:(t + 1) * P], biased[:, 2, t * tile:(t + 1) * tile], k.ident)
                        last.then_inc(sig("values_turned").sem, 1)

                    every_chunk(pe, project)

                @block.scalar
                def _(act):
                    def biases(level, c, n):
                        for w in range(3):
                            act.wait_ge(sig("projection").sem, sig("projection").at(n * 3 + w + 1))
                            if w < 2:
                                act.wait_ge(sig("biased_used").sem, sig("biased_used").at(n))
                            else:
                                act.wait_ge(sig("values_turned").sem, sig("values_turned").at(n))
                            act.activation(biased[:, w, 0:level.chunk], proj[:, w, 0:level.chunk], ACT.Identity, bias=level.bias(w)).then_inc(sig("projected").sem, 1)

                    every_chunk(act, biases)

                @block.vector
                def _(dve):
                    steps = 2 + (2 if rope else 0)

                    def parts(level, c, n):
                        chunk, tile = level.chunk, level.tile
                        chain = Chain(dve, sig("dve_step"), n, steps)
                        src, rest = biased[:, 0:2, 0:chunk], turned[:, :, 0:chunk]
                        dve.wait_ge(sig("projected").sem, sig("projected").at(n * 3 + 2))
                        dve.wait_ge(sig("parts_made").sem, sig("parts_made").at(n))
                        if rope:
                            cosines, sines = (a.unsqueeze(1).to_broadcast([P, 2, chunk]) for a in rope[1:])
                            chain.link(dve.tensor_tensor(rest, src, cosines, ALU.mult))
                            dve.wait_ge(sig("rotation").sem, sig("rotation").at(n * 2 + 2))
                            dve.tensor_tensor(src, rot[:, :, 0:chunk], sines, ALU.mult).then_inc(sig("rotated").sem, 1)
                            dve.wait_ge(sig("rotated").sem, sig("rotated").at(n + 1))
                            chain.link(dve.tensor_tensor(src, src, rest, ALU.add))
                        at = [level.parts[:, c, i:2 * PARTS:PARTS, :] for i in range(PARTS)]
                        chain.link(dve.tensor_copy(at[0], src))
                        dve.tensor_tensor(rest, src, at[0], ALU.subtract).then_inc(sig("biased_used").sem, 1)
                        dve.wait_ge(sig("biased_used").sem, sig("biased_used").at(n + 1))
                        chain.link(dve.tensor_copy(at[1], rest))
                        dve.tensor_tensor(at[2], rest, at[1], ALU.subtract).then_inc(sig("parts_made").sem, 1)
                        assert chain.n == steps
                        dve.wait_ge(sig("values_turned").sem, sig("values_turned").at(n + 1))
                        dve.tensor_copy(level.values[0:tile, bass.ts(c, per), :], vt[0:tile, :].rearrange("p (t n) -> p t n", n=P)).then_inc(sig("values_kept").sem, 1)

                    every_chunk(dve, parts)
                    sig("dve_step").advance(chunks * steps)

                @block.gpsimd
                def _(pool):
                    chain = Chain(pool, sig("pool_step"))
                    chain.link(pool.memset(keys[64:P, :, :], 1.0))
                    for level in levels:
                        chain.link(pool.memset(level.sums[:, :], 1.0))
                    chain.link(pool.memset(spread[:, :, :].bitcast(F32), 0.0))
                    for ones in columns(P, slice(0, 2 * per), SUMS, VCOLS + 1, 1):
                        chain.link(pool.memset(ones.bitcast(F32), 1.0))
                    assert chain.n == fills

                @block.sync
                def _(sp):
                    def store(level, c, n, stored="parts_stored"):
                        sp.wait_ge(sig("parts_made").sem, sig("parts_made").at(n + 1))
                        for w in range(2):
                            for i in range(PARTS):
                                to = level.parts_dram[w, bass.ds((c * PARTS + i) * HD, HD), :].rearrange("d (h t) -> h d t", t=level.chunk)
                                sp.dma_start(to, level.parts[:, c, w * PARTS + i, :]).then_inc(sig(stored).sem, 16)

                    store(levels[0], 0, 0, "first_parts_stored")
                    store(levels[0], 1, 1)
                    sp.wait_ge(sig("first_parts_stored").sem, sig("first_parts_stored").at(2 * PARTS))
                    sp.wait_ge(sig("pool_step").sem, sig("pool_step").at(1))
                    for group in range(2):
                        stack(sp, start[0], group)
                    every_chunk(sp, store, skipped=2)
                    sp.wait_ge(sig("parts_stored").sem, sig("parts_stored").at(2 * PARTS * (chunks - 1)))
            for name, n in (("projection", 3 * chunks), ("projected", 3 * chunks), ("rotation", 2 * chunks if rope else 0),
                            ("rotated", chunks if rope else 0), ("values_turned", chunks), ("values_kept", chunks),
                            ("parts_made", chunks), ("biased_used", chunks), ("pool_step", fills), ("parts_stored", 2 * PARTS * (chunks - 1)), ("first_parts_stored", 2 * PARTS)):
                sig(name).advance(n)

        with ExitStack() as st2:
            banks = k.ps("banks", [P, 8, 512], stack=st2)
            s_ps, m_ps, o_ps = banks[:, 0:4, :], banks[:, 4:6, :], banks[:, 6:8, :]
            peaks_as_rows = m_ps[0:PARTS * HALF, 0, :].bitcast(BF16)
            p_hi = k.sb("p_hi", [P, RINGS, 2, longest], F32R, stack=st2)
            p_lo = k.sb("p_lo", [P, RINGS, 2, longest], F32R, stack=st2)
            probs = k.sb("probs", [P, RINGS, 2, longest], stack=st2)
            unit_values = k.sb("unit_values", [P, per, HALF * HD], stack=st2)
            by_low = k.sb("by_low", [GROUP * HD, 2, big], stack=st2)
            peak = k.sb("peak", [P, per, HALF], stack=st2)
            peak_parts = k.sb("peak_parts", [P, per, PARTS * HALF], BF16, stack=st2)
            peak_rows = k.sb("peak_rows", [PARTS * HALF, big], BF16, stack=st2)
            BLOCKS = per * HALF
            LAG = 3
            PEAKS_FROM, PEAKS_BY = 10, 7
            ROWS_AT = 8

            def first_bank(u, h):
                return 4 * (h % 2) if u == 0 else 4

            def on_pool(m, tile_):
                return tile_ == 1 or m in (0, 3, 5, 6)

            made = {"pool": [0], "dve": [0]}
            for m in range(HALVES):
                for who in made:
                    made[who].append(made[who][-1] + sum(on_pool(m, t) == (who == "pool") for t in range(2)))

            def units(eng, body):
                for level in levels:
                    if level.chunks > 1:
                        with eng.Fori(0, level.chunks - 1) as c:
                            for half in range(2):
                                body(Unit(level, c, half, looped=True))
                    for half in range(2):
                        body(Unit(level, level.chunks - 1, half))


            def ahead(unit, n, by):
                if n + by < HALVES:
                    return unit, n + by
                after = unit.following(1)
                return (after, n + by - HALVES) if after else None

            def peak_blocks(unit, n):
                half_ = BLOCKS // 2
                if n < PEAKS_BY and unit.following(1):
                    return [(unit.following(1), half_ + b) for b in range(n * half_ // PEAKS_BY, (n + 1) * half_ // PEAKS_BY)]
                if n >= PEAKS_FROM and unit.following(2):
                    steps, n = HALVES - PEAKS_FROM, n - PEAKS_FROM
                    return [(unit.following(2), b) for b in range(n * half_ // steps, (n + 1) * half_ // steps)]
                return []

            with nc.Block() as block:

                @block.tensor
                def _(pe):
                    def stack_in(unit, group):
                        came = sig(f"stack_in_{unit.half * 2 + group}")
                        pe.wait_ge(came.sem, came.at((unit.number - unit.half + 2) * (DMAS // 2)))

                    def peak_scores(unit, block_):
                        h, t = divmod(block_, per)
                        g, slot, tile = unit.level, unit.half, unit.level.tile
                        pe.wait_ge(sig("peak_found").sem, sig("peak_found").at(unit.number * BLOCKS + block_ - 1))
                        if block_ % (BLOCKS // 2) == 0:
                            stack_in(unit, h // GROUP)
                        if block_ == 0:
                            pe.wait_ge(sig("peak_rows").sem, sig("peak_rows").at(unit.number))
                        pe.matmul(m_ps[0:tile, t % 2, 0:g.seq], g.queries[0:STACK, slot, h, t * tile:(t + 1) * tile],
                                  g.keys[0:STACK, slot, h, g.keys_of(t)], start=True, stop=True).then_inc(sig("peak_scores").sem, 1)

                    def first_peaks(u, h):
                        g, tile = start[u].level, start[u].level.tile
                        pe.wait_ge(sig("peak_found").sem, sig("peak_found").at((u * HALF + h - (1 - u)) * per))
                        if h % GROUP == 0:
                            stack_in(start[u], h // GROUP)
                        if h == 0:
                            pe.wait_ge(sig("peak_rows").sem, sig("peak_rows").at(u))
                        for t in range(per):
                            last = pe.matmul(banks[0:tile, first_bank(u, h) + t, 0:g.seq], g.queries[0:STACK, u, h, t * tile:(t + 1) * tile],
                                             g.keys[0:STACK, u, h, g.keys_of(t)], start=True, stop=True)
                        last.then_inc(sig("peak_scores").sem, per)

                    def peaks_turned(unit):
                        tile = unit.level.tile
                        pe.wait_ge(sig("peaks_split").sem, sig("peaks_split").at(unit.number + 1))
                        for t in range(per):
                            last = pe.transpose(peaks_as_rows[:, t * tile:(t + 1) * tile], peak_parts[0:tile, t, :], k.ident_bf[0:tile, 0:tile])
                        last.then_inc(sig("peaks_turned").sem, 1)

                    def scores(unit, m):
                        g, slot, tile = unit.level, unit.half, unit.level.tile
                        if m == 0:
                            pe.wait_ge(sig("peaks_in").sem, sig("peaks_in").at(unit.number + 1))
                        pe.wait_ge(sig("probs").sem, sig("probs").at(unit.number * HALVES + m - 1))
                        for t in (m % 2 * 2, m % 2 * 2 + 1):
                            last = pe.matmul(s_ps[0:tile, t, 0:g.seq], g.keys[0:STACK + PARTS, slot, m // 2, t * tile:(t + 1) * tile],
                                             g.queries[0:STACK + PARTS, slot, m // 2, g.keys_of(t)], start=True, stop=True)
                        last.then_inc(sig("scores").sem, 1)

                    def context(unit, m, between):
                        g, u, tile = unit.level, unit.number, unit.level.tile
                        bank, first = divmod(m, BANK)
                        if m == 0:
                            pe.wait_ge(sig("values_spread").sem, sig("values_spread").at(u + 1))
                        if first == 0:
                            pe.wait_ge(sig("context_kept").sem, sig("context_kept").at(u * 2 + bank - 1))
                            pe.wait_ge(sig("sums_kept").sem, sig("sums_kept").at(u * 2 + bank - 1))
                        pe.wait_ge(sig("probs_low").sem, sig("probs_low").at(u * made["dve"][-1] + made["dve"][m + 1]))
                        pe.wait_ge(sig("probs_low_pool").sem, sig("probs_low_pool").at(u * made["pool"][-1] + made["pool"][m + 1]))
                        for two in range(2):
                            t = m % 2 * 2 + two
                            for part in (p_hi, p_lo):
                                last = pe.matmul(o_ps[0:VCOLS, bank, g.keys_of(t)], spread[0:tile, unit.half * per + t, m // 2 * VCOLS:(m // 2 + 1) * VCOLS],
                                                 part[0:tile, m % RINGS, two, 0:g.seq], start=(first == 0 and two == 0 and part is p_hi),
                                                 stop=(first == BANK - 1 and two == 1 and part is p_lo), skip_group_check=True)
                                if two == 1 and part is p_lo:
                                    last.then_inc(sig("context_sums").sem, 1)
                                between()

                    def work(unit):
                        for n in range(HALVES):
                            blocks = peak_blocks(unit, n)
                            spots = [4]

                            def between():
                                for _ in range(-(-len(blocks) // spots[0]) if spots[0] else 0):
                                    peak_scores(*blocks.pop(0))
                                spots[0] -= 1

                            step = ahead(unit, n, LAG)
                            if step:
                                scores(*step)
                            context(unit, n, between)
                            if n == PEAKS_BY and unit.following(1):
                                peaks_turned(unit.following(1))

                    for h in range(HALF):
                        first_peaks(0, h)
                    peaks_turned(start[0])
                    first_peaks(1, 0)
                    for m in range(LAG):
                        first_peaks(1, m + 1)
                        scores(start[0], m)
                    pe.wait_ge(sig("peak_found").sem, sig("peak_found").at(BLOCKS + BLOCKS // 2))
                    units(pe, work)

                @block.scalar
                def _(act):
                    def peak_rows_kept(unit):
                        act.wait_ge(sig("peaks_turned").sem, sig("peaks_turned").at(unit.number + 1))
                        act.wait_ge(sig("peaks_out").sem, sig("peaks_out").at(unit.number))
                        act.activation(peak_rows[:, 0:unit.level.chunk], peaks_as_rows[:, 0:unit.level.chunk], ACT.Copy).then_inc(sig("peak_rows").sem, 1)

                    def exponentials(unit, m):
                        tile, seq = unit.level.tile, unit.level.seq
                        act.wait_ge(sig("context_sums").sem, sig("context_sums").at(unit.number * HALVES + m + 1 - RINGS))
                        act.wait_ge(sig("scores").sem, sig("scores").at(unit.number * HALVES + m + 1))
                        of = s_ps[0:tile, m % 2 * 2:m % 2 * 2 + 2, 0:seq]
                        act.activation(probs[0:tile, m % RINGS, :, 0:seq], of, ACT.Exp, scale=SOFTMAX_SCALE)
                        act.activation(p_hi[0:tile, m % RINGS, :, 0:seq], of, ACT.Exp, scale=SOFTMAX_SCALE).then_inc(sig("probs").sem, 1)

                    def kept(unit, bank):
                        u, chunk = unit.number, unit.level.chunk
                        at = (unit.half * 2 + bank) * 32
                        act.wait_ge(sig("context_kept").sem, sig("context_kept").at(u * 2 + bank - 1))
                        act.wait_ge(sig("context_sums").sem, sig("context_sums").at(u * HALVES + (bank + 1) * BANK))
                        act.activation(by_low[:, bank, 0:chunk], o_ps[LOW:SUMS, bank, 0:chunk], ACT.Copy).then_inc(sig("context_low").sem, 1)
                        act.activation(unit.level.sums[at:at + GROUP, unit.cols], o_ps[SUMS:VCOLS, bank, 0:chunk], ACT.Copy).then_inc(sig("sums_kept").sem, 1)

                    def work(unit):
                        for n in range(HALVES):
                            if n % BANK == BANK - 1:
                                kept(unit, n // BANK)
                            step = ahead(unit, n, RINGS)
                            if step:
                                exponentials(*step)
                            if n == ROWS_AT and unit.following(1):
                                peak_rows_kept(unit.following(1))

                    peak_rows_kept(start[0])
                    for m in range(RINGS):
                        exponentials(start[0], m)
                    units(act, work)

                @block.vector
                def _(dve):
                    steps = 4

                    def found(unit, block_):
                        h, t = divmod(block_, per)
                        tile = unit.level.tile
                        dve.wait_ge(sig("peak_scores").sem, sig("peak_scores").at(unit.number * BLOCKS + block_ + 1))
                        dve.tensor_reduce(peak[0:tile, t, h:h + 1], m_ps[0:tile, t % 2, 0:unit.level.seq], AX.X, ALU.max).then_inc(sig("peak_found").sem, 1)

                    def first_found(u, h):
                        tile = start[u].level.tile
                        dve.wait_ge(sig("peak_scores").sem, sig("peak_scores").at(u * BLOCKS + (h + 1) * per))
                        of = banks[0:tile, first_bank(u, h):first_bank(u, h) + per, 0:start[u].level.seq]
                        dve.tensor_reduce(peak[0:tile, :, h], of, AX.X, ALU.max).then_inc(sig("peak_found").sem, per)

                    def split(unit):
                        u, tile = unit.number, unit.level.tile
                        dve.wait_ge(sig("peak_found").sem, sig("peak_found").at(u * BLOCKS + BLOCKS))
                        dve.wait_ge(sig("peaks_turned").sem, sig("peaks_turned").at(u))
                        chain = Chain(dve, sig("dve_step"), u, steps)
                        at = [peak_parts[0:tile, :, n * HALF:(n + 1) * HALF] for n in range(PARTS)]
                        chain.link(dve.tensor_scalar(peak[0:tile, :, :], peak[0:tile, :, :], -1.0, None, ALU.mult))
                        chain.link(dve.tensor_copy(at[0], peak[0:tile, :, :]))
                        chain.link(dve.tensor_tensor(peak[0:tile, :, :], peak[0:tile, :, :], at[0], ALU.subtract))
                        chain.link(dve.tensor_copy(at[1], peak[0:tile, :, :]))
                        assert chain.n == steps
                        dve.tensor_tensor(at[2], peak[0:tile, :, :], at[1], ALU.subtract).then_inc(sig("peaks_split").sem, 1)

                    def low(unit, m):
                        tile, seq = unit.level.tile, unit.level.seq
                        dve.wait_ge(sig("probs").sem, sig("probs").at(unit.number * HALVES + m + 1))
                        for t in range(2):
                            if not on_pool(m, t):
                                at = (slice(0, tile), m % RINGS, t, slice(0, seq))
                                dve.tensor_tensor(p_lo[at], probs[at], p_hi[at].bitcast(F32), ALU.subtract).then_inc(sig("probs_low").sem, 1)

                    def kept(unit, bank):
                        at = (unit.half * 2 + bank) * 32
                        dve.wait_ge(sig("context_low").sem, sig("context_low").at(unit.number * 2 + bank + 1))
                        dve.tensor_tensor(unit.level.ctx[at:at + GROUP * HD, unit.cols], o_ps[0:LOW, bank, 0:unit.level.chunk], by_low[:, bank, 0:unit.level.chunk],
                                          ALU.add).then_inc(sig("context_kept").sem, 1)

                    def work(unit):
                        for n in range(HALVES):
                            for peaks in peak_blocks(unit, n):
                                found(*peaks)
                            if n == PEAKS_BY - 1 and unit.following(1):
                                split(unit.following(1))
                            step = ahead(unit, n, LAG)
                            if step:
                                low(*step)
                            if n == BANK:
                                kept(unit, 0)
                        kept(unit, 1)

                    for h in range(HALF):
                        first_found(0, h)
                    split(start[0])
                    first_found(1, 0)
                    for m in range(LAG):
                        first_found(1, m + 1)
                        if m > 0:
                            low(start[0], m - 1)
                    low(start[0], LAG - 1)
                    units(dve, work)
                    sig("dve_step").advance(2 * chunks * steps)

                @block.gpsimd
                def _(pool):
                    def split_heads(a):
                        return [a[:, :, g * GROUP * HD:(g + 1) * GROUP * HD].rearrange("p t (h w) -> p t h w", w=HD) for g in range(HALF // GROUP)]

                    def values_spread(unit):
                        u, tile, half = unit.number, unit.level.tile, unit.half
                        pool.wait_ge(sig("context_sums").sem, sig("context_sums").at(u * HALVES - HALVES))
                        slot = slice(half * per, (half + 1) * per)
                        of = unit.level.values[0:tile, bass.ts(unit.c, per), half * HALF * HD:(half + 1) * HALF * HD]
                        pool.tensor_copy(unit_values[0:tile, :, :], of).then_inc(sig("pool_step").sem, 1)
                        for to, v in zip(columns(tile, slot, 0, VCOLS + HD, HD), split_heads(of)):
                            pool.tensor_copy(to, v).then_inc(sig("pool_step").sem, 1)
                        pool.wait_ge(sig("pool_step").sem, sig("pool_step").at(u * 3 + 3))
                        for to, v, hi in zip(columns(tile, slot, LOW, VCOLS + HD, HD), split_heads(unit_values[0:tile, :, :]), columns(tile, slot, 0, VCOLS + HD, HD, bits=True)):
                            last = pool.tensor_tensor(to, v, hi, ALU.subtract)
                        last.then_inc(sig("values_spread").sem, 1)

                    def work(unit):
                        tile, seq = unit.level.tile, unit.level.seq
                        for m in range(HALVES):
                            for t in range(2):
                                if on_pool(m, t):
                                    at = (slice(0, tile), m % RINGS, t, slice(0, seq))
                                    pool.wait_ge(sig("probs").sem, sig("probs").at(unit.number * HALVES + m + 1))
                                    pool.tensor_tensor(p_lo[at], probs[at], p_hi[at].bitcast(F32), ALU.subtract).then_inc(sig("probs_low_pool").sem, 1)
                            if m == BANK and unit.following(1):
                                values_spread(unit.following(1))

                    values_spread(start[0])
                    units(pool, work)

                @block.sync
                def _(sp):
                    def peak_rows_in(unit):
                        g, slot = unit.level, unit.half
                        sp.wait_ge(sig("peak_rows").sem, sig("peak_rows").at(unit.number + 1))
                        sp.dma_start(peaks_dram[slot, :, 0:g.chunk], peak_rows[:, 0:g.chunk]).then_inc(sig("peaks_out").sem, 16)
                        sp.wait_ge(sig("peaks_out").sem, sig("peaks_out").at(unit.number + 1))
                        sp.dma_start(g.queries[STACK:STACK + PARTS, slot, :, :], peaks_dram[slot, :, 0:g.chunk].rearrange("(n h) t -> n h t", h=HALF)).then_inc(sig("peaks_in").sem, 16)

                    def work(unit):
                        def stack_over(group):
                            unit_ = unit.following(2)
                            if unit_:
                                sp.wait_ge(sig("scores").sem, sig("scores").at(unit.number * HALVES + (group + 1) * BANK))
                                stack(sp, unit_, group)

                        stack_over(0)
                        if unit.following(1):
                            peak_rows_in(unit.following(1))
                        stack_over(1)

                    for group in range(2):
                        stack(sp, start[1], group)
                    peak_rows_in(start[0])
                    units(sp, work)
            n = 2 * chunks
            for name, total in (("peak_found", n * BLOCKS), ("peak_scores", n * BLOCKS), ("peaks_split", n), ("peaks_turned", n), ("peak_rows", n),
                                ("peaks_out", n), ("peaks_in", n), ("scores", n * HALVES), ("probs", n * HALVES), ("context_sums", n * HALVES),
                                ("probs_low", n * made["dve"][-1]), ("probs_low_pool", n * made["pool"][-1]), ("context_low", 2 * n),
                                ("context_kept", 2 * n), ("sums_kept", 2 * n), ("values_spread", n), ("pool_step", 3 * n),
                                *[(f"stack_in_{s}", chunks * DMAS) for s in range(4)]):
                sig(name).advance(total)

        with ExitStack() as st2:
            per_row = k.ps("per_row", [P, chunks, 512], stack=st2)
            every = [(level, c, slice(c * level.chunk, (c + 1) * level.chunk)) for level in levels for c in range(level.chunks)]
            with nc.Block() as block:

                @block.tensor
                def _(pe):
                    for n, (level, c, cols) in enumerate(every):
                        pe.wait_ge(sig("rstd").sem, sig("rstd").at(n + 1))
                        pe.matmul(per_row[:, n, 0:level.chunk], k.head_rows[:, :], level.sums[:, cols], start=True, stop=True).then_inc(sig("sums_spread").sem, 1)

                @block.scalar
                def _(act):
                    act.preload_act_table(ACT.Ln)
                    for level, c, cols in every:
                        act.activation(level.sums[:, cols], level.sums[:, cols], ACT.Ln).then_inc(sig("logs").sem, 1)
                    for n, (level, c, cols) in enumerate(every):
                        act.wait_ge(sig("logs").sem, sig("logs").at(n + 1))
                        act.activation(level.sums[:, cols], level.sums[:, cols], ACT.Exp, scale=-1.0).then_inc(sig("rstd").sem, 1)

                @block.vector
                def _(dve):
                    for n, (level, c, cols) in enumerate(every):
                        dve.wait_ge(sig("sums_spread").sem, sig("sums_spread").at(n + 1))
                        last = dve.tensor_tensor(level.ctx[:, cols], level.ctx[:, cols], per_row[:, n, 0:level.chunk], ALU.mult)
                        if residual:
                            last.then_inc(sig("normed").sem, 1)
                    if residual:
                        for n, (level, c, cols) in enumerate(every):
                            dve.wait_ge(sig("normed").sem, sig("normed").at(n + 1))
                            dve.tensor_tensor(k.X[:, cols], k.X[:, cols], level.ctx[:, cols], ALU.add)
                        sig("normed").advance(chunks)
            sig("sums_spread").advance(chunks)
            sig("logs").advance(chunks)
            sig("rstd").advance(chunks)


def sampled(k, x, parts):
    with k.nc.Block() as block:

        @block.gpsimd
        def _(pool):
            for l, part in parts.items():
                whole = x.rearrange("p (n s) -> p n s", s=2 ** l)
                pool.tensor_copy(part, whole[:, :, 0])


def combine_levels(k, contexts, out_w, up_w, out_b, up_b, also):
    nc = k.nc
    sig = k.count_of
    with ExitStack() as st:
        ps = k.ps("level_ps", [P, 4, 512], stack=st)
        level = [k.sb(f"level{l}", [P, NT >> l], stack=st) for l in range(LEVELS)]
        quarter = k.sb("quarter", [P, NT // 2], stack=st)
        fine = [k.sb(f"fine{l}", [P, NT >> l], stack=st) for l in range(LEVELS - 1)]
        both = k.sb("both_b", [P, LEVELS], stack=st)
        work = []
        for l in range(LEVELS - 1, -1, -1):
            n = NT >> l
            work += [(l, at, min(CH, n - at)) for at in range(0, n, CH)]
        done = {l: sum(1 for w in work if w[0] >= l) for l in range(LEVELS)}
        with nc.Block() as block:

            @block.tensor
            def _(pe):
                for n, (l, at, size) in enumerate(work):
                    pe.wait_ge(sig("level_kept").sem, sig("level_kept").at(n - 3))
                    coarser = l < LEVELS - 1
                    last = pe.matmul(ps[:, n % 4, 0:size], out_w(l), contexts[l][:, at:at + size], start=True, stop=not coarser)
                    if coarser:
                        pe.wait_ge(sig("upsampled").sem, sig("upsampled").at(LEVELS - 1 - l))
                        last = pe.matmul(ps[:, n % 4, 0:size], up_w(l), fine[l][:, at:at + size], start=False, stop=True)
                    last.then_inc(sig("level_product").sem, 1)

            @block.scalar
            def _(act):
                act.wait_ge(sig("normed").sem, sig("normed").at(1))
                for n, (l, at, size) in enumerate(work):
                    act.wait_ge(sig("level_product").sem, sig("level_product").at(n + 1))
                    act.activation(level[l][:, at:at + size], ps[:, n % 4, 0:size], ACT.Identity, bias=both[:, l:l + 1]).then_inc(sig("level_kept").sem, 1)
                also["scalar"](act)

            @block.vector
            def _(dve):
                chain = Chain(dve, sig("dve_step"))
                chain.link(dve.tensor_copy(both[:, :], out_b))
                dve.tensor_tensor(both[:, 0:LEVELS - 1], both[:, 0:LEVELS - 1], up_b, ALU.add).then_inc(sig("normed").sem, 1)
                for l in range(LEVELS - 2, -1, -1):
                    n = S >> (l + 1)
                    c = level[l + 1][:, :].rearrange("p (b n) -> p b n", n=n)
                    q = quarter[:, 0:B * n].rearrange("p (b n) -> p b n", n=n)
                    u = fine[l][:, :].rearrange("p (b n two) -> p b n two", n=n, two=2)
                    dve.wait_ge(sig("level_kept").sem, sig("level_kept").at(done[l + 1]))
                    chain.link(dve.tensor_scalar(q, c, 0.25, None, ALU.mult))
                    dve.scalar_tensor_tensor(out=u[:, :, 0:n - 1, 1], in0=c[:, :, 0:n - 1], scalar=0.75, in1=q[:, :, 1:n], op0=ALU.mult, op1=ALU.add)
                    dve.scalar_tensor_tensor(out=u[:, :, 1:n, 0], in0=c[:, :, 1:n], scalar=0.75, in1=q[:, :, 0:n - 1], op0=ALU.mult, op1=ALU.add)
                    dve.tensor_copy(u[:, :, 0, 0], c[:, :, 0])
                    dve.tensor_copy(u[:, :, n - 1, 1], c[:, :, n - 1]).then_inc(sig("upsampled").sem, 1)
                    if l > 0:
                        dve.wait_ge(sig("upsampled").sem, sig("upsampled").at(LEVELS - 1 - l))
                for c in range(NC):
                    cols = slice(c * CH, (c + 1) * CH)
                    dve.wait_ge(sig("level_kept").sem, sig("level_kept").at(done[1] + c + 1))
                    dve.tensor_tensor(k.X[:, cols], k.X[:, cols], level[0][:, cols], ALU.add)
                sig("dve_step").advance(chain.n)
                also["vector"](dve)

            block.gpsimd(also["gpsimd"])
            block.sync(also["sync"])
        for name, n in (("level_kept", len(work)), ("level_product", len(work)), ("upsampled", LEVELS - 1), ("normed", 1)):
            sig(name).advance(n)


K_CLAMP = 60.0


def mixed(dve, sig, out, x, coef, b):
    n = sig("mix_step")

    def landed(step):
        dve.wait_ge(n.sem, n.at(b * 2 + step))

    dve.tensor_scalar(out[:, bass.ts(b, S)], x[:, bass.ts(b, S)], coef[:, 0:1], None, ALU.mult).then_inc(n.sem, 1)
    landed(1)
    dve.scalar_tensor_tensor(out=out[:, bass.ds(b * S + 1, S - 1)], in0=x[:, bass.ds(b * S, S - 1)], scalar=coef[:, 1:2], in1=out[:, bass.ds(b * S + 1, S - 1)],
                             op0=ALU.mult, op1=ALU.add).then_inc(n.sem, 1)
    landed(2)
    dve.scalar_tensor_tensor(out=out[:, bass.ds(b * S, S - 1)], in0=x[:, bass.ds(b * S + 1, S - 1)], scalar=coef[:, 2:3], in1=out[:, bass.ds(b * S, S - 1)],
                             op0=ALU.mult, op1=ALU.add).then_inc(sig("mixed").sem, 1)


def mix_coefficients(chain, dve, coef, time_mix, combined_mix, first_half, second_half):
    chain.link(dve.tensor_copy(coef[:, 0:1], time_mix))
    chain.link(dve.tensor_scalar(coef[:, 1:2], time_mix, -1.0, 1.0, ALU.mult, ALU.add))
    chain.link(dve.scalar_tensor_tensor(out=coef[:, 1:2], in0=combined_mix, scalar=first_half, in1=coef[:, 1:2], op0=ALU.mult, op1=ALU.add))
    chain.link(dve.tensor_scalar(coef[:, 2:3], combined_mix, second_half, None, ALU.mult))


def time_mix(k, x, out, mats, vec):
    nc = k.nc
    sig = k.count_of
    with ExitStack() as st:
        k_ps, v_ps, r_ps, o_ps = (k.ps(f"{n}_ps", [P, 2, S], stack=st) for n in "kvro")
        coef = k.sb("coef", [P, 3], stack=st)
        rates = k.sb("rates", [P, 3], stack=st)
        decay = k.sb("decay", [P, S], stack=st)
        xm = k.sb("xm", [P, NT], stack=st)
        key = k.sb("key", [P, NT], stack=st)
        kv = k.sb("kv", [P, NT], stack=st)
        val = k.sb("val", [P, NT], stack=st)
        gate = k.sb("gate", [P, NT], stack=st)
        a = k.sb("a", [P, B, S + 1], stack=st)
        d = k.sb("d", [P, B, S + 1], stack=st)
        with nc.Block() as block:

            @block.tensor
            def _(pe):
                for b in range(B):
                    cols = slice(b * S, (b + 1) * S)
                    pe.wait_ge(sig("mixed").sem, sig("mixed").at(b + 1))
                    pe.wait_ge(sig("key_clamped").sem, sig("key_clamped").at(b - 1))
                    pe.matmul(k_ps[:, b % 2, :], mats("Wk"), xm[:, cols], start=True, stop=True).then_inc(sig("projection").sem, 1)
                    pe.wait_ge(sig("values_copied").sem, sig("values_copied").at(b * 2 - 2))
                    pe.matmul(v_ps[:, b % 2, :], mats("Wv"), xm[:, cols], start=True, stop=True).then_inc(sig("projection").sem, 1)
                    pe.matmul(r_ps[:, b % 2, :], mats("Wr"), xm[:, cols], start=True, stop=True).then_inc(sig("projection").sem, 1)
                for b in range(B):
                    pe.wait_ge(sig("gated").sem, sig("gated").at(b + 1))
                    pe.wait_ge(sig("residual").sem, sig("residual").at(b - 1))
                    pe.matmul(o_ps[:, b % 2, :], mats("Wo"), gate[:, b * S:(b + 1) * S], start=True, stop=True).then_inc(sig("mlp_out").sem, 1)

            @block.scalar
            def _(act):
                r = sig("rstd")
                act.activation(rates[:, 0:1], vec("time_decay"), ACT.Exp).then_inc(r.sem, 1)
                act.activation(rates[:, 2:3], vec("time_first"), ACT.Exp).then_inc(r.sem, 1)
                act.wait_ge(r.sem, r.at(1))
                act.activation(rates[:, 1:2], rates[:, 0:1], ACT.Exp, scale=-1.0).then_inc(r.sem, 1)
                for b in range(B):
                    cols = slice(b * S, (b + 1) * S)
                    act.wait_ge(sig("projection").sem, sig("projection").at(b * 3 + 3))
                    act.activation(val[:, cols], v_ps[:, b % 2, :], ACT.Copy).then_inc(sig("values_copied").sem, 1)
                    act.activation(gate[:, cols], r_ps[:, b % 2, :], ACT.Copy).then_inc(sig("values_copied").sem, 1)
                    act.wait_ge(sig("key_clamped").sem, sig("key_clamped").at(b + 1))
                    act.activation(key[:, cols], key[:, cols], ACT.Exp).then_inc(sig("probs").sem, 1)
                for b in range(B):
                    cols = slice(b * S, (b + 1) * S)
                    act.wait_ge(sig("values_copied").sem, sig("values_copied").at(b * 2 + 2))
                    act.activation(gate[:, cols], gate[:, cols], ACT.Sigmoid).then_inc(sig("sigmoids").sem, 1)

            @block.vector
            def _(dve):
                chain = Chain(dve, sig("dve_step"))
                mix_coefficients(chain, dve, coef, vec("att_time_mix"), vec("att_combined_mix"), vec("first_half"), vec("second_half"))
                chain.link(dve.memset(a[:, :, 0:1], 0.0))
                chain.link(dve.memset(d[:, :, 0:1], 0.0))
                chain.link(dve.memset(decay[:, :], 1.0))
                with dve.Fori(0, B) as b:
                    mixed(dve, sig, xm, x, coef, b)
                dve.wait_ge(sig("rstd").sem, sig("rstd").at(3))
                chain.link(dve.tensor_scalar(decay[:, :], decay[:, :], rates[:, 1:2], None, ALU.mult))
                for b in range(B):
                    cols = slice(b * S, (b + 1) * S)
                    dve.wait_ge(sig("projection").sem, sig("projection").at(b * 3 + 1))
                    dve.tensor_scalar(key[:, cols], k_ps[:, b % 2, :], K_CLAMP, None, ALU.min).then_inc(sig("key_clamped").sem, 1)
                for b in range(B):
                    cols = slice(b * S, (b + 1) * S)
                    dve.wait_ge(sig("probs").sem, sig("probs").at(b + 1))
                    dve.tensor_tensor_scan(d[:, b, 1:S + 1], decay[:, :], key[:, cols], 0.0, ALU.mult, ALU.add).then_inc(sig("memories").sem, 1)
                    dve.wait_ge(sig("key_values").sem, sig("key_values").at(b + 1))
                    dve.tensor_tensor_scan(a[:, b, 1:S + 1], decay[:, :], kv[:, cols], 0.0, ALU.mult, ALU.add).then_inc(sig("memories").sem, 1)
                    dve.wait_ge(sig("memories").sem, sig("memories").at(b * 2 + 2))
                    chain.link(dve.scalar_tensor_tensor(out=key[:, cols], in0=key[:, cols], scalar=rates[:, 2:3], in1=d[:, b, 0:S], op0=ALU.mult, op1=ALU.add))
                    dve.reciprocal(key[:, cols], key[:, cols]).then_inc(sig("rotated").sem, 1)
                    chain.link(dve.scalar_tensor_tensor(out=kv[:, cols], in0=kv[:, cols], scalar=rates[:, 2:3], in1=a[:, b, 0:S], op0=ALU.mult, op1=ALU.add))
                    dve.wait_ge(sig("rotated").sem, sig("rotated").at(b + 1))
                    dve.tensor_tensor(kv[:, cols], kv[:, cols], key[:, cols], ALU.mult).then_inc(sig("averaged").sem, 1)
                for b in range(B):
                    cols = slice(b * S, (b + 1) * S)
                    dve.wait_ge(sig("mlp_out").sem, sig("mlp_out").at(b + 1))
                    dve.tensor_tensor(out[:, cols], x[:, cols], o_ps[:, b % 2, :], ALU.add).then_inc(sig("residual").sem, 1)
                sig("dve_step").advance(chain.n)

            @block.gpsimd
            def _(pool):
                for b in range(B):
                    cols = slice(b * S, (b + 1) * S)
                    pool.wait_ge(sig("probs").sem, sig("probs").at(b + 1))
                    pool.wait_ge(sig("values_copied").sem, sig("values_copied").at(b * 2 + 1))
                    pool.tensor_tensor(kv[:, cols], key[:, cols], val[:, cols], ALU.mult).then_inc(sig("key_values").sem, 1)
                for b in range(B):
                    cols = slice(b * S, (b + 1) * S)
                    pool.wait_ge(sig("sigmoids").sem, sig("sigmoids").at(b + 1))
                    pool.wait_ge(sig("averaged").sem, sig("averaged").at(b + 1))
                    pool.tensor_tensor(gate[:, cols], gate[:, cols], kv[:, cols], ALU.mult).then_inc(sig("gated").sem, 1)
        for name, n in (("mixed", B), ("mix_step", 2 * B), ("projection", 3 * B), ("key_clamped", B), ("values_copied", 2 * B), ("probs", B), ("sigmoids", B),
                        ("rstd", 3), ("memories", 2 * B), ("key_values", B), ("rotated", B), ("averaged", B), ("gated", B), ("mlp_out", B), ("residual", B)):
            sig(name).advance(n)


def channel_mix(k, x, mats, vec):
    nc = k.nc
    sig = k.count_of
    G = 4
    with ExitStack() as st:
        h_ps = k.ps("h_ps", [P, 2, S], stack=st)
        r_ps = k.ps("r_ps", [P, 2, S], stack=st)
        o_ps = k.ps("o_ps", [P, 2, S], stack=st)
        coef = k.sb("coef", [P, 3], stack=st)
        xm = k.sb("xm", [P, NT], stack=st)
        relu = k.sb("relu", [P, G, S], stack=st)
        hidden = k.sb("hidden", [P, G, S], stack=st)
        gate = k.sb("gate", [P, NT], stack=st)
        with nc.Block() as block:

            @block.tensor
            def _(pe):
                def down(n):
                    b, g = n // G, n % G
                    pe.wait_ge(sig("silu_up").sem, sig("silu_up").at(n + 1))
                    if g == 0:
                        pe.wait_ge(sig("residual").sem, sig("residual").at(b - 1))
                    last = pe.matmul(o_ps[:, b % 2, :], mats("Fv", g), hidden[:, g, :], start=(g == 0), stop=(g == G - 1))
                    if g == G - 1:
                        last.then_inc(sig("mlp_out").sem, 1)

                for b in range(B):
                    cols = slice(b * S, (b + 1) * S)
                    pe.wait_ge(sig("mixed").sem, sig("mixed").at(b + 1))
                    pe.wait_ge(sig("sigmoids").sem, sig("sigmoids").at(b - 1))
                    pe.matmul(r_ps[:, b % 2, :], mats("Fr"), xm[:, cols], start=True, stop=True).then_inc(sig("angle_product").sem, 1)
                    for g in range(G):
                        n = b * G + g
                        pe.wait_ge(sig("silu_up").sem, sig("silu_up").at(n - 1))
                        pe.matmul(h_ps[:, n % 2, :], mats("Fk", g), xm[:, cols], start=True, stop=True).then_inc(sig("hidden_product").sem, 1)
                        if n >= 2:
                            down(n - 2)
                down(B * G - 2)
                down(B * G - 1)

            @block.scalar
            def _(act):
                for b in range(B):
                    act.wait_ge(sig("angle_product").sem, sig("angle_product").at(b + 1))
                    act.activation(gate[:, b * S:(b + 1) * S], r_ps[:, b % 2, :], ACT.Sigmoid).then_inc(sig("sigmoids").sem, 1)
                    for g in range(G):
                        n = b * G + g
                        act.wait_ge(sig("hidden_product").sem, sig("hidden_product").at(n + 1))
                        act.wait_ge(sig("silu_up").sem, sig("silu_up").at(n - G + 1))
                        act.activation(relu[:, g, :], h_ps[:, n % 2, :], ACT.Relu).then_inc(sig("gelus").sem, 1)

            @block.vector
            def _(dve):
                chain = Chain(dve, sig("dve_step"))
                mix_coefficients(chain, dve, coef, vec("ffn_time_mix"), vec("ffn_combined_mix"), vec("first_half"), vec("second_half"))
                with dve.Fori(0, B) as b:
                    mixed(dve, sig, xm, x, coef, b)
                for b in range(B):
                    cols = slice(b * S, (b + 1) * S)
                    dve.tensor_tensor(k.X[:, cols], k.X[:, cols], x[:, cols], ALU.add).then_inc(sig("normed").sem, 1)
                    for g in range(G):
                        n = b * G + g
                        dve.wait_ge(sig("gelus").sem, sig("gelus").at(n + 1))
                        dve.wait_ge(sig("mlp_out").sem, sig("mlp_out").at(b))
                        dve.tensor_tensor(hidden[:, g, :], relu[:, g, :], h_ps[:, n % 2, :], ALU.mult).then_inc(sig("silu_up").sem, 1)
                    dve.wait_ge(sig("mlp_out").sem, sig("mlp_out").at(b + 1))
                    chain.link(dve.tensor_tensor(gate[:, cols], gate[:, cols], o_ps[:, b % 2, :], ALU.mult))
                    dve.wait_ge(sig("normed").sem, sig("normed").at(b + 1))
                    dve.tensor_tensor(k.X[:, cols], k.X[:, cols], gate[:, cols], ALU.add).then_inc(sig("residual").sem, 1)
                sig("dve_step").advance(chain.n)
        for name, n in (("mixed", B), ("mix_step", 2 * B), ("angle_product", B), ("hidden_product", B * G), ("silu_up", B * G), ("gelus", B * G),
                        ("mlp_out", B), ("sigmoids", B), ("normed", B), ("residual", B)):
            sig(name).advance(n)


MATS = {
    "kept": ["centring", "ident", "rotation", "Wq", "Wk", "Wv"],
    "first": ["W_mag", "W_q", *[f"W1.{n}" for n in range(8)], "W2.0", "W2.1"],
    "levels": [*[f"in.{l}.{w}" for l in range(LEVELS) for w in range(3)], *[f"out.{l}" for l in range(LEVELS)], *[f"up.{l}" for l in range(LEVELS - 1)]],
    "mixing": ["rk", "rv", "rr", "ro", *[f"Fk.{g}" for g in range(4)], *[f"Fv.{g}" for g in range(4)], "Fr"],
}
VECS = ["phases", "b_mag", "b_q", "b1.0", "b1.1", "b2", *[f"ln_g.{f}" for f in range(4)], *[f"ln_b.{f}" for f in range(4)],
        "bq", "bk", "bv", *[f"in_b.{l}.{w}" for l in range(LEVELS) for w in range(3)], *[f"out_b.{l}" for l in range(LEVELS)],
        *[f"up_b.{l}" for l in range(LEVELS - 1)], "ln1_g", "ln1_b", "ln2_g", "ln2_b", "att_time_mix", "att_combined_mix",
        "time_decay", "time_first", "ffn_time_mix", "ffn_combined_mix", "first_half", "second_half"]


def build(nc, args):
    with ExitStack() as stack:
        k = Kernel(nc, args, stack)
        open_signals(k)
        sig = k.count_of
        k.X = k.sb("X", [P, NT])
        xn = k.sb("xn", [P, NT])
        vecs = k.sb("vecs", [P, len(VECS)])
        mats = {"kept": k.sb("mats", [P, len(MATS["kept"]), P])}
        k.mean_of = k.sb("mean_of", [P, P])
        k.mean_of_4 = k.sb("mean_of_4", [P, P])
        k.ident_bf = k.sb("ident_bf", [P, P], BF16)
        k.head_rows = k.sb("head_rows", [P, P])
        k.eps, k.tiny, k.half_pi = (k.sb(n, [P, 1]) for n in ("eps", "tiny", "half_pi"))
        gates = k.sb("gates", [P, EXPERTS0 + EXPERTS1])

        def mat(name):
            group = next(g for g, names in MATS.items() if name in names)
            return mats[group][:, MATS[group].index(name), :]

        def load_mats(group, st):
            mats[group] = k.sb(f"mats_{group}", [P, len(MATS[group]), P], stack=st)

            def load(sp):
                arrived = sig("mats_in")
                sp.dma_start(mats[group][:, :, :], args["mats_" + group]).then_inc(arrived.sem, 16)
                sp.wait_ge(arrived.sem, arrived.at(1))
                arrived.advance(1)
            return {"sync": load}

        def vec(name):
            at = VECS.index(name)
            return vecs[:, at:at + 1]

        k.centring, k.ident = mat("centring"), mat("ident")
        with nc.Block() as block:

            @block.sync
            def _(sp):
                loads = [(k.X[:, :], args["x"]), (vecs[:, :], args["vecs"]), (mats["kept"][:, :, :], args["mats_kept"]), (k.head_rows[:, :], args["head_rows"]),
                         (gates[:, :], args["gates"]), (k.ident_bf[:, :], args["ident_bf"].bitcast(BF16))]
                for to, of in loads:
                    sp.dma_start(to, of).then_inc(sig("inputs_in").sem, 16)
                sp.wait_ge(sig("inputs_in").sem, sig("inputs_in").at(len(loads)))
                sig("inputs_in").advance(len(loads))

            @block.vector
            def _(dve):
                for to, value in ((k.mean_of, 1 / P), (k.mean_of_4, 1 / (4 * P)), (k.eps, EPS), (k.tiny, 1e-8), (k.half_pi, float(np.pi / 2))):
                    dve.memset(to[:, :], value)

        def layer_weights(st, tiles):
            hi = k.sb("w_hi", [P, tiles * 3 * P], F32R, stack=st)
            lo = k.sb("w_lo", [P, tiles * 3 * P], F32R, stack=st)
            rows = k.sb("rows", [P, tiles, P], BF16, stack=st)
            return hi, lo, rows

        def loader(st, w, tiles, name, alone=False):
            hi, lo, rows = w
            k.raw_weights = k.sb("raw_weights", [P, RAW_ALONE if alone else RAW, 2 * 3 * P], stack=st)
            also, done = expert_loader(k, args[name], tiles, hi, lo, alone)

            def loads(sp):
                sp.dma_start(rows[:, :, :], args[name + "_rows"].bitcast(BF16)).then_inc(sig("consts_in").sem, 16)
                also["sync"](sp)
                sp.wait_ge(sig("consts_in").sem, sig("consts_in").at(1))
                sig("consts_in").advance(1)
            return {**also, "sync": loads}, done

        def mlp(w, tiles, experts, top, gate, softmax):
            hi, lo, rows = w
            with ExitStack() as st:
                room = ExitStack()
                logits = k.ps("logits", [P, TILES, experts], stack=room)
                layernorm(k, k.X, xn, routing=(logits, gate), sigmoid_next=not softmax)
                x_hi = k.sb("x_hi", [P, NT], F32R, stack=st)
                x_lo = k.sb("x_lo", [P, NT], F32R, stack=st)
                k.route_rows = k.sb("route_rows", [P, NT], BF16, stack=st)
                routed_mlp(k, xn, logits, room, x_hi, x_lo, hi, lo, tiles, experts, top, rows, softmax)

        def table_in(to, of):
            def load(sp):
                arrived = sig("consts_in")
                sp.dma_start(to, of).then_inc(arrived.sem, 16)
                sp.wait_ge(arrived.sem, arrived.at(1))
                arrived.advance(1)
            return load

        with ExitStack() as st:
            w = layer_weights(st, TILES0)
            gate = gates[:, 0:EXPERTS0]
            with ExitStack() as st2:
                positions = k.sb("positions", [P, S], stack=st2)
                load_first = load_mats("first", st2)["sync"]
                load_positions = table_in(positions[:, :], args["positions"])

                def loads(sp):
                    load_first(sp)
                    load_positions(sp)

                layernorm(k, k.X, xn, also={"sync": loads})
                also, done = loader(st2, w, TILES0, "mlp0", alone=True)
                phase_memory(k, xn, lambda n, i=None: mat(n if i is None else f"{n}.{i}"), lambda n, i=None: vec(n if i is None else f"{n}.{i}"), positions[:, :], also)
                done()
            mlp(w, TILES0, EXPERTS0, TOP0, gate, False)
            with ExitStack() as st2:
                turns = k.sb("turns", [P, 2, S], stack=st2)
                layernorm(k, k.X, xn, also={"sync": table_in(turns[:, :, :], args["rope"])})
                only = Level(xn, xn, S, B, S, lambda i: mat(("Wq", "Wk", "Wv")[i]), lambda i: vec(("bq", "bk", "bv")[i]))
                attention(k, [only], rope=(mat("rotation"), turns[:, 0, :], turns[:, 1, :]), residual=True)
            mlp(w, TILES0, EXPERTS0, TOP0, gate, False)
        with ExitStack() as st:
            layernorm(k, k.X, xn, also=load_mats("levels", st))
            contexts = [xn, *[k.sb(f"context{l}", [P, NT >> l], stack=st) for l in range(1, LEVELS)]]
            with ExitStack() as st2:
                coarse = {l: k.sb(f"coarse{l}", [P, NT >> l], stack=st2) for l in range(1, LEVELS)}
                sampled(k, xn[:, :], {l: c[:, :] for l, c in coarse.items()})
                levels = []
                for l in range(LEVELS):
                    seq = S >> l
                    chunk = min(CH, B * seq)
                    levels.append(Level(coarse[l] if l else xn, contexts[l], seq, B * seq // chunk, chunk,
                                        lambda i, l=l: mat(f"in.{l}.{i}"), lambda i, l=l: vec(f"in_b.{l}.{i}")))
                attention(k, levels)
            w = layer_weights(st, TILES1)
            also, done = loader(st, w, TILES1, "mlp1")
            at = VECS.index("out_b.0")
            combine_levels(k, contexts, lambda l: mat(f"out.{l}"), lambda l: mat(f"up.{l}"), vecs[:, at:at + LEVELS], vecs[:, at + LEVELS:at + 2 * LEVELS - 1], also)
            done()
            gate = gates[:, EXPERTS0:]
            mlp(w, TILES1, EXPERTS1, TOP1, gate, True)
            with ExitStack() as st2:
                layernorm(k, k.X, xn, also=load_mats("mixing", st2))
                x1 = k.sb("x1", [P, NT], stack=st2)
                layernorm(k, xn, x1, gain=vec("ln1_g"), shift=vec("ln1_b"))
                names = {"Wk": "rk", "Wv": "rv", "Wr": "rr", "Wo": "ro"}
                time_mix(k, x1, xn, lambda n: mat(names[n]), vec)
                layernorm(k, xn, x1, gain=vec("ln2_g"), shift=vec("ln2_b"))
                channel_mix(k, x1, lambda n, i=None: mat(n if i is None else f"{n}.{i}"), vec)
            mlp(w, TILES1, EXPERTS1, TOP1, gate, True)

        with nc.Block() as block:

            @block.sync
            def _(sp):
                sp.dma_start(args["out"], k.X[:, :]).then_inc(sig("out_stored").sem, 16)
                sp.wait_ge(sig("out_stored").sem, sig("out_stored").at(1))


BF16_ONE = np.uint16(0x3F80)


def shape_constants():
    rotation = np.zeros((P, P), np.float32)
    for i in range(0, P, 2):
        rotation[i + 1, i] = -1.0
        rotation[i, i + 1] = 1.0
    inv = np.power(np.float32(10000.0), -2.0 * np.arange(HD // 2, dtype=np.float32) / HD).astype(np.float32)
    ang = np.arange(S, dtype=np.float32)[:, None] * inv[None, :]
    table = [np.tile(np.repeat(f(ang), 2, axis=-1).T, (HEADS, 1)) for f in (np.cos, np.sin)]
    head_rows = np.zeros((P, P), np.float32)
    for h in range(HEADS):
        head_rows[32 * (h // GROUP) + h % GROUP, h * HD:(h + 1) * HD] = 1.0

    def rows(tiles, hidden, experts):
        out = np.zeros((P, tiles * P), np.uint16)
        for m in range(tiles * P):
            e = m // hidden
            out[[e, 32 + e, 64 + e] if e < experts else [96], m] = BF16_ONE
        return out.reshape(P, tiles, P)

    return {
        "centring": np.eye(P, dtype=np.float32) - np.float32(1 / P), "ident": np.eye(P, dtype=np.float32), "rotation": rotation,
        "first_half": (np.arange(P) < P // 2).astype(np.float32), "second_half": (np.arange(P) >= P // 2).astype(np.float32),
        "positions": np.tile(np.arange(S, dtype=np.float32), (P, 1)), "rope": np.stack(table, axis=1).astype(np.float32),
        "head_rows": head_rows, "ident_bf": np.eye(P, dtype=np.uint16) * BF16_ONE,
        "mlp0_rows": rows(TILES0, HIDDEN0, EXPERTS0), "mlp1_rows": rows(TILES1, HIDDEN1, EXPERTS1),
    }


def laid_out(inputs):
    d = {n: np.asarray(a) for n, a in inputs.items()}
    const = shape_constants()
    a, b = "L0_attn_a_", "L0_attn_b_"
    m, v = {n: const[n] for n in ("centring", "ident", "rotation")}, {n: const[n] for n in ("first_half", "second_half")}
    m["W_mag"], m["W_q"] = d[a + "W_mag"].T, d[a + "W_q"].T
    for f in range(4):
        for g in range(2):
            m[f"W1.{f * 2 + g}"] = d[a + "W1"][g * P:(g + 1) * P, f * P:(f + 1) * P].T
    for g in range(2):
        m[f"W2.{g}"] = d[a + "W2"][:, g * P:(g + 1) * P].T
        v[f"b1.{g}"] = d[a + "b1"][g * P:(g + 1) * P]
    v["phases"], v["b_mag"], v["b_q"], v["b2"] = d[a + "random_phases"], d[a + "b_mag"], d[a + "b_q"], d[a + "b2"]
    for f in range(4):
        v[f"ln_g.{f}"], v[f"ln_b.{f}"] = d[a + "ln_g"][f * P:(f + 1) * P], d[a + "ln_b"][f * P:(f + 1) * P]
    for w in "qkv":
        m["W" + w], v["b" + w] = d[b + "W" + w], d[b + "b" + w]
    c = "L1_attn_a_"
    for l in range(LEVELS):
        for w in range(3):
            m[f"in.{l}.{w}"] = d[c + "in_proj_w"][l, w * P:(w + 1) * P].T
            v[f"in_b.{l}.{w}"] = d[c + "in_proj_b"][l, w * P:(w + 1) * P]
        m[f"out.{l}"], v[f"out_b.{l}"] = d[c + "out_w"][l].T, d[c + "out_b"][l]
        if l < LEVELS - 1:
            m[f"up.{l}"], v[f"up_b.{l}"] = d[c + "up_w"][l].T, d[c + "up_b"][l]
    r = "L1_attn_b_"
    for n, w in (("rk", "Wk"), ("rv", "Wv"), ("rr", "Wr"), ("ro", "Wo"), ("Fr", "Fr")):
        m[n] = d[r + w].T
    for g in range(4):
        m[f"Fk.{g}"], m[f"Fv.{g}"] = d[r + "Fk"][g * P:(g + 1) * P].T, d[r + "Fv"][:, g * P:(g + 1) * P].T
    for n in ("ln1_g", "ln1_b", "ln2_g", "ln2_b", "att_time_mix", "att_combined_mix", "time_decay", "time_first", "ffn_time_mix", "ffn_combined_mix"):
        v[n] = d[r + n].reshape(P)

    def mlp(gate, up, down):
        n = gate.shape[1] // P
        parts = gate.reshape(P, n, P), up.reshape(P, n, P), down.reshape(n, P, P).transpose(1, 0, 2)
        return np.stack(parts, axis=2).reshape(P, n * 3 * P)

    f0, f1 = "L0_ffn_", "L1_ffn_"
    mlp0 = mlp(np.concatenate([d[f0 + "exp_wg"].transpose(1, 0, 2).reshape(P, -1), d[f0 + "shared_wg"]], 1),
               np.concatenate([d[f0 + "exp_wu"].transpose(1, 0, 2).reshape(P, -1), d[f0 + "shared_wu"]], 1),
               np.concatenate([d[f0 + "exp_wd"].reshape(-1, P), d[f0 + "shared_wd"]], 0))
    mlp1 = mlp(d[f1 + "w1"].reshape(-1, P).T, d[f1 + "w3"].reshape(-1, P).T, d[f1 + "w2"].transpose(0, 2, 1).reshape(-1, P))
    arrays = {"x": d[a + "x"].reshape(NT, P).T, "vecs": np.stack([v[n] for n in VECS], axis=1), **{"mats_" + g: np.stack([m[n] for n in names], axis=1) for g, names in MATS.items()},
              "gates": np.concatenate([d[f0 + "gate_w"].T, d[f1 + "gate_w"].T], axis=1), "mlp0": mlp0, "mlp1": mlp1,
              **{n: const[n] for n in ("positions", "rope", "head_rows", "ident_bf", "mlp0_rows", "mlp1_rows")}}
    return {n: np.ascontiguousarray(x) for n, x in arrays.items()}


def kernel(**inputs):
    import concourse.bacc as bacc
    from concourse.bass_utils import run_bass_kernel_spmd

    nc = bacc.Bacc("TRN2", target_bir_lowering=False, num_devices=1)
    arrays = {f"in_{n}": x for n, x in laid_out(inputs).items()}
    args = {n[3:]: nc.dram_tensor(n, x.shape, mybir.dt.from_np(x.dtype), kind="ExternalInput").ap() for n, x in arrays.items()}
    args["out"] = nc.dram_tensor("out_x", (P, NT), F32, kind="ExternalOutput").ap()
    build(nc, args)
    result = run_bass_kernel_spmd(nc, [arrays], core_ids=[0]).results[0]["out_x"]
    return np.ascontiguousarray(result.T).reshape(B, S, P)
```
